# Optimizing a Trainium2 kernel written in Bass

```python
import numpy as np
import jax
import jax.numpy as jnp

def _softmax(x, axis=-1):
    return jax.nn.softmax(x, axis=axis)

def _gelu(x):
    return jax.nn.gelu(x, approximate=True)

def _silu(x):
    return jax.nn.silu(x)

def _sigmoid(x):
    return jax.nn.sigmoid(x)

def _layernorm(x, axis=-1, eps=1e-05):
    m = jnp.mean(x, axis=axis, keepdims=True)
    v = jnp.var(x, axis=axis, keepdims=True)
    return (x - m) / jnp.sqrt(v + eps)

def _scatter_add(tgt, idx, src, axis=0):
    return tgt.at[idx].add(src)

def _segment_sum(src, seg, n):
    return jax.ops.segment_sum(src, seg, n)
kernel_name = 'mk_xattn_ffn_d2_seqx_r8_c68101'

def setup_inputs(seed: int=0):
    np.random.seed(seed)
    _w = jnp.asarray

    def _rec_inputs():
        import jax
        import jax.numpy as jnp
        _rk = jax.random.key(seed)
        x = -0.0002928 + 1 * jax.random.normal(jax.random.fold_in(_rk, 1), (8, 256, 256), jnp.float32)
        _lenS = 256 - jax.random.randint(jax.random.fold_in(_rk, 7), (8,), 0, max(1, 256 // 4) + 1, jnp.int32)
        _lenS2 = 1601 - jax.random.randint(jax.random.fold_in(_rk, 8), (8,), 0, max(1, 1601 // 4) + 1, jnp.int32)
        _ctx_512P = jax.random.normal(jax.random.fold_in(_rk, 11), (8, 16, 64), jnp.float32)
        _ctx_512c = jax.random.dirichlet(jax.random.fold_in(_rk, 511), 0.3 * jnp.ones((16,), jnp.float32), (8, 1601))
        _ctx_512t = jnp.einsum('bsk,bkd->bsd', _ctx_512c, _ctx_512P)
        _ctx_512t = _ctx_512t * jax.lax.rsqrt(jnp.mean(jnp.square(_ctx_512t)) + 1e-12) * 0.953939
        ctx_512 = 0.000227908 + 0.99994 * (_ctx_512t + 0.3 * jax.random.normal(jax.random.fold_in(_rk, 611), (8, 1601, 64), jnp.float32))
        return (x, ctx_512)
    x, ctx_512 = _rec_inputs()

    def _L0_xattn_setup():
        import jax, jax.numpy as jnp
        import numpy as np
        B, S, L = (2, 128, 128)
        DIM_Q, H, K, D_C, D_CQ, R = (256, 16, 128, 64, 192, 64)

        def _rope_tables(length, dim):
            inv = 1.0 / 10000.0 ** (jnp.arange(0, dim, 2, dtype=jnp.float32) / dim)
            f = jnp.arange(length, dtype=jnp.float32)[:, None] * inv[None, :]
            sin = jnp.repeat(jnp.sin(f), 2, axis=-1)
            cos = jnp.repeat(jnp.cos(f), 2, axis=-1)
            return (sin, cos)

        def _rotate_half(x):
            half = x.shape[-1] // 2
            return jnp.concatenate([-x[..., half:], x[..., :half]], axis=-1)

        def _apply_rope(x, sin, cos):
            return x * cos + _rotate_half(x) * sin
        key = jax.random.key(seed)
        ks = jax.random.split(key, 8)
        return {'hidden_q': jax.random.normal(ks[0], (B, S, DIM_Q), jnp.float32), 'kv_c': jax.random.normal(ks[1], (B, L, D_C), jnp.float32), 'Wq': jax.random.normal(ks[2], (H * K, DIM_Q), jnp.float32) / np.sqrt(DIM_Q).astype(np.float32), 'w_kc_q': jax.random.normal(ks[3], (H, K, D_CQ), jnp.float32) / np.sqrt(K).astype(np.float32), 'w_kc_kv': jax.random.normal(ks[4], (H, K, D_C), jnp.float32) / np.sqrt(K).astype(np.float32), 'W_qr': jax.random.normal(ks[5], (H, D_CQ, R), jnp.float32) / np.float32(np.sqrt(D_CQ) * np.sqrt(R)), 'W_kr': jax.random.normal(ks[6], (H, D_C, R), jnp.float32) / np.sqrt(D_C).astype(np.float32), 'Wo': jax.random.normal(ks[7], (DIM_Q, H * K), jnp.float32) / np.sqrt(H * K).astype(np.float32)}
    _L0_xattn_all = _L0_xattn_setup()
    _L0_xattn_in = {k: v for k, v in _L0_xattn_all.items() if k in ('Wq', 'w_kc_q', 'w_kc_kv', 'W_qr', 'W_kr', 'Wo')}
    del _L0_xattn_all

    def _L0_ffn_setup():
        import jax, jax.numpy as jnp
        import numpy as np
        B, S, D = (4, 512, 256)
        DFF = 4 * D
        CAPACITY = 0.125
        K = int(CAPACITY * S)
        key = jax.random.key(seed)
        ks = jax.random.split(key, 8)
        sc = 1.0 / np.sqrt(D)
        return {'x': jax.random.normal(ks[0], (B, S, D), dtype=jnp.float32), 'W_r': jax.random.normal(ks[1], (D, 1), dtype=jnp.float32) * sc, 'b_r': jnp.zeros((1,), dtype=jnp.float32), 'W1': jax.random.normal(ks[2], (D, DFF), dtype=jnp.float32) * sc, 'b1': jnp.zeros((DFF,), dtype=jnp.float32), 'W2': jax.random.normal(ks[3], (DFF, D), dtype=jnp.float32) * (1.0 / np.sqrt(DFF)), 'b2': jnp.zeros((D,), dtype=jnp.float32), 'position_ids': jnp.arange(B * S, dtype=jnp.int64 if jax.config.jax_enable_x64 else jnp.int32).reshape(B, S), 'cache_position': jnp.arange(S, dtype=jnp.int64 if jax.config.jax_enable_x64 else jnp.int32)}
    _L0_ffn_all = _L0_ffn_setup()
    _L0_ffn_in = {k: v for k, v in _L0_ffn_all.items() if k in ('W_r', 'b_r', 'W1', 'b1', 'W2', 'b2', 'position_ids', 'cache_position')}
    del _L0_ffn_all

    def _L1_xattn_setup():
        import jax, jax.numpy as jnp
        import numpy as np
        B, S, H, NH, L = (2, 256, 256, 16, 64)
        HD = H // NH
        key = jax.random.key(seed)
        k1, k2, k3, k4, k5 = jax.random.split(key, 5)
        scale = 0.02
        return {'q': jax.random.normal(k1, (B, S, H), dtype=jnp.float32), 'latent_kv': jax.random.normal(k2, (B, S, L), dtype=jnp.float32), 'Wq': jax.random.normal(k3, (H, H), dtype=jnp.float32) * scale, 'Wkv_expand': jax.random.normal(k4, (2 * H, L), dtype=jnp.float32) * scale, 'Wout': jax.random.normal(k5, (H, H), dtype=jnp.float32) * scale}
    _L1_xattn_all = _L1_xattn_setup()
    _L1_xattn_in = {k: v for k, v in _L1_xattn_all.items() if k in ('Wq', 'Wkv_expand', 'Wout')}
    del _L1_xattn_all

    def _L1_ffn_setup():
        import jax, jax.numpy as jnp
        import numpy as np
        B, S, D = (4, 256, 256)
        E = 8
        H = 352
        CAP_F = 1.0

        def _moe(x, Wg, W1, W3, W2, sw1, sw3, sw2):
            b, sl, d = x.shape
            T = b * sl
            C = int(CAP_F * T / E)
            xt = x.reshape(T, d)
            probs = jax.nn.softmax(xt @ Wg, axis=-1)
            eidx = jnp.argmax(probs, axis=-1)
            gate = jnp.take_along_axis(probs, eidx[:, None], 1)[:, 0]
            oh = jax.nn.one_hot(eidx, E, dtype=jnp.int32)
            pos = (jnp.cumsum(oh, axis=0) * oh).sum(-1) - 1
            keep = pos < C
            flat = jnp.where(keep, eidx * C + pos, E * C)
            xd = jnp.zeros((E * C, d), x.dtype).at[flat].set(xt, mode='drop')
            xd = xd.reshape(E, C, d)
            h = jax.nn.silu(jnp.einsum('ecd,edh->ech', xd, W1)) * jnp.einsum('ecd,edh->ech', xd, W3)
            oe = jnp.einsum('ech,ehd->ecd', h, W2).reshape(E * C, d)
            out = jnp.take(oe, jnp.minimum(flat, E * C - 1), axis=0)
            out = out * (gate * keep.astype(x.dtype))[:, None]
            shared = jax.nn.silu(xt @ sw1) * (xt @ sw3) @ sw2
            return (out + shared).reshape(b, sl, d)
        key = jax.random.key(seed)
        ks = jax.random.split(key, 8)
        s = lambda fan: 1.0 / np.sqrt(fan)
        return {'x': jax.random.normal(ks[0], (B, S, D), jnp.float32), 'Wg': jax.random.normal(ks[1], (D, E), jnp.float32) * s(D), 'W1': jax.random.normal(ks[2], (E, D, H), jnp.float32) * s(D), 'W3': jax.random.normal(ks[3], (E, D, H), jnp.float32) * s(D), 'W2': jax.random.normal(ks[4], (E, H, D), jnp.float32) * s(H), 'sw1': jax.random.normal(ks[5], (D, H), jnp.float32) * s(D), 'sw3': jax.random.normal(ks[6], (D, H), jnp.float32) * s(D), 'sw2': jax.random.normal(ks[7], (H, D), jnp.float32) * s(H)}
    _L1_ffn_all = _L1_ffn_setup()
    _L1_ffn_in = {k: v for k, v in _L1_ffn_all.items() if k in ('Wg', 'W1', 'W3', 'W2', 'sw1', 'sw3', 'sw2')}
    del _L1_ffn_all
    return {'x': x, 'ctx_512': ctx_512, 'L0_xattn_Wq': _L0_xattn_in['Wq'], 'L0_xattn_w_kc_q': _L0_xattn_in['w_kc_q'], 'L0_xattn_w_kc_kv': _L0_xattn_in['w_kc_kv'], 'L0_xattn_W_qr': _L0_xattn_in['W_qr'], 'L0_xattn_W_kr': _L0_xattn_in['W_kr'], 'L0_xattn_Wo': _L0_xattn_in['Wo'], 'L0_ffn_W_r': _L0_ffn_in['W_r'], 'L0_ffn_b_r': _L0_ffn_in['b_r'], 'L0_ffn_W1': _L0_ffn_in['W1'], 'L0_ffn_b1': _L0_ffn_in['b1'], 'L0_ffn_W2': _L0_ffn_in['W2'], 'L0_ffn_b2': _L0_ffn_in['b2'], 'L0_ffn_position_ids': _L0_ffn_in['position_ids'], 'L0_ffn_cache_position': _L0_ffn_in['cache_position'], 'L1_xattn_Wq': _L1_xattn_in['Wq'], 'L1_xattn_Wkv_expand': _L1_xattn_in['Wkv_expand'], 'L1_xattn_Wout': _L1_xattn_in['Wout'], 'L1_ffn_Wg': _L1_ffn_in['Wg'], 'L1_ffn_W1': _L1_ffn_in['W1'], 'L1_ffn_W3': _L1_ffn_in['W3'], 'L1_ffn_W2': _L1_ffn_in['W2'], 'L1_ffn_sw1': _L1_ffn_in['sw1'], 'L1_ffn_sw3': _L1_ffn_in['sw3'], 'L1_ffn_sw2': _L1_ffn_in['sw2']}

def reference(x, ctx_512, L0_xattn_Wq, L0_xattn_w_kc_q, L0_xattn_w_kc_kv, L0_xattn_W_qr, L0_xattn_W_kr, L0_xattn_Wo, L0_ffn_W_r, L0_ffn_b_r, L0_ffn_W1, L0_ffn_b1, L0_ffn_W2, L0_ffn_b2, L0_ffn_position_ids, L0_ffn_cache_position, L1_xattn_Wq, L1_xattn_Wkv_expand, L1_xattn_Wout, L1_ffn_Wg, L1_ffn_W1, L1_ffn_W3, L1_ffn_W2, L1_ffn_sw1, L1_ffn_sw3, L1_ffn_sw2):
    import jax
    import jax.numpy as jnp

    def _L0_xattn_ref(hidden_q, kv_c, Wq, w_kc_q, w_kc_kv, W_qr, W_kr, Wo):
        import jax, jax.numpy as jnp
        import numpy as np
        B, S, L = (2, 128, 128)
        DIM_Q, H, K, D_C, D_CQ, R = (256, 16, 128, 64, 192, 64)

        def _rope_tables(length, dim):
            inv = 1.0 / 10000.0 ** (jnp.arange(0, dim, 2, dtype=jnp.float32) / dim)
            f = jnp.arange(length, dtype=jnp.float32)[:, None] * inv[None, :]
            sin = jnp.repeat(jnp.sin(f), 2, axis=-1)
            cos = jnp.repeat(jnp.cos(f), 2, axis=-1)
            return (sin, cos)

        def _rotate_half(x):
            half = x.shape[-1] // 2
            return jnp.concatenate([-x[..., half:], x[..., :half]], axis=-1)

        def _apply_rope(x, sin, cos):
            return x * cos + _rotate_half(x) * sin
        Bv, Sv, _ = hidden_q.shape
        _, Lv, _ = kv_c.shape
        q_hk = (hidden_q @ Wq.T).reshape(Bv, Sv, H, K)
        q_big = jnp.einsum('bshk,hkq->bshq', q_hk, w_kc_q)
        sin_q, cos_q = _rope_tables(Sv, D_CQ)
        q_big = _apply_rope(q_big, sin_q[None, :, None, :], cos_q[None, :, None, :])
        sin_k, cos_k = _rope_tables(Lv, D_C)
        kv_r = _apply_rope(kv_c, sin_k[None], cos_k[None])
        q_r = jnp.einsum('bshq,hqr->bhsr', q_big, W_qr)
        k_r = jnp.einsum('bld,hdr->bhlr', kv_r, W_kr)
        scores = jnp.einsum('bhsr,bhlr->bhsl', q_r, k_r)
        attn = jax.nn.softmax(scores, axis=-1)
        ctx_c = jnp.einsum('bhsl,bld->bhsd', attn, kv_r)
        ctx_lat = jnp.einsum('bhsd,hkd->bhsk', ctx_c, w_kc_kv)
        ctx = ctx_lat.transpose(0, 2, 1, 3).reshape(Bv, Sv, H * K)
        return ctx @ Wo.T

    def _L0_ffn_ref(x, W_r, b_r, W1, b1, W2, b2, position_ids, cache_position):
        import jax, jax.numpy as jnp
        import numpy as np
        B, S, D = (4, 512, 256)
        DFF = 4 * D
        CAPACITY = 0.125
        K = int(CAPACITY * S)
        b, s, d = x.shape
        weights = jnp.einsum('bsd,do->bso', x, W_r).squeeze(-1) + b_r
        topk_vals, topk_idx = jax.lax.top_k(weights, K)
        threshold = topk_vals[:, -1]
        sel_mask = weights > threshold[:, None]
        xg = jnp.take_along_axis(x, topk_idx[..., None], axis=1)
        h = jax.nn.gelu(jnp.einsum('bkd,df->bkf', xg, W1) + b1)
        blk = jnp.einsum('bkf,fd->bkd', h, W2) + b2
        gate = (topk_vals > threshold[:, None]).astype(x.dtype)
        wg = jnp.take_along_axis(weights, topk_idx, axis=1)
        vals = blk * (wg * gate)[..., None]
        bidx = jnp.arange(b)[:, None]
        processed = jnp.zeros_like(x).at[bidx, topk_idx].add(vals)
        return processed + x * (~sel_mask)[..., None].astype(x.dtype)

    def _L1_xattn_ref(q, latent_kv, Wq, Wkv_expand, Wout):
        import jax, jax.numpy as jnp
        import numpy as np
        B, S, H, NH, L = (2, 256, 256, 16, 64)
        HD = H // NH
        b, sq, _ = q.shape
        sk = latent_kv.shape[1]
        qp = q @ Wq.T
        kv = latent_kv @ Wkv_expand.T
        k, v = jnp.split(kv, 2, axis=-1)
        qh = qp.reshape(b, sq, NH, HD).transpose(0, 2, 1, 3)
        kh = k.reshape(b, sk, NH, HD).transpose(0, 2, 1, 3)
        vh = v.reshape(b, sk, NH, HD).transpose(0, 2, 1, 3)
        inv_sqrt_d = 1.0 / jnp.sqrt(jnp.float32(HD))
        scores = jnp.einsum('bhqd,bhkd->bhqk', qh, kh) * inv_sqrt_d
        causal = jnp.tril(jnp.ones((sq, sk), dtype=bool))
        scores = jnp.where(causal, scores, jnp.finfo(scores.dtype).min)
        attn = jax.nn.softmax(scores, axis=-1)
        out = jnp.einsum('bhqk,bhkd->bhqd', attn, vh)
        out = out.transpose(0, 2, 1, 3).reshape(b, sq, H)
        return out @ Wout.T

    def _L1_ffn_ref(x, Wg, W1, W3, W2, sw1, sw3, sw2):
        import jax, jax.numpy as jnp
        import numpy as np
        B, S, D = (4, 256, 256)
        E = 8
        H = 352
        CAP_F = 1.0

        def _moe(x, Wg, W1, W3, W2, sw1, sw3, sw2):
            b, sl, d = x.shape
            T = b * sl
            C = int(CAP_F * T / E)
            xt = x.reshape(T, d)
            probs = jax.nn.softmax(xt @ Wg, axis=-1)
            eidx = jnp.argmax(probs, axis=-1)
            gate = jnp.take_along_axis(probs, eidx[:, None], 1)[:, 0]
            oh = jax.nn.one_hot(eidx, E, dtype=jnp.int32)
            pos = (jnp.cumsum(oh, axis=0) * oh).sum(-1) - 1
            keep = pos < C
            flat = jnp.where(keep, eidx * C + pos, E * C)
            xd = jnp.zeros((E * C, d), x.dtype).at[flat].set(xt, mode='drop')
            xd = xd.reshape(E, C, d)
            h = jax.nn.silu(jnp.einsum('ecd,edh->ech', xd, W1)) * jnp.einsum('ecd,edh->ech', xd, W3)
            oe = jnp.einsum('ech,ehd->ecd', h, W2).reshape(E * C, d)
            out = jnp.take(oe, jnp.minimum(flat, E * C - 1), axis=0)
            out = out * (gate * keep.astype(x.dtype))[:, None]
            shared = jax.nn.silu(xt @ sw1) * (xt @ sw3) @ sw2
            return (out + shared).reshape(b, sl, d)
        return _moe(x, Wg, W1, W3, W2, sw1, sw3, sw2)
    x = x + _L0_xattn_ref(_layernorm(x, axis=-1), ctx_512, L0_xattn_Wq, L0_xattn_w_kc_q, L0_xattn_w_kc_kv, L0_xattn_W_qr, L0_xattn_W_kr, L0_xattn_Wo)
    x = x + _L0_ffn_ref(_layernorm(x, axis=-1), L0_ffn_W_r, L0_ffn_b_r, L0_ffn_W1, L0_ffn_b1, L0_ffn_W2, L0_ffn_b2, L0_ffn_position_ids, L0_ffn_cache_position)
    x = x + _L1_xattn_ref(_layernorm(x, axis=-1), ctx_512, L1_xattn_Wq, L1_xattn_Wkv_expand, L1_xattn_Wout)
    x = x + _L1_ffn_ref(_layernorm(x, axis=-1), L1_ffn_Wg, L1_ffn_W1, L1_ffn_W3, L1_ffn_W2, L1_ffn_sw1, L1_ffn_sw3, L1_ffn_sw2)
    return x

_drawn_inputs = setup_inputs


def setup_inputs(seed=0):
    import zlib

    import numpy as np

    out = dict(_drawn_inputs(seed))
    spreads = {'L0_ffn_b1': (0.0, 0.1), 'L0_ffn_b2': (0.0, 0.1)}
    factors = {'L1_xattn_Wq': 8.0, 'L1_xattn_Wkv_expand': 3.199, 'L1_xattn_Wout': 3.065}
    for name, (base, spread) in spreads.items():
        noise = np.random.default_rng([zlib.crc32(name.encode()), seed]).standard_normal(out[name].shape)
        drawn = base * np.exp(spread * noise) if base else spread * noise
        out[name] = jnp.asarray(drawn.astype(out[name].dtype))
    for name, factor in factors.items():
        out[name] = (out[name] * factor).astype(out[name].dtype)
    return out
```

```python
from contextlib import ExitStack

import numpy as np

import concourse.bass as bass
from concourse import mybir

ALU = mybir.AluOpType
ACT = mybir.ActivationFunctionType
F32 = mybir.dt.float32
F16 = mybir.dt.float16
BF16 = mybir.dt.bfloat16
U32 = mybir.dt.uint32
AX = mybir.AxisListType
P = 128
BF_NP = mybir.dt.np(BF16)

B, S, D = 8, 256, 256
L = 1601
ST = S // P
NT = B * ST
DK = D // P
H0, K0, DC, DCQ, R0 = 16, 128, 64, 192, 64
LT = -(-L // P)
LLAST = L - (LT - 1) * P
HALF = DCQ // 2
EPS = 1e-5

QK_TOP = 2.0 ** 14
SHIFT_ONE = 2.0 ** 15
SHIFT_ROWS = 16
SHIFT_MUL = 1.0 / (SHIFT_ONE * SHIFT_ROWS)
LN_1024 = float(np.log(1024.0))


LIVE = []


def new_semaphore(nc, name):
    LIVE.append(nc.alloc_semaphore(name))
    return LIVE[-1]


def clear_semaphores(nc):
    nc.all_engine_barrier()
    nc.clear_and_free_semaphores(list(LIVE))
    nc.all_engine_barrier()
    LIVE.clear()


def layer_norm_stats(dve, nc, link, x, stats, agg, n):
    for j in range(n):
        link(nc.vector.bn_stats(stats[:, j, :], x[:, j, :]))
        link(nc.vector.bn_aggr(agg[:, j, :], stats[:, j, :]))


def rstd_refined(nc, link, rstd, root, agg, tmp):
    var = agg[:, :, 1]
    link(nc.vector.reciprocal(rstd, root))
    link(nc.vector.tensor_tensor(tmp, rstd, rstd, ALU.mult))
    link(nc.vector.scalar_tensor_tensor(out=tmp, in0=var, scalar=EPS, in1=tmp, op0=ALU.add, op1=ALU.mult))
    link(nc.vector.tensor_scalar(tmp, tmp, -0.5, 1.5, ALU.mult, ALU.add))
    link(nc.vector.tensor_tensor(rstd, rstd, tmp, ALU.mult))


def phase_weights(nc, ctx, t, keep):
    def sb(name, shape, dt=F32):
        return ctx.enter_context(nc.sbuf_tensor(name, shape, dt))

    def sem(name):
        return new_semaphore(nc, name)

    wq = sb("a_wq", [P, H0, D])
    wkcq = sb("a_wkcq", [P, H0, DCQ])
    wqr = sb("a_wqr", [HALF, H0, 2, R0])
    wkr = sb("a_wkr", [DC, H0, R0])
    wkckv = sb("a_wkckv", [P, H0, DC])
    wo = sb("a_wo", [P, DK, H0 * K0])
    x = sb("a_x", [P, NT, D])
    w2 = sb("a_w2", [P, H0, DK * DCQ])
    rT = sb("a_rT", [R0, H0, DCQ + DC])
    m = sb("a_m", [HALF, H0, 2, DC])
    m2 = sb("a_m2", [HALF, H0, 2, 2, DC])
    woT = sb("a_woT", [P, H0, D])
    wvo = sb("a_wvo", [P, H0 // 2, D])
    junk = sb("a_junk", [P, DK * DCQ])
    norms = sb("a_norms", [P, 2 * H0])
    nsum = sb("a_nsum", [P, 2 * H0])
    bound = sb("a_bound", [P, H0])
    stats = sb("a_stats", [P, NT, 6])
    agg = sb("a_agg", [P, NT, 2])
    root = sb("a_root", [P, NT])
    rstd = sb("a_rstd", [P, NT])
    tmp = sb("a_tmp", [P, NT])
    ones = sb("a_ones", [P, P])
    eps = sb("a_eps", [P, 1])
    ident = sb("a_ident", [P, P])
    psA = [ctx.enter_context(nc.psum_tensor(f"a_psA{i}", [P, 512], F32)) for i in range(4)]
    psD = [ctx.enter_context(nc.psum_tensor(f"a_psD{i}", [P, 512], F32)) for i in range(4)]

    in_q, in_r, in_o, in_x = sem("in_q"), sem("in_r"), sem("in_o"), sem("in_x")
    a_full, a_done = sem("a_full"), sem("a_done")
    d_full, d_done = sem("d_full"), sem("d_done")
    chain = sem("a_chain")
    consts = sem("a_consts")
    var_ready, root_ready, xln_ready = sem("var_ready"), sem("root_ready"), sem("xln_ready")
    norms_ready, b2_ready, bound_ready = sem("norms_ready"), sem("b2_ready"), sem("bound_ready")
    m2_ready, sq_done, stored = sem("m2_ready"), sem("sq_done"), sem("a_stored")

    N_A = H0 + H0 // 2 + H0 // 2
    N_M, N_VO, N_XT = H0 // 2, H0 // 4, NT // 2
    A_RT, A_WOT = H0, H0 + H0 // 2

    with nc.Block() as block:
        @block.sync
        def _(sp):
            sp.dma_start(wq[:], t["L0_xattn_Wq"].rearrange("(h k) d -> k h d", h=H0)).then_inc(in_q, 16)
            sp.dma_start(wkcq[:], t["L0_xattn_w_kc_q"].rearrange("h k q -> k h q")).then_inc(in_q, 16)
            sp.dma_start(ident[:], t["ident"]).then_inc(in_r, 16)
            sp.dma_start(wqr[:], t["L0_xattn_W_qr"].rearrange("h (e q) r -> q h e r", e=2)).then_inc(in_r, 16)
            sp.dma_start(wkr[:], t["L0_xattn_W_kr"].rearrange("h d r -> d h r")).then_inc(in_r, 16)
            sp.dma_start(wo[:], t["L0_xattn_Wo"].rearrange("(c e) k -> e c k", e=P)).then_inc(in_o, 16)
            sp.dma_start(wkckv[:], t["L0_xattn_w_kc_kv"].rearrange("h k d -> k h d")).then_inc(in_o, 16)
            sp.wait_ge(a_done, H0)
            sp.dma_start(t["w2_scr"].rearrange("h p c -> p h c"), w2[:]).then_inc(stored, 16)
            sp.wait_ge(d_done, N_M + N_VO)
            sp.dma_start(t["wvo_scr"], wvo[:]).then_inc(stored, 16)
            sp.wait_ge(m2_ready, 2)
            sp.dma_start(t["m_scr"].rearrange("h p c -> p h c"),
                         m2[:].rearrange("p h a b d -> p h (a b d)")).then_inc(stored, 16)
            sp.wait_ge(stored, 48)

        @block.tensor
        def _(pe):
            pe.wait_ge(in_q, 32)
            for h in range(H0):
                if h >= 4:
                    pe.wait_ge(a_done, h - 3)
                for c in range(DK):
                    mm = pe.matmul(psA[h % 4][:, c * DCQ:(c + 1) * DCQ], wq[:, h, c * P:(c + 1) * P],
                                   wkcq[:, h, :], start=True, stop=True)
                mm.then_inc(a_full, 1)
            pe.wait_ge(in_r, 48)
            for g in range(H0 // 2):
                n = A_RT + g
                pe.wait_ge(a_done, n - 3)
                for u in range(2):
                    h, o = 2 * g + u, u * (DCQ + DC)
                    for e in range(2):
                        pe.transpose(psA[n % 4][0:R0, o + e * HALF:o + (e + 1) * HALF], wqr[:, h, e, :],
                                     ident[0:HALF, 0:HALF])
                    mm = pe.transpose(psA[n % 4][0:R0, o + DCQ:o + DCQ + DC], wkr[:, h, :], ident[0:DC, 0:DC])
                mm.then_inc(a_full, 1)
            pe.wait_ge(in_o, 32)
            for g in range(H0 // 2):
                n = A_WOT + g
                pe.wait_ge(a_done, n - 3)
                for u in range(2):
                    for c in range(DK):
                        mm = pe.transpose(psA[n % 4][:, u * D + c * P:u * D + (c + 1) * P],
                                          wo[:, c, (2 * g + u) * P:(2 * g + u + 1) * P], ident[:])
                mm.then_inc(a_full, 1)
            for g in range(N_M):
                pe.wait_ge(a_done, A_RT + g + 1)
                if g >= 4:
                    pe.wait_ge(d_done, g - 3)
                for u in range(2):
                    h = 2 * g + u
                    for e in range(2):
                        mm = pe.matmul(psD[g % 4][0:HALF, (2 * u + e) * DC:(2 * u + e + 1) * DC],
                                       rT[:, h, e * HALF:(e + 1) * HALF], rT[:, h, DCQ:DCQ + DC],
                                       start=True, stop=True)
                mm.then_inc(d_full, 1)
            for g in range(N_VO):
                n = N_M + g
                pe.wait_ge(a_done, A_WOT + 2 * g + 2)
                pe.wait_ge(d_done, n - 3)
                for u in range(2):
                    for k in range(2):
                        h = 4 * g + 2 * u + k
                        mm = pe.matmul(psD[n % 4][k * DC:(k + 1) * DC, u * D:(u + 1) * D], wkckv[:, h, :],
                                       woT[:, h, :], start=True, stop=True)
                mm.then_inc(d_full, 1)
            pe.wait_ge(norms_ready, 2 * H0)
            pe.wait_ge(consts, 2)
            n = N_M + N_VO
            pe.wait_ge(d_done, n - 3)
            pe.matmul(psD[n % 4][:, 0:2 * H0], ones[:], norms[:], start=True, stop=True).then_inc(d_full, 1)
            for g in range(N_XT):
                n = N_M + N_VO + 1 + g
                pe.wait_ge(xln_ready, 2 * g + 2)
                pe.wait_ge(d_done, n - 3)
                for c in range(DK):
                    for u in range(2):
                        mm = pe.transpose(psD[n % 4][:, c * 256 + u * P:c * 256 + (u + 1) * P],
                                          x[:, 2 * g + u, c * P:(c + 1) * P], ident[:])
                mm.then_inc(d_full, 1)

        @block.scalar
        def _(act):
            act.dma_start(x[:], t["x"].rearrange("b (s p) d -> p (b s) d", p=P)).then_inc(in_x, 16)
            for h in range(H0):
                act.wait_ge(a_full, h + 1)
                nc.scalar.activation(w2[:, h, :], psA[h % 4][:, 0:DK * DCQ], ACT.Copy).then_inc(a_done, 1)
            act.wait_ge(consts, 1)
            act.wait_ge(var_ready, 1)
            nc.scalar.activation(root[:], agg[:, :, 1], ACT.Sqrt, bias=eps[:, 0:1]).then_inc(root_ready, 1)
            for g in range(H0 // 2):
                n = A_RT + g
                act.wait_ge(a_full, n + 1)
                nc.scalar.activation(rT[:, 2 * g:2 * g + 2, :].rearrange("r h c -> r (h c)"),
                                     psA[n % 4][0:R0, :], ACT.Copy).then_inc(a_done, 1)
            for g in range(H0 // 2):
                n = A_WOT + g
                act.wait_ge(a_full, n + 1)
                nc.scalar.activation(woT[:, 2 * g:2 * g + 2, :].rearrange("k h e -> k (h e)"),
                                     psA[n % 4][:, :], ACT.Copy).then_inc(a_done, 1)
            for h in range(H0):
                if h == 0:
                    act.wait_ge(a_done, H0)
                    act.wait_ge(consts, 3)
                else:
                    act.wait_ge(norms_ready, h)
                nc.scalar.activation(junk[:], w2[:, h, :], ACT.Square,
                                     accum_out=norms[:, h:h + 1]).then_inc(norms_ready, 1)
            act.wait_ge(d_done, N_M)
            for h in range(H0):
                act.wait_ge(norms_ready, H0 + h)
                nc.scalar.activation(junk[0:HALF, 0:2 * DC], m[:, h, :, :].rearrange("p e d -> p (e d)"),
                                     ACT.Square,
                                     accum_out=norms[0:HALF, H0 + h:H0 + h + 1]).then_inc(norms_ready, 1)
            act.wait_ge(b2_ready, 1)
            nc.scalar.activation(bound[:], bound[:], ACT.Sqrt).then_inc(bound_ready, 1)

        @block.vector
        def _(dve):
            count = [0]

            def link(ins):
                count[0] += 1
                ins.then_inc(chain, 1)
                dve.wait_ge(chain, count[0])

            link(nc.vector.memset(keep["ln1024"][:], LN_1024))
            nc.vector.memset(eps[:], EPS).then_inc(consts, 1)
            nc.vector.memset(ones[:], 1.0).then_inc(consts, 1)
            nc.vector.memset(norms[:], 0.0).then_inc(consts, 1)
            dve.wait_ge(in_x, 16)
            layer_norm_stats(dve, nc, link, x, stats, agg, NT)
            dve.sem_inc(var_ready, 1)

            def drain_m():
                for g in range(N_M):
                    dve.wait_ge(d_full, g + 1)
                    nc.vector.tensor_copy(m[:, 2 * g:2 * g + 2, :, :].rearrange("p h e d -> p (h e d)"),
                                          psD[g % 4][0:HALF, 0:4 * DC]).then_inc(d_done, 1)

            drain_m()
            dve.wait_ge(root_ready, 1)
            rstd_refined(nc, link, rstd[:], root[:], agg, tmp[:])
            for j in range(NT):
                nc.vector.tensor_scalar(x[:, j, :], x[:, j, :], agg[:, j, 0:1], rstd[:, j:j + 1],
                                        ALU.subtract, ALU.mult).then_inc(xln_ready, 1)
            for g in range(N_VO):
                n = N_M + g
                dve.wait_ge(d_full, n + 1)
                nc.vector.tensor_copy(wvo[:, 2 * g:2 * g + 2, :].rearrange("p g e -> p (g e)"),
                                      psD[n % 4][:, :]).then_inc(d_done, 1)
            n = N_M + N_VO
            dve.wait_ge(d_full, n + 1)
            nc.vector.tensor_copy(nsum[:], psD[n % 4][:, 0:2 * H0]).then_inc(d_done, 1)
            dve.wait_ge(d_done, n + 1)
            link(nc.vector.tensor_tensor(bound[:], nsum[:, 0:H0], nsum[:, H0:2 * H0], ALU.mult))
            link(nc.vector.tensor_scalar(bound[:], bound[:], 4.0 * D, 1e-30, ALU.mult, ALU.add))
            dve.sem_inc(b2_ready, 1)
            dve.wait_ge(bound_ready, 1)
            link(nc.vector.reciprocal(bound[:], bound[:]))
            link(nc.vector.tensor_scalar(keep["qscale"][:], bound[:], QK_TOP, None, ALU.mult))
            for k in range(2):
                nc.vector.tensor_tensor(
                    m2[:, :, :, k, :], m[:],
                    keep["qscale"][0:HALF, :].unsqueeze(2).unsqueeze(3).broadcast_to([HALF, H0, 2, DC]),
                    ALU.mult).then_inc(m2_ready, 1)
            for g in range(N_XT):
                n = N_M + N_VO + 1 + g
                dve.wait_ge(d_full, n + 1)
                nc.vector.tensor_copy(keep["xT"][:, :, 256 * g:256 * (g + 1)],
                                      psD[n % 4][:].rearrange("p (c s) -> p c s", c=DK)).then_inc(d_done, 1)


def phase_context(nc, ctx, t, keep):
    def sb(name, shape, dt=F32):
        return ctx.enter_context(nc.sbuf_tensor(name, shape, dt))

    def sem(name):
        return new_semaphore(nc, name)

    kv = sb("b_kv", [P, B, LT, DC])
    rot = sb("b_rot", [P, B, LT, DC])
    cosk = sb("b_cosk", [P, LT, DC])
    sink = sb("b_sink", [P, LT, DC])
    amax = sb("b_amax", [P, B])
    aall = sb("b_aall", [P, B])
    ktop = sb("b_ktop", [P, 1])
    kscale = sb("b_kscale", [P, 1])
    ps = [ctx.enter_context(nc.psum_tensor(f"b_ps{i}", [P, 1024], F16)) for i in range(8)]
    in_t, in_ident, zeroed = sem("in_t"), sem("in_ident"), sem("b_zeroed")
    in_k = [sem(f"in_k{b}") for b in range(B)]
    rotated, roped, chain = sem("rotated"), sem("roped"), sem("b_chain")
    amax_ready, aall_ready = sem("amax_ready"), sem("aall_ready")
    v_ready, kt_full, k1_done, k2_done = sem("v_ready"), sem("kt_full"), sem("k1_done"), sem("k2_done")
    filled = sem("b_filled")
    V, KK1, KK2 = keep["V"], keep["KK1"], keep["KK2"]
    FIRST = 7
    jobs = [(b, lo, hi) for b in range(B) for lo, hi in ((0, FIRST), (FIRST, LT))]

    with nc.Block() as block:
        @block.sync
        def _(sp):
            sp.dma_start(cosk[:], t["cosk"]).then_inc(in_t, 16)
            sp.dma_start(sink[:], t["sink"]).then_inc(in_t, 16)
            sp.wait_ge(zeroed, 1)
            for b in range(B):
                sp.dma_start(kv[:, b, 0:LT - 1, :],
                             t["ctx_512"][b, 0:(LT - 1) * P, :].rearrange("(t p) d -> p t d", p=P)
                             ).then_inc(in_k[b], 16)
                sp.dma_start(kv[0:LLAST, b, LT - 1, :], t["ctx_512"][b, (LT - 1) * P:L, :]).then_inc(in_k[b], 16)

        @block.gpsimd
        def _(pool):
            nc.gpsimd.memset(kv[:, :, LT - 1, :], 0.0).then_inc(zeroed, 1)
            pool.wait_ge(in_t, 32)
            h = DC // 2
            for b in range(B):
                pool.wait_ge(in_k[b], 32)
                nc.gpsimd.tensor_tensor(rot[:, b, :, 0:h], kv[:, b, :, h:DC], sink[:, :, 0:h],
                                        ALU.mult).then_inc(rotated, 1)
                nc.gpsimd.tensor_tensor(rot[:, b, :, h:DC], kv[:, b, :, 0:h], sink[:, :, h:DC],
                                        ALU.mult).then_inc(rotated, 1)
            pool.wait_ge(amax_ready, B)
            nc.gpsimd.partition_all_reduce(aall[:], amax[:], P, bass.bass_isa.ReduceOp.max
                                           ).then_inc(aall_ready, 1)
            pool.wait_ge(aall_ready, 1)
            nc.gpsimd.memset(KK2[0:2 * SHIFT_ROWS, :], SHIFT_ONE).then_inc(filled, 1)
            pool.wait_ge(filled, 1)
            nc.gpsimd.memset(KK2[2 * SHIFT_ROWS:DC, :], 0.0).then_inc(filled, 1)
            pool.wait_ge(filled, 2)

        @block.vector
        def _(dve):
            count = [0]

            def link(ins):
                count[0] += 1
                ins.then_inc(chain, 1)
                dve.wait_ge(chain, count[0])

            def drain(b):
                for k in range(2):
                    n = 2 * b + k
                    _, lo, hi = jobs[n]
                    w = min(hi * P, L) - lo * P
                    dve.wait_ge(k1_done, n + 1)
                    nc.vector.tensor_copy(KK2[DC:P, b * L + lo * P:b * L + lo * P + w],
                                          KK1[DC:P, b * L + lo * P:b * L + lo * P + w]).then_inc(k2_done, 1)

            for b in range(B):
                nc.vector.memset(V[:, b, :, 2 * DC:2 * DC + 1], 1.0).then_inc(v_ready, 1)
            dve.wait_ge(in_t, 32)
            for b in range(B):
                dve.wait_ge(rotated, 2 * (b + 1))
                dve.wait_ge(in_k[b], 32)
                link(nc.vector.tensor_tensor(kv[:, b], kv[:, b], cosk[:], ALU.mult))
                nc.vector.tensor_tensor(kv[:, b], kv[:, b], rot[:, b], ALU.add).then_inc(roped, 1)
                dve.wait_ge(roped, b + 1)
                nc.vector.tensor_reduce(amax[:, b:b + 1], kv[:, b], AX.XY, ALU.max,
                                        apply_absolute_value=True).then_inc(amax_ready, 1)
            dve.wait_ge(aall_ready, 1)
            link(nc.vector.tensor_reduce(ktop[:], aall[:], AX.X, ALU.max))
            link(nc.vector.tensor_scalar(ktop[:], ktop[:], 1e-30, 1.0 / QK_TOP, ALU.add, ALU.mult))
            link(nc.vector.reciprocal(kscale[:], ktop[:]))
            link(nc.vector.tensor_scalar(keep["qk_scale"][:], keep["qscale"][:], kscale[:, 0:1], None, ALU.mult))
            link(nc.vector.reciprocal(keep["qk_scale"][:], keep["qk_scale"][:]))
            link(nc.vector.tensor_copy(keep["k_unscale"][:], ktop[:]))
            for b in range(B):
                link(nc.vector.tensor_scalar(V[:, b, :, DC:2 * DC], kv[:, b], kscale[:, 0:1], None, ALU.mult))
                nc.vector.scalar_tensor_tensor(out=V[:, b, :, 0:DC], in0=kv[:, b], scalar=kscale[:, 0:1],
                                               in1=V[:, b, :, DC:2 * DC], op0=ALU.mult,
                                               op1=ALU.subtract).then_inc(v_ready, 1)
                if b >= 1:
                    drain(b - 1)
            drain(B - 1)

        @block.tensor
        def _(pe):
            pe.wait_ge(in_ident, 16)
            for n, (b, lo, hi) in enumerate(jobs):
                pe.wait_ge(v_ready, B + b + 1)
                if n >= 8:
                    pe.wait_ge(k1_done, n - 7)
                for i in range(lo, hi):
                    r = P if i < LT - 1 else LLAST
                    mm = pe.transpose(ps[n % 8][:, (i - lo) * P:(i - lo) * P + r], V[0:r, b, i, 0:2 * DC],
                                      keep["ident16"][0:r, 0:r])
                mm.then_inc(kt_full, 1)

        @block.scalar
        def _(act):
            act.dma_start(keep["ident16"][:], t["ident16"]).then_inc(in_ident, 16)
            for n, (b, lo, hi) in enumerate(jobs):
                w = min(hi * P, L) - lo * P
                act.wait_ge(kt_full, n + 1)
                nc.scalar.activation(KK1[:, b * L + lo * P:b * L + lo * P + w], ps[n % 8][:, 0:w],
                                     ACT.Copy).then_inc(k1_done, 1)


def phase_attention0(nc, ctx, t, keep):
    def sb(name, shape, dt=F32):
        return ctx.enter_context(nc.sbuf_tensor(name, shape, dt))

    def sem(name):
        return new_semaphore(nc, name)

    V, KK1, KK2, xT = keep["V"], keep["KK1"], keep["KK2"], keep["xT"]
    ident16 = keep["ident16"]
    tabA = sb("c_tabA", [HALF, 2 * S])
    tabB = sb("c_tabB", [HALF, 2 * S])
    w2s = sb("c_w2s", [P, DK * DCQ])
    ms = sb("c_ms", [HALF, 2, P])
    ropeA = sb("c_ropeA", [HALF, 2, S])
    ropeB = sb("c_ropeB", [HALF, 2, S])
    q1 = [sb(f"c_q1_{i}", [P, S], F16) for i in range(2)]
    q2 = [sb(f"c_q2_{i}", [P, S], F16) for i in range(2)]
    prob = [sb(f"c_prob{i}", [P, 4 * S]) for i in range(2)]
    rest = [sb(f"c_rest{i}", [P, 4 * S], F16) for i in range(2)]
    mxp = sb("c_mxp", [P, ST, 2])
    mx = sb("c_mx", [P, ST])
    mcol = sb("c_mcol", [P, ST, DC], F16)
    exp_scale = [sb(f"c_exp_scale{i}", [P, 1]) for i in range(2)]
    W = 2 * DC + 1
    acc = [sb(f"c_acc{i}", [P, ST, W]) for i in range(2)]
    psS = [ctx.enter_context(nc.psum_tensor(f"c_psS{i}", [P, 1024], F32)) for i in range(2)]
    psM = ctx.enter_context(nc.psum_tensor("c_psM", [P, 2, 512], F32))
    psQ = ctx.enter_context(nc.psum_tensor("c_psQ", [P, 512], F32))
    psV = ctx.enter_context(nc.psum_tensor("c_psV", [P, 512], F32))
    shiftT = psV[0:DC, 384:512].bitcast(F16)

    in_tab, in_w2, in_m = sem("in_tab"), sem("in_w2"), sem("in_m")
    qb_full, rope_done, qk_full = sem("qb_full"), sem("rope_done"), sem("qk_full")
    qh_done, ql_done = sem("qh_done"), sem("ql_done")
    mx_full, mx_done, mx_joined, mcol_done = sem("mx_full"), sem("mx_done"), sem("mx_joined"), sem("mcol_done")
    shift_full, shift_done = sem("shift_full"), sem("shift_done")
    s_full, exp_done = sem("s_full"), sem("exp_done")
    rest_dve, rest_pool = sem("rest_dve"), sem("rest_pool")
    pv_done = sem("pv_done")
    pv_drained = sem("pv_drained")
    sent = [sem(f"sent{i}") for i in range(2)]
    zeroed = sem("c_zeroed")
    begun = sem("begun")

    N = B * H0
    GROUPS = [(0, 4), (4, 8), (8, 12), (12, 13)]
    HALF_L = 400
    TAIL = L - 3 * HALF_L
    CHUNKS = [((0, HALF_L), (HALF_L, HALF_L)), ((L - 2 * TAIL, TAIL), (L - TAIL, TAIL))]
    POOL_COLS = 704

    def head(n):
        return n % H0

    def batch(n):
        return (n // H0) % B

    with nc.Block() as block:
        @block.sync
        def _(sp):
            sp.sem_inc(begun, 1)
            sp.dma_start(tabA[:], t["tabA"]).then_inc(in_tab, 16)
            sp.dma_start(tabB[:], t["tabB"]).then_inc(in_tab, 16)

            def load_w2(n):
                sp.dma_start(w2s[:], t["w2_scr"][head(n)]).then_inc(in_w2, 16)

            def load_m(n):
                sp.dma_start(ms[:], t["m_scr"][head(n)].rearrange("p (a b) -> p a b", a=2)).then_inc(in_m, 16)

            load_w2(0)
            load_m(0)
            sp.wait_ge(qb_full, 1)
            load_w2(1)
            sp.wait_ge(qk_full, 1)
            load_m(1)
            sp.sem_inc(sent[0], 16)
            sp.sem_inc(sent[1], 16)
            with sp.Fori(0, N // 2) as j:
                for u in range(2):
                    n = 2 * j + u
                    sp.wait_ge(qb_full, n + 2)
                    load_w2(n + 2)
                    sp.wait_ge(qk_full, n + 2)
                    load_m(n + 2)
                    sp.wait_ge(pv_drained, n + 2)
                    sp.dma_start(t["acc_scr"][n], acc[u][:]).then_inc(sent[u], 16)
            for u in range(2):
                sp.wait_ge(sent[u], 16 + 16 * (N // 2))
            sp.wait_ge(in_w2, 16 * (N + 2))
            sp.wait_ge(in_m, 16 * (N + 2))

        @block.tensor
        def _(pe):
            def q_big(n, b, e):
                if e == 0:
                    pe.wait_ge(in_w2, 16 * (n + 1))
                for c in range(DK):
                    mm = pe.matmul(psQ[0:HALF, e * S:(e + 1) * S],
                                   w2s[:, c * DCQ + e * HALF:c * DCQ + (e + 1) * HALF],
                                   xT[:, c, bass.ds(b * S, S)], start=(c == 0), stop=(c == DK - 1))
                if e == 1:
                    mm.then_inc(qb_full, 1)

            def q_lat(n):
                pe.wait_ge(rope_done, 2 * n + 2)
                pe.wait_ge(in_m, 16 * (n + 1))
                terms = [(0, ropeA[:, 0, :]), (1, ropeA[:, 1, :]), (1, ropeB[:, 0, :]), (0, ropeB[:, 1, :])]
                for i, (e, r) in enumerate(terms):
                    mm = pe.matmul(psQ[:, 0:S], ms[:, e, :], r, start=(i == 0), stop=(i == 3))
                mm.then_inc(qk_full, 1)

            def maxima(n, b, k, slot):
                st, half = divmod(k, 2)
                if not (isinstance(n, int) and n == 0 and k == 0):
                    pe.wait_ge(mx_done, 4 * n + k)
                for i, (c0, w) in enumerate(CHUNKS[half]):
                    mm = pe.matmul(psM[:, i, 0:w], q1[slot][:, st * P:(st + 1) * P],
                                   KK1[:, bass.ds(b * L + c0, w)], start=True, stop=True)
                mm.then_inc(mx_full, 1)

            def shift(n):
                pe.wait_ge(begun, 1)
                pe.wait_ge(mcol_done, 2 * n + 2)
                pe.wait_ge(pv_drained, n + 1)
                for st in range(ST):
                    mm = pe.transpose(shiftT[:, st * P:(st + 1) * P], mcol[:, st, :], ident16[:])
                mm.then_inc(shift_full, 1)

            def scores(n, b, g, part, slot):
                lo, hi = GROUPS[g]
                if part != 1:
                    pe.wait_ge(exp_done, 4 * n + g + 1)
                for one in ((0, 1) if part is None else (part,)):
                    for i in range(lo, hi):
                        r = P if i < LT - 1 else LLAST
                        src, mov = ((KK1, q1), (KK2, q2))[one]
                        mm = pe.matmul(psS[g % 2][0:r, (i - lo) * S:(i - lo + 1) * S],
                                       src[:, bass.ds(b * L + i * P, r)], mov[slot][:, :],
                                       start=(one == 0 and (i - lo) % 2 == 0),
                                       stop=(one == 1), skip_group_check=True)
                if part != 0:
                    mm.then_inc(s_full, 1)

            def values(n, b, g):
                lo, hi = GROUPS[g]
                if g == 0:
                    pe.wait_ge(pv_drained, n + 1)
                if g < 3:
                    pe.wait_ge(rest_pool, 3 * n + g + 1)
                pe.wait_ge(rest_dve, 4 * n + g + 1)
                high = prob[g % 2][:].bitcast(BF16).rearrange("p (c t) -> p c t", t=2)[:, :, 1]
                for i in range(lo, hi):
                    r = P if i < LT - 1 else LLAST
                    for st in range(ST):
                        c0 = (i - lo) * S + st * P
                        pe.matmul(psV[:, st * W:(st + 1) * W], high[0:r, c0:c0 + P],
                                  V[0:r, bass.ds(b, 1), i, :].rearrange("p o w -> p (o w)"),
                                  start=(i == 0 and st == 0), stop=False, skip_group_check=True)
                        mm = pe.matmul(psV[:, st * W + DC:(st + 1) * W], rest[g % 2][0:r, c0:c0 + P],
                                       V[0:r, bass.ds(b, 1), i, DC:W].rearrange("p o w -> p (o w)"),
                                       start=False, stop=(i == LT - 1), skip_group_check=True)
                mm.then_inc(pv_done, 1)

            pe.sem_inc(pv_done, 2)
            q_big(0, 0, 0)
            q_big(0, 0, 1)
            q_lat(0)
            pe.wait_ge(qh_done, 1)
            for k in range(4):
                maxima(0, 0, k, 0)
            pe.wait_ge(ql_done, 1)
            q_big(1, 0, 0)
            q_big(1, 0, 1)
            scores(0, 0, 0, 0, 0)
            shift(0)
            with pe.Fori(0, N // 2) as j:
                for u in range(2):
                    n = 2 * j + u
                    v = 1 - u
                    b0, b1, b2 = batch(n), batch(n + 1), batch(n + 2)
                    pe.wait_ge(shift_done, n + 1)
                    pe.wait_ge(ql_done, n + 1)
                    scores(n, b0, 0, 1, u)
                    q_lat(n + 1)
                    scores(n, b0, 1, None, u)
                    pe.wait_ge(qh_done, n + 2)
                    maxima(n + 1, b1, 0, v)
                    values(n, b0, 0)
                    scores(n, b0, 2, None, u)
                    maxima(n + 1, b1, 1, v)
                    values(n, b0, 1)
                    scores(n, b0, 3, None, u)
                    maxima(n + 1, b1, 2, v)
                    pe.wait_ge(ql_done, n + 2)
                    q_big(n + 2, b2, 0)
                    maxima(n + 1, b1, 3, v)
                    q_big(n + 2, b2, 1)
                    values(n, b0, 2)
                    values(n, b0, 3)
                    scores(n + 1, b1, 0, 0, v)
                    shift(n + 1)

        @block.scalar
        def _(act):
            def q_high(n, slot):
                act.wait_ge(qk_full, n + 1)
                nc.scalar.activation(q1[slot][:], psQ[:, 0:S], ACT.Copy).then_inc(qh_done, 1)

            def shift_copy(n, slot):
                act.wait_ge(shift_full, n + 1)
                nc.scalar.activation(q2[slot][0:DC, :], shiftT, ACT.Copy).then_inc(shift_done, 1)

            def exp(n, g, slot):
                lo, hi = GROUPS[g]
                r = P if hi < LT else LLAST
                w = (hi - lo) * S
                act.wait_ge(s_full, 4 * n + g + 1)
                act.wait_ge(pv_done, 4 * n + g + 1)
                nc.scalar.activation(prob[g % 2][0:r, 0:w], psS[g % 2][0:r, 0:w], ACT.Exp, bias=keep["ln1024"][0:r, :],
                                     scale=exp_scale[slot][0:r, :]).then_inc(exp_done, 1)

            act.sem_inc(exp_done, 2)
            act.sem_inc(pv_drained, 1)
            q_high(0, 0)
            shift_copy(0, 0)
            with act.Fori(0, N // 2) as j:
                for u in range(2):
                    n = 2 * j + u
                    exp(n, 0, u)
                    q_high(n + 1, 1 - u)
                    exp(n, 1, u)
                    exp(n, 2, u)
                    exp(n, 3, u)
                    act.wait_ge(pv_done, 4 * n + 6)
                    act.wait_ge(sent[u], 16 * j + 16)
                    nc.scalar.activation(acc[u][:].rearrange("p s w -> p (s w)"), psV[:, 0:ST * W],
                                         ACT.Copy).then_inc(pv_drained, 1)
                    shift_copy(n + 1, 1 - u)

        @block.vector
        def _(dve):
            def rope(n):
                dve.wait_ge(qb_full, n + 1)
                if not isinstance(n, int) or n > 0:
                    dve.wait_ge(qk_full, n)
                for out, tab in ((ropeA, tabA), (ropeB, tabB)):
                    nc.vector.tensor_tensor(out[:].rearrange("p e s -> p (e s)"), psQ[0:HALF, :], tab[:],
                                            ALU.mult).then_inc(rope_done, 1)

            def q_low(n, slot):
                dve.wait_ge(qh_done, n + 1)
                nc.vector.tensor_tensor(q2[slot][DC:P, :], psQ[DC:P, 0:S], q1[slot][DC:P, :],
                                        ALU.subtract).then_inc(ql_done, 1)

            def reduce_max(n, k):
                st, half = divmod(k, 2)
                dve.wait_ge(mx_full, 4 * n + k + 1)
                w = CHUNKS[half][0][1]
                nc.vector.tensor_reduce(mxp[:, st, half:half + 1], psM[:, :, 0:w], AX.XY,
                                        ALU.max).then_inc(mx_done, 1)

            def join(n, slot):
                dve.wait_ge(mx_done, 4 * n + 4)
                nc.vector.tensor_scalar(exp_scale[slot][:], keep["qk_scale"][:, bass.ds(head(n), 1)], 1.0, None,
                                        ALU.mult).then_inc(mx_joined, 1)
                nc.vector.tensor_reduce(mx[:], mxp[:], AX.X, ALU.max).then_inc(mx_joined, 1)
                dve.wait_ge(mx_joined, 2 * n + 2)
                if not isinstance(n, int) or n > 0:
                    dve.wait_ge(shift_full, n)
                m = mx[:].unsqueeze(2).broadcast_to([P, ST, SHIFT_ROWS])
                nc.vector.tensor_scalar(mcol[:, :, 0:SHIFT_ROWS], m, -SHIFT_MUL, None,
                                        ALU.mult).then_inc(mcol_done, 1)
                dve.wait_ge(mcol_done, 2 * n + 1)
                nc.vector.scalar_tensor_tensor(out=mcol[:, :, SHIFT_ROWS:2 * SHIFT_ROWS], in0=m,
                                               scalar=-SHIFT_MUL, in1=mcol[:, :, 0:SHIFT_ROWS],
                                               op0=ALU.mult, op1=ALU.subtract).then_inc(mcol_done, 1)

            def rest_of(n, g):
                lo, hi = GROUPS[g]
                r = P if hi < LT else LLAST
                c0, c1 = (POOL_COLS if g < 3 else 0), (hi - lo) * S
                dve.wait_ge(exp_done, 4 * n + g + 3)
                high = prob[g % 2][:].bitcast(BF16).rearrange("p (c t) -> p c t", t=2)[:, :, 1]
                nc.vector.tensor_tensor(rest[g % 2][0:r, c0:c1], prob[g % 2][0:r, c0:c1], high[0:r, c0:c1],
                                        ALU.subtract).then_inc(rest_dve, 1)

            nc.vector.memset(mcol[:], 0.0).then_inc(zeroed, 1)
            dve.wait_ge(zeroed, 1)
            dve.wait_ge(in_tab, 32)
            rope(0)
            q_low(0, 0)
            for k in range(4):
                reduce_max(0, k)
            join(0, 0)
            rope(1)
            with dve.Fori(0, N // 2) as j:
                for u in range(2):
                    n = 2 * j + u
                    rest_of(n, 0)
                    q_low(n + 1, 1 - u)
                    reduce_max(n + 1, 0)
                    rest_of(n, 1)
                    reduce_max(n + 1, 1)
                    rest_of(n, 2)
                    reduce_max(n + 1, 2)
                    rest_of(n, 3)
                    reduce_max(n + 1, 3)
                    join(n + 1, 1 - u)
                    rope(n + 2)

        @block.gpsimd
        def _(pool):
            with pool.Fori(0, N // 2) as j:
                for u in range(2):
                    n = 2 * j + u
                    for g in range(3):
                        pool.wait_ge(exp_done, 4 * n + g + 3)
                        high = prob[g % 2][:].bitcast(BF16).rearrange("p (c t) -> p c t", t=2)[:, :, 1]
                        nc.gpsimd.tensor_tensor(rest[g % 2][:, 0:POOL_COLS], prob[g % 2][:, 0:POOL_COLS],
                                                high[:, 0:POOL_COLS], ALU.subtract).then_inc(rest_pool, 1)


def phase_project0(nc, ctx, t, keep, x):
    def sb(name, shape, dt=F32):
        return ctx.enter_context(nc.sbuf_tensor(name, shape, dt))

    def sem(name):
        return new_semaphore(nc, name)

    W = 2 * DC + 1
    G = H0 // 2
    wvo = sb("d_wvo", [P, G, D])
    ident = sb("d_ident", [P, P])
    acc = [sb(f"d_acc{i}", [P, H0, ST, W]) for i in range(2)]
    cs = [sb(f"d_cs{i}", [P, ST, H0, DC]) for i in range(2)]
    rec = sb("d_rec", [P, H0, ST])
    cT = [sb(f"d_cT{i}", [P, G, P]) for i in range(2)]
    psT = [ctx.enter_context(nc.psum_tensor(f"d_psT{i}", [P, 512], F32)) for i in range(4)]
    psO = [ctx.enter_context(nc.psum_tensor(f"d_psO{i}", [P, 512], F32)) for i in range(2)]
    in_c = sem("d_in_c")
    in_x = sem("d_in_x")
    in_acc = [sem(f"d_in_acc{i}") for i in range(2)]
    chain, cs_ready, cs_read = sem("d_chain"), sem("cs_ready"), sem("cs_read")
    t_full, t_done, o_full, o_done = sem("d_t_full"), sem("d_t_done"), sem("d_o_full"), sem("d_o_done")

    with nc.Block() as block:
        @block.sync
        def _(sp):
            sp.dma_start(ident[:], t["ident"]).then_inc(in_c, 16)
            sp.dma_start(wvo[:], t["wvo_scr"]).then_inc(in_c, 16)
            sp.dma_start(x[:], t["x"].rearrange("b (s p) d -> p (b s) d", p=P)).then_inc(in_x, 16)

            with sp.Fori(0, B // 2) as j:
                for u in range(2):
                    b = 2 * j + u
                    sp.wait_ge(cs_read, b + 1)
                    sp.dma_start(acc[u][:].rearrange("p h s w -> p h (s w)"),
                                 t["acc_scr"][bass.ds(b * H0, H0)].rearrange("h p s w -> p h (s w)")
                                 ).then_inc(in_acc[u], 16)

        @block.vector
        def _(dve):
            dve.sem_inc(cs_read, 2)
            dve.sem_inc(o_done, 2)
            dve.wait_ge(in_x, 16)
            with dve.Fori(0, B // 2) as j:
                for u in range(2):
                    b = 2 * j + u
                    dve.wait_ge(in_acc[u], 16 * j + 16)
                    dve.wait_ge(t_full, 4 * b + 1)
                    nc.vector.reciprocal(rec[:], acc[u][:, :, :, 2 * DC]).then_inc(chain, 1)
                    nc.vector.tensor_tensor(cs[u][:].rearrange("p s h d -> p h s d"), acc[u][:, :, :, 0:DC],
                                            acc[u][:, :, :, DC:2 * DC], ALU.add).then_inc(chain, 1)
                    dve.wait_ge(chain, 4 * b + 2)
                    dve.sem_inc(cs_read, 1)
                    nc.vector.tensor_scalar(rec[:], rec[:], keep["k_unscale"][:, 0:1], None,
                                            ALU.mult).then_inc(chain, 1)
                    dve.wait_ge(chain, 4 * b + 3)
                    nc.vector.tensor_tensor(cs[u][:].rearrange("p s h d -> p h s d"),
                                            cs[u][:].rearrange("p s h d -> p h s d"),
                                            rec[:].unsqueeze(3).broadcast_to([P, H0, ST, DC]),
                                            ALU.mult).then_inc(chain, 1)
                    dve.wait_ge(chain, 4 * b + 4)
                    dve.sem_inc(cs_ready, 1)
                    for s in range(ST):
                        dve.wait_ge(o_full, 2 * b + s + 3)
                        xt = x[:, bass.ds(2 * b + s, 1), :].rearrange("p o d -> p (o d)")
                        nc.vector.tensor_tensor(xt, xt, psO[s][:, 0:D], ALU.add).then_inc(o_done, 1)

        @block.tensor
        def _(pe):
            pe.wait_ge(in_c, 32)
            pe.sem_inc(t_full, 5)
            pe.sem_inc(o_full, 2)
            with pe.Fori(0, B // 2) as j:
                for u in range(2):
                    b = 2 * j + u
                    pe.wait_ge(cs_ready, b + 1)
                    for s in range(ST):
                        for half in range(2):
                            pe.wait_ge(t_done, 4 * b + 2 * s + half + 1)
                            for g in range(4):
                                h = 2 * (4 * half + g)
                                mm = pe.transpose(psT[2 * s + half][:, g * P:(g + 1) * P],
                                                  cs[u][:, s, h:h + 2, :].rearrange("p h d -> p (h d)"), ident[:])
                            mm.then_inc(t_full, 1)
                    for s in range(ST):
                        pe.wait_ge(t_done, 4 * b + 2 * s + 6)
                        pe.wait_ge(o_done, 2 * b + s + 1)
                        for g in range(G):
                            mm = pe.matmul(psO[s][:, 0:D], cT[s][:, g, :], wvo[:, g, :],
                                           start=(g == 0), stop=(g == G - 1))
                        mm.then_inc(o_full, 1)

        @block.scalar
        def _(act):
            act.sem_inc(t_done, 4)
            with act.Fori(0, B // 2) as j:
                for u in range(2):
                    b = 2 * j + u
                    for s in range(ST):
                        for half in range(2):
                            act.wait_ge(t_full, 4 * b + 2 * s + half + 6)
                            if half == 0:
                                act.wait_ge(o_full, 2 * b + s + 1)
                            nc.scalar.activation(
                                cT[s][:, 4 * half:4 * half + 4, :].rearrange("p g c -> p (g c)"),
                                psT[2 * s + half][:], ACT.Copy).then_inc(t_done, 1)


def phase_norm(nc, ctx, t, x, xn, xT, tag):
    def sb(name, shape, dt=F32):
        return ctx.enter_context(nc.sbuf_tensor(tag + name, shape, dt))

    def sem(name):
        return new_semaphore(nc, tag + name)

    ident = sb("ident", [P, P])
    stats = sb("stats", [P, NT, 6])
    agg = sb("agg", [P, NT, 2])
    root = sb("root", [P, NT])
    rstd = sb("rstd", [P, NT])
    tmp = sb("tmp", [P, NT])
    eps = sb("eps", [P, 1])
    ps = [ctx.enter_context(nc.psum_tensor(f"{tag}ps{i}", [P, 512], F32)) for i in range(8)]
    in_c, chain, var_ready, root_ready = sem("in_c"), sem("chain"), sem("var"), sem("root_ready")
    xn_ready, full, done = sem("xn_ready"), sem("full"), sem("done")

    with nc.Block() as block:
        @block.sync
        def _(sp):
            sp.dma_start(ident[:], t["ident"]).then_inc(in_c, 16)

        @block.vector
        def _(dve):
            count = [0]

            def link(ins):
                count[0] += 1
                ins.then_inc(chain, 1)
                dve.wait_ge(chain, count[0])

            link(nc.vector.memset(eps[:], EPS))
            layer_norm_stats(dve, nc, link, x, stats, agg, NT)
            dve.sem_inc(var_ready, 1)
            dve.wait_ge(root_ready, 1)
            rstd_refined(nc, link, rstd[:], root[:], agg, tmp[:])
            for j in range(NT):
                nc.vector.tensor_scalar(xn[:, j, :], x[:, j, :], agg[:, j, 0:1], rstd[:, j:j + 1],
                                        ALU.subtract, ALU.mult).then_inc(xn_ready, 1)

        @block.tensor
        def _(pe):
            pe.wait_ge(in_c, 16)
            for g in range(NT // 2):
                pe.wait_ge(xn_ready, 2 * g + 2)
                for c in range(DK):
                    for u in range(2):
                        mm = pe.transpose(ps[g][:, c * 256 + u * P:c * 256 + (u + 1) * P],
                                          xn[:, 2 * g + u, c * P:(c + 1) * P], ident[:])
                mm.then_inc(full, 1)

        @block.scalar
        def _(act):
            act.wait_ge(var_ready, 1)
            nc.scalar.activation(root[:], agg[:, :, 1], ACT.Sqrt, bias=eps[:, 0:1]).then_inc(root_ready, 1)
            for g in range(NT // 2):
                act.wait_ge(full, g + 1)
                nc.scalar.activation(xT[:, :, 256 * g:256 * (g + 1)],
                                     ps[g][:].rearrange("p (c s) -> p c s", c=DK), ACT.Copy).then_inc(done, 1)


CAP = 64
DFF = 1024
FT = DFF // P
NSEL = B * CAP
SEL_T = NSEL // P
OUT_OF_RANGE = 16384.0


def phase_ffn0(nc, ctx, t, x, xn, xT):
    def sb(name, shape, dt=F32):
        return ctx.enter_context(nc.sbuf_tensor("e_" + name, shape, dt))

    def sem(name):
        return new_semaphore(nc, "e_" + name)

    ident = sb("ident", [P, P])
    upper = sb("upper", [P, P], BF16)
    onesb = sb("ones", [P, P], BF16)
    wr = sb("wr", [P, DK])
    wrb = sb("wrb", [P, DK, P])
    onesf = sb("onesf", [P, P])
    br = sb("br", [P, 1])
    b1 = sb("b1", [P, FT])
    b2 = sb("b2", [P, D])
    w1 = sb("w1", [P, DK, DFF])
    w2 = sb("w2", [P, FT, D])
    rows = sb("rows", [P, NT * P])
    diag = sb("diag", [P, NT, P])
    wcol = sb("wcol", [P, NT])
    ge = sb("ge", [P, S])
    cnt = sb("cnt", [P, NT])
    sel = sb("sel", [P, NT])
    selb = sb("selb", [P, NT], BF16)
    slot = sb("slot", [P, NT])
    base = sb("base", [P, NT])
    s_idx = sb("s_idx", [P, NT], U32)
    g_idx = sb("g_idx", [P, NT], U32)
    gate = sb("gate", [P, NT])
    left = sb("left", [P, NT])
    zero = sb("zero", [P, SEL_T, D])
    xg = sb("xg", [P, SEL_T, D])
    xgT = sb("xgT", [P, DK, NSEL])
    hT = sb("hT", [P, FT, NSEL])
    y = sb("y", [P, SEL_T, D])
    back = sb("back", [P, NT, D])
    ps = [ctx.enter_context(nc.psum_tensor(f"e_ps{i}", [P, 512], F32)) for i in range(8)]
    in_c, in_w, in_z = sem("in_c"), sem("in_w"), sem("in_z")
    made, wrb_made, chain = sem("made"), sem("wrb_made"), sem("chain")
    r_full, r_done, sel_ready, cum_full, idx_ready = (sem("r_full"), sem("r_done"), sem("sel_ready"),
                                                      sem("cum_full"), sem("idx_ready"))
    scattered, in_xg, t_full, t_done = sem("scattered"), sem("in_xg"), sem("t_full"), sem("t_done")
    h_full, h_done, y_full, y_done = sem("h_full"), sem("h_done"), sem("y_full"), sem("y_done")
    stored, gathered = sem("stored"), sem("gathered")
    NB = NT * P // 512

    with nc.Block() as block:
        @block.sync
        def _(sp):
            sp.dma_start(ident[:], t["ident"]).then_inc(in_c, 16)
            sp.dma_start(upper[:], t["upper"]).then_inc(in_c, 16)
            sp.dma_start(base[:], t["cap_base"]).then_inc(in_c, 16)
            sp.dma_start(wr[:], t["L0_ffn_W_r"].rearrange("(c d) o -> d (c o)", d=P),
                         allow_slow_non_contiguous=True).then_inc(in_c, 16)
            sp.dma_start(br[:], t["L0_ffn_b_r"].partition_broadcast(P)).then_inc(in_c, 16)
            sp.dma_start(b1[:], t["L0_ffn_b1"].rearrange("(f p) -> p f", p=P),
                         allow_slow_non_contiguous=True).then_inc(in_w, 16)
            sp.dma_start(b2[:], t["L0_ffn_b2"].partition_broadcast(P)).then_inc(in_w, 16)
            sp.dma_start(w1[:], t["L0_ffn_W1"].rearrange("(c d) f -> d c f", d=P)).then_inc(in_w, 16)
            sp.dma_start(w2[:], t["L0_ffn_W2"].rearrange("(f p) d -> p f d", p=P)).then_inc(in_w, 16)
            sp.wait_ge(made, 1)
            sp.dma_start(t["xg_scr"].rearrange("(t p) d -> p t d", p=P), zero[:]).then_inc(in_z, 16)
            sp.wait_ge(scattered, 16 * NT)
            sp.dma_start(xg[:], t["xg_scr"].rearrange("(t p) d -> p t d", p=P)).then_inc(in_xg, 16)
            sp.wait_ge(y_done, SEL_T)
            sp.dma_start(t["y_scr"].rearrange("(t p) d -> p t d", p=P), y[:]).then_inc(stored, 16)
            sp.wait_ge(stored, 16)

        @block.gpsimd
        def _(pool):
            nc.gpsimd.memset(zero[:], 0.0).then_inc(made, 1)
            pool.wait_ge(in_z, 16)
            pool.wait_ge(idx_ready, 1)
            for j in range(NT):
                nc.gpsimd.indirect_dma_start(
                    out=t["xg_scr"], out_offset=bass.IndirectOffsetOnAxis(ap=s_idx[:, j:j + 1], axis=0),
                    in_=xn[:, j, :], in_offset=None, bounds_check=NSEL - 1, oob_is_err=False
                ).then_inc(scattered, 16)
            pool.wait_ge(stored, 16)
            for j in range(NT):
                nc.gpsimd.indirect_dma_start(
                    out=back[:, j, :], out_offset=None, in_=t["y_scr"],
                    in_offset=bass.IndirectOffsetOnAxis(ap=g_idx[:, j:j + 1], axis=0),
                    bounds_check=NSEL - 1, oob_is_err=False).then_inc(gathered, 16)
            pool.wait_ge(gathered, 16 * NT)

        @block.vector
        def _(dve):
            count = [0]

            def link(ins):
                count[0] += 1
                ins.then_inc(chain, 1)
                dve.wait_ge(chain, count[0])

            link(nc.vector.memset(onesf[:], 1.0))
            link(nc.vector.memset(onesb[:], 1.0))
            dve.wait_ge(in_c, 80)
            for c in range(DK):
                link(nc.vector.tensor_scalar(wrb[:, c, :], onesf[:], wr[:, c:c + 1], None, ALU.mult))
            dve.sem_inc(wrb_made, 1)
            for k in range(NB):
                dve.wait_ge(r_full, k + 1)
                nc.vector.tensor_scalar(rows[:, k * 512:(k + 1) * 512], ps[k][:], br[:, 0:1], None,
                                        ALU.add).then_inc(r_done, 1)
            dve.wait_ge(r_done, NB)
            link(nc.vector.tensor_tensor(diag[:], rows[:].rearrange("p (t q) -> p t q", t=NT),
                                         ident[:].unsqueeze(1).broadcast_to([P, NT, P]), ALU.mult))
            link(nc.vector.tensor_reduce(wcol[:], diag[:], AX.X, ALU.add))
            for j in range(NT):
                b = j // ST
                link(nc.vector.tensor_scalar(ge[:], rows[:, b * S:(b + 1) * S], wcol[:, j:j + 1], None,
                                             ALU.is_ge))
                link(nc.vector.tensor_reduce(cnt[:, j:j + 1], ge[:], AX.X, ALU.add))
            link(nc.vector.tensor_scalar(sel[:], cnt[:], CAP - 0.5, None, ALU.is_lt))
            nc.vector.tensor_copy(selb[:], sel[:]).then_inc(sel_ready, 1)
            dve.wait_ge(cum_full, 1)
            link(nc.vector.tensor_tensor(slot[:], ps[4][:, 0:NT], base[:], ALU.add))
            link(nc.vector.tensor_tensor(slot[:], slot[:], sel[:], ALU.mult))
            link(nc.vector.tensor_copy(g_idx[:], slot[:]))
            link(nc.vector.tensor_scalar(left[:], sel[:], -1.0, 1.0, ALU.mult, ALU.add))
            link(nc.vector.scalar_tensor_tensor(out=slot[:], in0=left[:], scalar=OUT_OF_RANGE, in1=slot[:],
                                                op0=ALU.mult, op1=ALU.add))
            nc.vector.tensor_copy(s_idx[:], slot[:]).then_inc(idx_ready, 1)
            link(nc.vector.tensor_tensor(gate[:], wcol[:], sel[:], ALU.mult))
            for k in range(2):
                dve.wait_ge(t_full, k + 1)
                nc.vector.tensor_copy(xgT[:, :, 256 * k:256 * (k + 1)],
                                      ps[k][:].rearrange("p (c s) -> p c s", c=DK)).then_inc(t_done, 1)
            for k in range(SEL_T):
                dve.wait_ge(y_full, k + 1)
                nc.vector.tensor_tensor(y[:, k, :], ps[k][:, 0:D], b2[:], ALU.add).then_inc(y_done, 1)
            for j in range(NT):
                link(nc.vector.scalar_tensor_tensor(out=x[:, j, :], in0=xn[:, j, :], scalar=left[:, j:j + 1],
                                                    in1=x[:, j, :], op0=ALU.mult, op1=ALU.add))
            dve.wait_ge(gathered, 16 * NT)
            for j in range(NT):
                link(nc.vector.scalar_tensor_tensor(out=x[:, j, :], in0=back[:, j, :], scalar=gate[:, j:j + 1],
                                                    in1=x[:, j, :], op0=ALU.mult, op1=ALU.add))

        @block.tensor
        def _(pe):
            pe.wait_ge(wrb_made, 1)
            for k in range(NB):
                for c in range(DK):
                    mm = pe.matmul(ps[k][:], wrb[:, c, :], xT[:, c, k * 512:(k + 1) * 512],
                                   start=(c == 0), stop=(c == DK - 1))
                mm.then_inc(r_full, 1)
            pe.wait_ge(in_c, 80)
            pe.wait_ge(sel_ready, 1)
            pe.matmul(ps[4][:, 0:NT:2], upper[:], selb[:, 0:NT:2], start=True, stop=True)
            pe.matmul(ps[4][:, 1:NT:2], upper[:], selb[:, 1:NT:2], start=True, stop=False)
            pe.matmul(ps[4][:, 1:NT:2], onesb[:], selb[:, 0:NT:2], start=False,
                      stop=True).then_inc(cum_full, 1)
            pe.wait_ge(in_xg, 16)
            for k in range(2):
                for c in range(DK):
                    for u in range(2):
                        mm = pe.transpose(ps[k][:, c * 256 + u * P:c * 256 + (u + 1) * P],
                                          xg[:, 2 * k + u, c * P:(c + 1) * P], ident[:])
                mm.then_inc(t_full, 1)
            pe.wait_ge(in_w, 64)
            pe.wait_ge(t_done, 2)
            for f in range(FT):
                if f >= 4:
                    pe.wait_ge(h_done, f - 3)
                for c in range(DK):
                    mm = pe.matmul(ps[4 + f % 4][:], w1[:, c, f * P:(f + 1) * P], xgT[:, c, :],
                                   start=(c == 0), stop=(c == DK - 1))
                mm.then_inc(h_full, 1)
            for k in range(SEL_T):
                pe.wait_ge(h_done, FT)
                for f in range(FT):
                    mm = pe.matmul(ps[k][:, 0:D], hT[:, f, k * P:(k + 1) * P], w2[:, f, :],
                                   start=(f == 0), stop=(f == FT - 1))
                mm.then_inc(y_full, 1)

        @block.scalar
        def _(act):
            act.wait_ge(in_w, 64)
            for f in range(FT):
                act.wait_ge(h_full, f + 1)
                nc.scalar.activation(hT[:, f, :], ps[4 + f % 4][:], ACT.Gelu_apprx_tanh,
                                     bias=b1[:, f:f + 1]).then_inc(h_done, 1)


H1, HD = 16, 16
SCALE1 = 1.0 / float(np.sqrt(HD))
NH = P // HD
HH = H1 // NH
VROW = P + HD
MASKED = -3.0e38


def phase_qkv1(nc, ctx, t, xT, qT, kT, v):
    def sb(name, shape, dt=F32):
        return ctx.enter_context(nc.sbuf_tensor("f_" + name, shape, dt))

    def sem(name):
        return new_semaphore(nc, "f_" + name)

    ident = sb("ident", [P, P])
    wq = sb("wq", [P, DK, D])
    wkv = sb("wkv", [P, 2 * DK, DC])
    c = sb("c", [P, NT, DC])
    wqT = sb("wqT", [P, DK, D])
    wkvT = sb("wkvT", [DC, 2 * D])
    cT = sb("cT", [DC, NT * P])
    psA = [ctx.enter_context(nc.psum_tensor(f"f_psA{i}", [P, 512], F32)) for i in range(4)]
    psD = [ctx.enter_context(nc.psum_tensor(f"f_psD{i}", [P, 512], F32)) for i in range(4)]
    in_c = sem("in_c")
    a_full, a_done, d_full, d_done = sem("a_full"), sem("a_done"), sem("d_full"), sem("d_done")
    NQ = B * S // 512

    with nc.Block() as block:
        @block.sync
        def _(sp):
            sp.dma_start(ident[:], t["ident"]).then_inc(in_c, 16)
            sp.dma_start(wq[:], t["L1_xattn_Wq"].rearrange("(c e) d -> e c d", e=P)).then_inc(in_c, 16)
            sp.dma_start(wkv[:], t["L1_xattn_Wkv_expand"].rearrange("(c e) d -> e c d", e=P)).then_inc(in_c, 16)
            for b in range(B):
                sp.dma_start(c[:, b * ST:(b + 1) * ST, :],
                             t["ctx_512"][b, 0:S, :].rearrange("(s p) d -> p s d", p=P)).then_inc(in_c, 16)

        @block.tensor
        def _(pe):
            pe.wait_ge(in_c, 16 * (3 + B))
            for dk in range(DK):
                for ec in range(DK):
                    mm = pe.transpose(psA[0][:, dk * D + ec * P:dk * D + (ec + 1) * P],
                                      wq[:, ec, dk * P:(dk + 1) * P], ident[:])
            mm.then_inc(a_full, 1)
            for ec in range(2 * DK):
                mm = pe.transpose(psA[1][0:DC, ec * P:(ec + 1) * P], wkv[:, ec, :], ident[:])
            mm.then_inc(a_full, 1)
            for g in range(NQ):
                n = 2 + g
                if n >= 4:
                    pe.wait_ge(a_done, n - 3)
                for i in range(4):
                    mm = pe.transpose(psA[n % 4][0:DC, i * P:(i + 1) * P], c[:, 4 * g + i, :], ident[:])
                mm.then_inc(a_full, 1)
            pe.wait_ge(a_done, 1)
            for e in range(DK):
                for g in range(NQ):
                    n = e * NQ + g
                    if n >= 4:
                        pe.wait_ge(d_done, n - 3)
                    for dk in range(DK):
                        mm = pe.matmul(psD[n % 4][:], wqT[:, dk, e * P:(e + 1) * P],
                                       xT[:, dk, g * 512:(g + 1) * 512], start=(dk == 0), stop=(dk == DK - 1))
                    mm.then_inc(d_full, 1)
            for e in range(DK):
                for g in range(NQ):
                    n = 2 + NQ + e * NQ + g
                    pe.wait_ge(a_done, max(n - 3, 2 + NQ))
                    pe.matmul(psA[n % 4][:], wkvT[:, e * P:(e + 1) * P], cT[:, g * 512:(g + 1) * 512],
                              start=True, stop=True).then_inc(a_full, 1)
            for g in range(NT // 2):
                n = 2 * NQ + g
                pe.wait_ge(d_done, n - 3)
                for u in range(2):
                    i = 2 * g + u
                    mm = pe.matmul(psD[n % 4][:, u * D:(u + 1) * D], cT[:, i * P:(i + 1) * P],
                                   wkvT[:, D:2 * D], start=True, stop=True)
                mm.then_inc(d_full, 1)

        @block.scalar
        def _(act):
            act.wait_ge(a_full, 1)
            nc.scalar.activation(wqT[:].rearrange("p c e -> p (c e)"), psA[0][:], ACT.Copy).then_inc(a_done, 1)
            act.wait_ge(a_full, 2)
            nc.scalar.activation(wkvT[:], psA[1][0:DC, :], ACT.Copy).then_inc(a_done, 1)
            for g in range(NQ):
                act.wait_ge(a_full, 3 + g)
                nc.scalar.activation(cT[:, g * 512:(g + 1) * 512], psA[(2 + g) % 4][0:DC, :],
                                     ACT.Copy).then_inc(a_done, 1)
            for e in range(DK):
                for g in range(NQ):
                    n = 2 + NQ + e * NQ + g
                    act.wait_ge(a_full, n + 1)
                    nc.scalar.activation(kT[:, e, g * 512:(g + 1) * 512], psA[n % 4][:],
                                         ACT.Copy).then_inc(a_done, 1)

        @block.vector
        def _(dve):
            for e in range(DK):
                for g in range(NQ):
                    n = e * NQ + g
                    dve.wait_ge(d_full, n + 1)
                    nc.vector.tensor_copy(qT[:, e, g * 512:(g + 1) * 512], psD[n % 4][:]).then_inc(d_done, 1)
            for g in range(NT // 2):
                n = 2 * NQ + g
                dve.wait_ge(d_full, n + 1)
                nc.vector.tensor_copy(v[:, 2 * g:2 * g + 2, :].rearrange("p g e -> p (g e)"),
                                      psD[n % 4][:]).then_inc(d_done, 1)


def phase_attention1(nc, ctx, t, x, qT, kT, v):
    def sb(name, shape, dt=F32):
        return ctx.enter_context(nc.sbuf_tensor("g_" + name, shape, dt))

    def sem(name):
        return new_semaphore(nc, "g_" + name)

    ident = sb("ident", [P, P])
    identb = sb("identb", [P, P], BF16)
    causal = sb("causal", [P, P], BF16)
    hmask = sb("hmask", [P, NH])
    wo = sb("wo", [P, DK, D])
    woT = sb("woT", [P, DK, D])
    q = [sb(f"q{i}", [P, HH, S]) for i in range(2)]
    km = [sb(f"km{i}", [P, HH, NH, S]) for i in range(2)]
    vm = [sb(f"vm{i}", [P, ST * HH, NH * VROW]) for i in range(2)]
    prob = [sb(f"prob{i}", [P, 1024]) for i in range(2)]
    pT = [sb(f"pT{i}", [P, 1024]) for i in range(2)]
    mx = [sb(f"mx{i}", [P, NH]) for i in range(2)]
    bias = [sb(f"bias{i}", [P, NH]) for i in range(2)]
    sums = sb("sums", [P, HH, ST * NH])
    rec = sb("rec", [P, ST * NH])
    recx = sb("recx", [P, ST, NH, HD])
    rT = sb("rT", [P, S])
    oT = [sb(f"oT{i}", [P, S]) for i in range(HH)]
    psS = [ctx.enter_context(nc.psum_tensor(f"g_psS{i}", [P, 1024], F32)) for i in range(2)]
    psT = ctx.enter_context(nc.psum_tensor("g_psT", [P, 1024], F32))
    psO = ctx.enter_context(nc.psum_tensor("g_psO", [P, 512], F32))
    psX = ctx.enter_context(nc.psum_tensor("g_psX", [P, 512], F32))

    in_c, wo_full, wo_done = sem("in_c"), sem("wo_full"), sem("wo_done")
    zeroed, q_ready, km_ready, vm_ready = sem("zeroed"), sem("q_ready"), sem("km_ready"), sem("vm_ready")
    s_full = sem("s_full")
    mx_done, bias_ready = sem("mx_done"), sem("bias_ready")
    exp_done = sem("exp_done")
    t_full = sem("t_full")
    pt_done = sem("pt_done")
    pv_done = sem("pv_done")
    r_chain, r_ready, r_full = sem("r_chain"), sem("r_ready"), sem("r_full")
    r_copied = sem("r_copied")
    o_done = sem("o_done")
    p_full = sem("p_full")
    p_done = sem("p_done")
    UNITS = 3 * HH

    def heads(k):
        kind = k % 3
        return ((0, NH), P, 0) if kind == 0 else ((4 * (kind - 1), 4 * kind), S, 1)

    def nxt(b):
        return (b + 1) % B

    with nc.Block() as block:
        @block.sync
        def _(sp):
            sp.dma_start(ident[:], t["ident"]).then_inc(in_c, 16)
            sp.dma_start(identb[:], t["identb"]).then_inc(in_c, 16)
            sp.dma_start(causal[:], t["causal"]).then_inc(in_c, 16)
            sp.dma_start(hmask[:], t["hmask"]).then_inc(in_c, 16)
            sp.dma_start(wo[:], t["L1_xattn_Wout"].rearrange("(c e) d -> e c d", e=P)).then_inc(in_c, 16)

        @block.gpsimd
        def _(pool):
            def keys(b, u):
                for hh in range(HH):
                    ins = nc.gpsimd.tensor_tensor(
                        km[u][:, hh], kT[:, hh:hh + 1, bass.ds(b * S, S)].broadcast_to([P, NH, S]),
                        hmask[:].unsqueeze(2).broadcast_to([P, NH, S]), ALU.mult)
                ins.then_inc(km_ready, 1)

            def values(b, u):
                nc.gpsimd.tensor_copy(
                    vm[u][:].rearrange("p a (h w) -> p a h w", w=VROW)[:, :, :, 0:HD],
                    v[:, bass.ds(b * ST, ST), :].rearrange("p s (a h w) -> p (s a) h w", a=HH, h=NH)
                ).then_inc(vm_ready, 1)

            for u in range(2):
                nc.gpsimd.memset(vm[u][:], 0.0).then_inc(zeroed, 1)
            pool.wait_ge(zeroed, 2)
            pool.wait_ge(in_c, 80)
            keys(0, 0)
            values(0, 0)
            with pool.Fori(0, B // 2) as j:
                for u in range(2):
                    b = 2 * j + u
                    pool.wait_ge(s_full, UNITS * b + 1)
                    keys(nxt(b), 1 - u)
                    pool.wait_ge(pv_done, UNITS * b + 2)
                    values(nxt(b), 1 - u)

        @block.tensor
        def _(pe):
            def scores(b_count, k, u):
                (h0, h1), w, st = heads(k)
                hh = k // 3
                slot = psS[k % 2]
                if k == 0:
                    pe.wait_ge(q_ready, b_count + 1)
                    pe.wait_ge(km_ready, b_count + 1)
                per = 512 // w
                for half in range(2):
                    ha = h0 + half * per
                    bank = slot[:, half * 512:(half + 1) * 512]
                    pe.matmul(bank, q[u][:, hh, st * P:(st + 1) * P],
                              km[u][:, hh, ha:ha + per, 0:w], start=True, stop=True)
                    diag = bank.rearrange("p (h k) -> p h k", h=per)[:, :, w - P:w]
                    mm = pe.matmul(diag, identb[:], causal[:].unsqueeze(1).broadcast_to([P, per, P]),
                                   start=False, stop=True, skip_group_check=True)
                mm.then_inc(s_full, 1)

            def transposes(b, k):
                n = UNITS * b + k
                pe.wait_ge(exp_done, n + 2)
                pe.wait_ge(pt_done, n + 1)
                for i in range(8):
                    mm = pe.transpose(psT[:, i * P:(i + 1) * P], prob[k % 2][:, i * P:(i + 1) * P], ident[:])
                mm.then_inc(t_full, 1)

            def values(b, k, u):
                (h0, h1), w, st = heads(k)
                hh = k // 3
                n = UNITS * b + k
                pe.wait_ge(pt_done, n + 2)
                if k % 3 == 0:
                    pe.wait_ge(o_done, HH * b + hh + 1)
                    if hh == 0:
                        pe.wait_ge(vm_ready, b + 1)
                i = 0
                for h in range(h0, h1):
                    for kt in range(w // P):
                        mm = pe.matmul(psO[:, st * P:(st + 1) * P],
                                       vm[u][:, kt * HH + hh, h * P:(h + 1) * P],
                                       pT[k % 2][:, i * P:(i + 1) * P],
                                       start=(k % 3 == 0 and i == 0),
                                       stop=(k % 3 != 1 and i == 7), skip_group_check=True)
                        i += 1
                mm.then_inc(pv_done, 1)

            def reciprocals(b, hh):
                n = HH * b + hh
                pe.wait_ge(r_ready, n + 1)
                pe.wait_ge(r_copied, n + 1)
                pe.wait_ge(p_done, ST * b + 1)
                for st in range(ST):
                    mm = pe.transpose(psX[:, st * P:(st + 1) * P],
                                      recx[:, st].rearrange("p h w -> p (h w)"), ident[:])
                mm.then_inc(r_full, 1)

            def project(b):
                pe.wait_ge(o_done, HH * b + HH + 1)
                for st in range(ST):
                    pe.wait_ge(p_done, ST * b + st + 1)
                    for hh in range(HH):
                        mm = pe.matmul(psX[:, D:2 * D], oT[hh][:, st * P:(st + 1) * P], woT[:, hh, :],
                                       start=(hh == 0), stop=(hh == HH - 1))
                    mm.then_inc(p_full, 1)

            pe.wait_ge(in_c, 80)
            for dk in range(DK):
                for ec in range(DK):
                    mm = pe.transpose(psX[:, dk * D + ec * P:dk * D + (ec + 1) * P],
                                      wo[:, ec, dk * P:(dk + 1) * P], ident[:])
            mm.then_inc(wo_full, 1)
            pe.sem_inc(t_full, 1)
            pe.sem_inc(pv_done, 2)
            pe.wait_ge(wo_done, 1)
            scores(0, 0, 0)
            with pe.Fori(0, B // 2) as j:
                for u in range(2):
                    b = 2 * j + u
                    for k in range(UNITS):
                        pe.wait_ge(exp_done, UNITS * b + k + 1)
                        if k < UNITS - 1:
                            scores(b, k + 1, u)
                        else:
                            scores(b + 1, 0, 1 - u)
                        transposes(b, k)
                        if k >= 1:
                            values(b, k - 1, u)
                        if k == 3:
                            reciprocals(b, 0)
                    values(b, UNITS - 1, u)
                    reciprocals(b, 1)
                    project(b)

        @block.scalar
        def _(act):
            def exps(b, k):
                (h0, h1), w, st = heads(k)
                hh = k // 3
                n = UNITS * b + k
                act.wait_ge(bias_ready, n + 1)
                if not isinstance(n, int):
                    act.wait_ge(t_full, n)
                for h in range(h0, h1):
                    i = h - h0
                    ins = nc.scalar.activation(prob[k % 2][:, i * w:(i + 1) * w], psS[k % 2][:, i * w:(i + 1) * w],
                                               ACT.Exp, bias=bias[k % 2][:, i:i + 1], scale=SCALE1,
                                               accum_out=sums[:, hh, st * NH + h:st * NH + h + 1])
                ins.then_inc(exp_done, 1)

            def copy_r(b, hh):
                n = HH * b + hh
                act.wait_ge(r_full, n + 1)
                act.wait_ge(o_done, n + 1)
                nc.scalar.activation(rT[:], psX[:, 0:S], ACT.Copy).then_inc(r_copied, 1)

            act.sem_inc(exp_done, 1)
            act.sem_inc(r_copied, 1)
            exps(0, 0)
            with act.Fori(0, B // 2) as j:
                for u in range(2):
                    b = 2 * j + u
                    for k in range(UNITS):
                        if k < UNITS - 1:
                            exps(b, k + 1)
                        else:
                            exps(b + 1, 0)
                        if k == 3:
                            copy_r(b, 0)
                    copy_r(b, 1)

        @block.vector
        def _(dve):
            def maxima(b, k):
                (h0, h1), w, st = heads(k)
                n = UNITS * b + k
                dve.wait_ge(s_full, n + 1)
                nh = h1 - h0
                nc.vector.tensor_reduce(mx[k % 2][:, 0:nh], psS[k % 2][:].rearrange("p (h k) -> p h k", h=nh),
                                        AX.X, ALU.max).then_inc(mx_done, 1)
                dve.wait_ge(mx_done, n + 1)
                nc.vector.tensor_scalar(bias[k % 2][:, 0:nh], mx[k % 2][:, 0:nh], -SCALE1, None,
                                        ALU.mult).then_inc(bias_ready, 1)

            def drain_t(b, k):
                n = UNITS * b + k
                dve.wait_ge(t_full, n + 2)
                dve.wait_ge(pv_done, n + 1)
                nc.vector.tensor_copy(pT[k % 2][:], psT[:]).then_inc(pt_done, 1)

            def reciprocals(b, hh):
                n = HH * b + hh
                dve.wait_ge(exp_done, UNITS * b + 3 * hh + 4)
                nc.vector.reciprocal(rec[:], sums[:, hh, :]).then_inc(r_chain, 1)
                dve.wait_ge(r_chain, n + 1)
                nc.vector.tensor_copy(recx[:].rearrange("p s h w -> p (s h) w"),
                                      rec[:].unsqueeze(2).broadcast_to([P, ST * NH, HD])).then_inc(r_ready, 1)

            def normalise(b, hh):
                n = HH * b + hh
                dve.wait_ge(r_copied, n + 2)
                dve.wait_ge(pv_done, UNITS * b + 3 * hh + 5)
                nc.vector.tensor_tensor(oT[hh][:], psO[:, 0:S], rT[:], ALU.mult).then_inc(o_done, 1)

            def add(b):
                for st in range(ST):
                    dve.wait_ge(p_full, ST * b + st + 1)
                    xt = x[:, bass.ds(b * ST + st, 1), :].rearrange("p o d -> p (o d)")
                    nc.vector.tensor_tensor(xt, xt, psX[:, D:2 * D], ALU.add).then_inc(p_done, 1)

            def queries(b, u):
                nc.vector.tensor_copy(q[u][:], qT[:, :, bass.ds(b * S, S)]).then_inc(q_ready, 1)

            dve.wait_ge(wo_full, 1)
            nc.vector.tensor_copy(woT[:].rearrange("p c e -> p (c e)"), psX[:]).then_inc(wo_done, 1)
            dve.sem_inc(pt_done, 1)
            dve.sem_inc(o_done, 1)
            dve.sem_inc(p_done, 1)
            queries(0, 0)
            maxima(0, 0)
            with dve.Fori(0, B // 2) as j:
                for u in range(2):
                    b = 2 * j + u
                    dve.wait_ge(s_full, UNITS * b + 1)
                    queries(nxt(b), 1 - u)
                    for k in range(UNITS):
                        if k < UNITS - 1:
                            maxima(b, k + 1)
                        else:
                            maxima(b + 1, 0)
                        drain_t(b, k)
                        if k == 2:
                            reciprocals(b, 0)
                        if k == 3:
                            normalise(b, 0)
                    reciprocals(b, 1)
                    normalise(b, 1)
                    add(b)


E1, HID = 8, 352
CAP1 = B * S // E1
FT1 = [(0, 128), (128, 128), (256, 96)]


def phase_moe(nc, ctx, t, x, xn, xT):
    def sb(name, shape, dt=F32):
        return ctx.enter_context(nc.sbuf_tensor("m_" + name, shape, dt))

    def sem(name):
        return new_semaphore(nc, "m_" + name)

    FTN = len(FT1)
    ident = sb("ident", [P, P])
    upper = sb("upper", [P, P], BF16)
    onesb = sb("ones", [P, P], BF16)
    wg = sb("wg", [P, DK, E1])
    rank = sb("rank", [P, E1])
    ebase = sb("ebase", [P, E1])
    sw1 = sb("sw1", [P, DK, HID])
    sw3 = sb("sw3", [P, DK, HID])
    sw2 = sb("sw2", [P, FTN, D])
    w1 = [sb(f"w1_{i}", [P, DK, HID]) for i in range(2)]
    w3 = [sb(f"w3_{i}", [P, DK, HID]) for i in range(2)]
    w2 = [sb(f"w2_{i}", [P, FTN, D]) for i in range(2)]
    xt = [sb(f"xt{i}", [P, DK, CAP1]) for i in range(2)]
    xd = [sb(f"xd{i}", [P, 2, D]) for i in range(2)]
    act_s = [sb(f"s{i}", [P, FTN, CAP1]) for i in range(2)]
    g = [sb(f"g{i}", [P, FTN, CAP1]) for i in range(2)]
    yo = [sb(f"yo{i}", [P, 2, D]) for i in range(2)]
    zero = sb("zero", [P, NT * D // 4])
    logit = sb("logit", [P, NT, E1])
    top = sb("top", [P, NT])
    ex = sb("ex", [P, NT, E1])
    tot = sb("tot", [P, NT])
    val = sb("val", [P, NT, E1])
    oh = sb("oh", [P, NT, E1])
    ohb = sb("ohb", [P, NT, E1], BF16)
    cum = sb("cum", [P, NT, E1])
    pos = sb("pos", [P, NT])
    ebs = sb("ebs", [P, NT])
    keepm = sb("keepm", [P, NT])
    gate = sb("gate", [P, NT])
    slot = sb("slot", [P, NT])
    s_idx = sb("s_idx", [P, NT], U32)
    g_idx = sb("g_idx", [P, NT], U32)
    back = sb("back", [P, NT, D])
    psR = ctx.enter_context(nc.psum_tensor("m_psR", [P, 512], F32))
    psH = [ctx.enter_context(nc.psum_tensor(f"m_psH{i}", [P, 512], F32)) for i in range(4)]
    psY = [ctx.enter_context(nc.psum_tensor(f"m_psY{i}", [P, 512], F32)) for i in range(2)]

    in_c, in_s, in_z = sem("in_c"), sem("in_s"), sem("in_z")
    in_w = [sem(f"in_w{i}") for i in range(2)]
    in_xd = [sem(f"in_xd{i}") for i in range(2)]
    zeroed, chain, const = sem("zeroed"), sem("chain"), sem("const")
    l_full, l_done, ex_ready = sem("l_full"), sem("l_done"), sem("ex_ready")
    oh_ready, cum_full, idx_ready = sem("oh_ready"), sem("cum_full"), sem("idx_ready")
    scattered, gathered = sem("scattered"), sem("gathered")
    xt_full, xt_done = sem("xt_full"), sem("xt_done")
    h_full, silu_done, g_done = sem("h_full"), sem("silu_done"), sem("g_done")
    y_full, y_done = sem("y_full"), sem("y_done")
    stored = [sem(f"stored{i}") for i in range(2)]
    out_sent = sem("out_sent")
    x_final = sem("x_final")
    NS = B * S // CAP1

    def load_ffn(sp, s, d1, d3, d2, a1, a3, a2):
        sp.dma_start(d1[:], a1.rearrange("(c d) f -> d c f", d=P)).then_inc(s, 16)
        sp.dma_start(d3[:], a3.rearrange("(c d) f -> d c f", d=P)).then_inc(s, 16)
        sp.dma_start(d2[:, 0:2, :], a2[0:256, :].rearrange("(c f) d -> f c d", f=P)).then_inc(s, 16)
        sp.dma_start(d2[0:96, 2, :], a2[256:352, :]).then_inc(s, 16)

    with nc.Block() as block:
        @block.sync
        def _(sp):
            sp.dma_start(ident[:], t["ident"]).then_inc(in_c, 16)
            sp.dma_start(upper[:], t["upper"]).then_inc(in_c, 16)
            sp.dma_start(rank[:], t["rank"]).then_inc(in_c, 16)
            sp.dma_start(ebase[:], t["ebase"]).then_inc(in_c, 16)
            sp.dma_start(wg[:], t["L1_ffn_Wg"].rearrange("(c d) e -> d c e", d=P)).then_inc(in_c, 16)
            load_ffn(sp, in_s, sw1, sw3, sw2, t["L1_ffn_sw1"], t["L1_ffn_sw3"], t["L1_ffn_sw2"])
            sp.wait_ge(zeroed, 1)
            for k in range(4):
                sp.dma_start(t["xd_scr"].rearrange("(k p r) d -> k p (r d)", k=4, p=P)[k],
                             zero[:]).then_inc(in_z, 16)

            def weights(e, u):
                ap = [a[bass.ds(e, 1)].rearrange("o a b -> (o a) b")
                      for a in (t["L1_ffn_W1"], t["L1_ffn_W3"], t["L1_ffn_W2"])]
                load_ffn(sp, in_w[u], w1[u], w3[u], w2[u], *ap)

            for u in range(2):
                sp.sem_inc(stored[u], 16)
            weights(0, 0)
            weights(1, 1)
            sp.wait_ge(scattered, 16 * NT)
            for u in range(2):
                sp.dma_start(xd[u][:], t["xd_scr"][u * CAP1:(u + 1) * CAP1, :].rearrange("(c p) d -> p c d", p=P)
                             ).then_inc(in_xd[u], 16)
            with sp.Fori(0, E1 // 2) as j:
                for u in range(2):
                    e = 2 * j + u
                    sp.wait_ge(y_full, 2 * (NS + e) + 2)
                    weights((e + 2) % E1, u)
                    sp.dma_start(xd[u][:], t["xd_scr"][bass.ds(((e + 2) % E1) * CAP1, CAP1), :]
                                 .rearrange("(c p) d -> p c d", p=P)).then_inc(in_xd[u], 16)
                    sp.wait_ge(y_done, 2 * (NS + e) + 4)
                    sp.dma_start(t["oe_scr"][bass.ds(e * CAP1, CAP1), :].rearrange("(c p) d -> p c d", p=P),
                                 yo[u][:]).then_inc(stored[u], 16)
            for u in range(2):
                sp.wait_ge(in_w[u], 64 * (E1 // 2 + 1))
                sp.wait_ge(in_xd[u], 16 * (E1 // 2 + 1))
                sp.wait_ge(stored[u], 16 + 16 * (E1 // 2))
            for j in range(NT // 4):
                sp.wait_ge(x_final, 4 * j + 4)
                sp.dma_start(t["out"].rearrange("b (s p) d -> p (b s) d", p=P)[:, 4 * j:4 * j + 4, :],
                             x[:, 4 * j:4 * j + 4, :]).then_inc(out_sent, 16)
            sp.wait_ge(out_sent, 16 * (NT // 4))

        @block.gpsimd
        def _(pool):
            nc.gpsimd.memset(zero[:], 0.0).then_inc(zeroed, 1)
            pool.wait_ge(in_z, 64)
            pool.wait_ge(idx_ready, 1)
            for j in range(NT):
                nc.gpsimd.indirect_dma_start(
                    out=t["xd_scr"], out_offset=bass.IndirectOffsetOnAxis(ap=s_idx[:, j:j + 1], axis=0),
                    in_=xn[:, j, :], in_offset=None, bounds_check=E1 * CAP1 - 1, oob_is_err=False
                ).then_inc(scattered, 16)
            for u in range(2):
                pool.wait_ge(stored[u], 16 + 16 * (E1 // 2))
            for j in range(NT):
                nc.gpsimd.indirect_dma_start(
                    out=back[:, j, :], out_offset=None, in_=t["oe_scr"],
                    in_offset=bass.IndirectOffsetOnAxis(ap=g_idx[:, j:j + 1], axis=0),
                    bounds_check=E1 * CAP1 - 1, oob_is_err=False).then_inc(gathered, 16)
            pool.wait_ge(gathered, 16 * NT)

        @block.tensor
        def _(pe):
            def hidden(n, a1, a3, moving):
                for f, (f0, fw) in enumerate(FT1):
                    slot = psH[f]
                    pe.wait_ge(g_done, FTN * n + f + 1)
                    for k, a in enumerate((a1, a3)):
                        for c in range(DK):
                            mm = pe.matmul(slot[0:fw, k * CAP1:(k + 1) * CAP1], a[:, c, f0:f0 + fw],
                                           moving(c), start=(c == 0), stop=(c == DK - 1))
                    mm.then_inc(h_full, 1)

            def down(n, a2, u):
                for r in range(2):
                    if r == 0:
                        pe.wait_ge(g_done, FTN * n + 6)
                    pe.wait_ge(y_done, 2 * n + r + 1)
                    for f, (_, fw) in enumerate(FT1):
                        mm = pe.matmul(psY[r][:, 0:D], g[u][0:fw, f, r * P:(r + 1) * P], a2[0:fw, f, :],
                                       start=(f == 0), stop=(f == FTN - 1))
                    mm.then_inc(y_full, 1)

            pe.wait_ge(in_c, 80)
            for j in range(NT):
                for c in range(DK):
                    mm = pe.matmul(psR[:, j * E1:(j + 1) * E1], xT[:, c, j * P:(j + 1) * P], wg[:, c, :],
                                   start=(c == 0), stop=(c == DK - 1))
            mm.then_inc(l_full, 1)
            pe.wait_ge(in_s, 64)
            for n in range(2):
                hidden(n, sw1, sw3, lambda c: xT[:, c, n * CAP1:(n + 1) * CAP1])
                down(n, sw2, n)
            pe.wait_ge(oh_ready, 1)
            pe.wait_ge(const, 1)
            w = NT * E1
            pe.matmul(psR[:, 0:w], upper[:], ohb[:].rearrange("p t e -> p (t e)"), start=True, stop=True)
            for j in range(NT - 1):
                left = NT - 1 - j
                mm = pe.matmul(psR[:, (j + 1) * E1:w], onesb[:],
                               ohb[:, j:j + 1, :].broadcast_to([P, left, E1]),
                               start=False, stop=True, skip_group_check=True)
            mm.then_inc(cum_full, 1)
            with pe.Fori(1, NS // 2) as j:
                for u in range(2):
                    n = 2 * j + u
                    hidden(n, sw1, sw3, lambda c: xT[:, c, bass.ds(n * CAP1, CAP1)])
                    down(n, sw2, u)
            with pe.Fori(0, E1 // 2) as j:
                for u in range(2):
                    e = 2 * j + u
                    pe.wait_ge(in_xd[u], 16 * j + 16)
                    pe.wait_ge(xt_done, e + 1)
                    for c in range(DK):
                        for r in range(2):
                            mm = pe.transpose(psH[3][:, c * 256 + r * P:c * 256 + (r + 1) * P],
                                              xd[u][:, r, c * P:(c + 1) * P], ident[:])
                    mm.then_inc(xt_full, 1)
                    pe.wait_ge(in_w[u], 64 * j + 64)
                    pe.wait_ge(xt_done, e + 2)
                    hidden(NS + e, w1[u], w3[u], lambda c: xt[u][:, c, :])
                    down(NS + e, w2[u], u)

        @block.scalar
        def _(act):
            def silu(n, u):
                for f, (_, fw) in enumerate(FT1):
                    act.wait_ge(h_full, FTN * n + f + 1)
                    act.wait_ge(g_done, FTN * n + f + 1)
                    nc.scalar.activation(act_s[u][0:fw, f, :], psH[f][0:fw, 0:CAP1], ACT.Silu
                                         ).then_inc(silu_done, 1)

            act.wait_ge(l_done, 2)
            nc.scalar.activation(ex[:], ex[:], ACT.Exp).then_inc(ex_ready, 1)
            with act.Fori(0, NS // 2) as j:
                for u in range(2):
                    silu(2 * j + u, u)
            act.sem_inc(xt_done, 1)
            with act.Fori(0, E1 // 2) as j:
                for u in range(2):
                    e = 2 * j + u
                    act.wait_ge(xt_full, e + 1)
                    nc.scalar.activation(xt[u][:].rearrange("p c s -> p (c s)"), psH[3][:],
                                         ACT.Copy).then_inc(xt_done, 1)
                    silu(NS + e, u)
                    for r in range(2):
                        if r == 0:
                            act.wait_ge(stored[u], 16 * j + 16)
                        act.wait_ge(y_full, 2 * (NS + e) + r + 1)
                        nc.scalar.activation(yo[u][:, r, :], psY[r][:, 0:D], ACT.Copy).then_inc(y_done, 1)

        @block.vector
        def _(dve):
            count = [0]

            def link(ins):
                count[0] += 1
                ins.then_inc(chain, 1)
                dve.wait_ge(chain, count[0])

            def gated(n, u):
                for f, (_, fw) in enumerate(FT1):
                    dve.wait_ge(silu_done, FTN * n + f + 1)
                    nc.vector.tensor_tensor(g[u][0:fw, f, :], act_s[u][0:fw, f, :],
                                            psH[f][0:fw, CAP1:2 * CAP1], ALU.mult).then_inc(g_done, 1)

            def add_shared(n, dyn):
                for r in range(2):
                    dve.wait_ge(y_full, 2 * n + r + 1)
                    row = x[:, bass.ds(2 * n + r, 1), :].rearrange("p o d -> p (o d)")
                    nc.vector.tensor_tensor(row, row, psY[r][:, 0:D], ALU.add).then_inc(y_done, 1)

            nc.vector.memset(onesb[:], 1.0).then_inc(const, 1)
            dve.sem_inc(g_done, FTN)
            dve.sem_inc(y_done, 2)
            dve.wait_ge(in_c, 80)
            dve.wait_ge(l_full, 1)
            nc.vector.tensor_copy(logit[:].rearrange("p t e -> p (t e)"), psR[:, 0:NT * E1]).then_inc(l_done, 1)
            dve.wait_ge(l_done, 1)
            link(nc.vector.tensor_reduce(top[:], logit[:], AX.X, ALU.max))
            nc.vector.tensor_tensor(ex[:], logit[:], top[:].unsqueeze(2).broadcast_to([P, NT, E1]),
                                    ALU.subtract).then_inc(l_done, 1)
            dve.wait_ge(ex_ready, 1)
            link(nc.vector.tensor_reduce(tot[:], ex[:], AX.X, ALU.add))
            link(nc.vector.tensor_reduce(top[:], ex[:], AX.X, ALU.max))
            link(nc.vector.tensor_tensor(val[:], ex[:], top[:].unsqueeze(2).broadcast_to([P, NT, E1]), ALU.is_ge))
            link(nc.vector.tensor_tensor(val[:], val[:], rank[:].unsqueeze(1).broadcast_to([P, NT, E1]), ALU.mult))
            link(nc.vector.tensor_reduce(pos[:], val[:], AX.X, ALU.max))
            link(nc.vector.tensor_tensor(oh[:], val[:], pos[:].unsqueeze(2).broadcast_to([P, NT, E1]),
                                         ALU.is_equal))
            nc.vector.tensor_copy(ohb[:], oh[:]).then_inc(oh_ready, 1)
            link(nc.vector.reciprocal(tot[:], tot[:]))
            link(nc.vector.tensor_tensor(gate[:], tot[:], top[:], ALU.mult))
            link(nc.vector.tensor_tensor(val[:], oh[:], ebase[:].unsqueeze(1).broadcast_to([P, NT, E1]), ALU.mult))
            link(nc.vector.tensor_reduce(ebs[:], val[:], AX.X, ALU.add))
            for n in range(2):
                gated(n, n)
                add_shared(n, False)
            dve.wait_ge(cum_full, 1)
            link(nc.vector.tensor_tensor(cum[:].rearrange("p t e -> p (t e)"), psR[:, 0:NT * E1],
                                         oh[:].rearrange("p t e -> p (t e)"), ALU.mult))
            link(nc.vector.tensor_reduce(pos[:], cum[:], AX.X, ALU.add))
            link(nc.vector.tensor_scalar(keepm[:], pos[:], CAP1 + 0.5, None, ALU.is_lt))
            link(nc.vector.scalar_tensor_tensor(out=slot[:], in0=pos[:], scalar=-1.0, in1=ebs[:],
                                                op0=ALU.add, op1=ALU.add))
            link(nc.vector.tensor_tensor(slot[:], slot[:], keepm[:], ALU.mult))
            link(nc.vector.tensor_copy(g_idx[:], slot[:]))
            link(nc.vector.tensor_tensor(gate[:], gate[:], keepm[:], ALU.mult))
            link(nc.vector.tensor_scalar(keepm[:], keepm[:], -OUT_OF_RANGE, OUT_OF_RANGE, ALU.mult, ALU.add))
            link(nc.vector.tensor_tensor(slot[:], slot[:], keepm[:], ALU.add))
            nc.vector.tensor_copy(s_idx[:], slot[:]).then_inc(idx_ready, 1)
            with dve.Fori(1, NS // 2) as j:
                for u in range(2):
                    gated(2 * j + u, u)
                    add_shared(2 * j + u, True)
            with dve.Fori(0, E1 // 2) as j:
                for u in range(2):
                    gated(NS + 2 * j + u, u)
            dve.wait_ge(y_done, 2 * NS + 2)
            dve.wait_ge(gathered, 16 * NT)
            for j in range(NT):
                nc.vector.scalar_tensor_tensor(out=x[:, j, :], in0=back[:, j, :], scalar=gate[:, j:j + 1],
                                               in1=x[:, j, :], op0=ALU.mult, op1=ALU.add).then_inc(x_final, 1)


SCRATCH = {
    "w2_scr": (H0, P, DK * DCQ),
    "m_scr": (H0, HALF, 4 * DC),
    "wvo_scr": (P, H0 // 2, D),
    "acc_scr": (B * H0, P, ST, 2 * DC + 1),
    "xg_scr": (NSEL, D),
    "y_scr": (NSEL, D),
    "xd_scr": (E1 * CAP1, D),
    "oe_scr": (E1 * CAP1, D),
}


def tables():
    def rope(length, dim):
        e = np.arange(0, dim, 2, dtype=np.float32) / np.float32(dim)
        inv = (np.float32(1.0) / np.power(10000.0, e.astype(np.float64)).astype(np.float32)).astype(np.float32)
        f = (np.arange(length, dtype=np.float32)[:, None] * inv[None, :]).astype(np.float64)
        return (np.repeat(np.sin(f), 2, axis=1).astype(np.float32),
                np.repeat(np.cos(f), 2, axis=1).astype(np.float32))

    sin_q, cos_q = rope(S, DCQ)
    sin_k, cos_k = rope(L, DC)
    sq, cq = sin_q.T, cos_q.T
    tabs = {
        "tabA": np.concatenate([cq[:HALF], cq[HALF:]], axis=1),
        "tabB": np.concatenate([sq[HALF:], -sq[:HALF]], axis=1),
    }
    sgn = np.concatenate([-sin_k[:, :DC // 2], sin_k[:, DC // 2:]], axis=1)
    for name, tab in (("cosk", cos_k), ("sink", sgn)):
        full = np.zeros((LT * P, DC), np.float32)
        full[:L] = tab
        tabs[name] = full.reshape(LT, P, DC).transpose(1, 0, 2)
    tabs["ident"] = np.eye(P, dtype=np.float32)
    tabs["upper"] = np.triu(np.ones((P, P), np.float32)).astype(BF_NP)
    first = np.repeat(np.arange(B, dtype=np.float32) * CAP - 1.0, ST)
    tabs["cap_base"] = np.broadcast_to(first, (P, NT))
    tabs["identb"] = np.eye(P, dtype=np.float32).astype(BF_NP)
    tabs["causal"] = np.where(np.tril(np.ones((P, P), bool)), 0.0, MASKED).astype(np.float32).astype(BF_NP)
    tabs["hmask"] = np.repeat(np.eye(NH, dtype=np.float32), HD, axis=0)
    tabs["rank"] = np.broadcast_to(np.arange(E1, 0, -1, dtype=np.float32), (P, E1))
    tabs["ebase"] = np.broadcast_to(np.arange(E1, dtype=np.float32) * CAP1, (P, E1))
    tabs["ident16"] = np.eye(P, dtype=np.float16)
    return {k: np.ascontiguousarray(v) for k, v in tabs.items()}


def build(nc, t):
    LIVE.clear()
    with ExitStack() as whole:
        def sb(ctx, name, shape, dt=F32):
            return ctx.enter_context(nc.sbuf_tensor(name, shape, dt))

        k_unscale = sb(whole, "k_unscale", [P, 1])
        layer0 = whole.enter_context(ExitStack())
        keep = {
            "qscale": sb(layer0, "qscale", [P, H0]),
            "qk_scale": sb(layer0, "qk_scale", [P, H0]),
            "k_unscale": k_unscale,
            "ln1024": sb(layer0, "ln1024", [P, 1]),
            "ident16": sb(layer0, "ident16_sb", [P, P], F16),
            "xT": sb(layer0, "xT", [P, DK, B * S]),
        }
        with ExitStack() as ctx:
            phase_weights(nc, ctx, t, keep)
        keep["V"] = sb(layer0, "V", [P, B, LT, 2 * DC + 1], F16)
        keep["KK1"] = sb(layer0, "KK1", [P, B * L], F16)
        keep["KK2"] = sb(layer0, "KK2", [P, B * L], F16)
        with ExitStack() as ctx:
            phase_context(nc, ctx, t, keep)
        with ExitStack() as ctx:
            phase_attention0(nc, ctx, t, keep)
        layer0.close()
        x = sb(whole, "x_rows", [P, NT, D])
        xn = sb(whole, "xn_rows", [P, NT, D])
        xT = sb(whole, "xT_rows", [P, DK, B * S])
        with ExitStack() as ctx:
            phase_project0(nc, ctx, t, keep, x)
        with ExitStack() as ctx:
            phase_norm(nc, ctx, t, x, xn, xT, "n1_")
        with ExitStack() as ctx:
            phase_ffn0(nc, ctx, t, x, xn, xT)
        clear_semaphores(nc)
        with ExitStack() as ctx:
            phase_norm(nc, ctx, t, x, xn, xT, "n2_")
        with ExitStack() as layer1:
            qT = sb(layer1, "qT", [P, DK, B * S])
            kT = sb(layer1, "kT", [P, DK, B * S])
            v = sb(layer1, "v", [P, NT, D])
            with ExitStack() as ctx:
                phase_qkv1(nc, ctx, t, xT, qT, kT, v)
            with ExitStack() as ctx:
                phase_attention1(nc, ctx, t, x, qT, kT, v)
        with ExitStack() as ctx:
            phase_norm(nc, ctx, t, x, xn, xT, "n3_")
        with ExitStack() as ctx:
            phase_moe(nc, ctx, t, x, xn, xT)


_INS = ["x", "ctx_512", "L0_xattn_Wq", "L0_xattn_w_kc_q", "L0_xattn_w_kc_kv", "L0_xattn_W_qr", "L0_xattn_W_kr",
        "L0_xattn_Wo", "L0_ffn_W_r", "L0_ffn_b_r", "L0_ffn_W1", "L0_ffn_b1", "L0_ffn_W2", "L0_ffn_b2",
        "L1_xattn_Wq", "L1_xattn_Wkv_expand", "L1_xattn_Wout", "L1_ffn_Wg", "L1_ffn_W1", "L1_ffn_W3",
        "L1_ffn_W2", "L1_ffn_sw1", "L1_ffn_sw3", "L1_ffn_sw2"]


def kernel(**inputs):
    import numpy as _np
    import concourse.bacc as _bacc
    from concourse import mybir as _mybir
    from concourse.bass_utils import run_bass_kernel_spmd as _run

    nc = _bacc.Bacc("TRN2", target_bir_lowering=False, num_devices=1)
    arrays, t = {}, {}
    given = {name: _np.ascontiguousarray(inputs[name]) for name in _INS}
    for name, a in {**given, **tables()}.items():
        arrays[f"in_{name}"] = a
        t[name] = nc.dram_tensor(f"in_{name}", a.shape, _mybir.dt.from_np(a.dtype), kind="ExternalInput").ap()
    for name, shape in SCRATCH.items():
        t[name] = nc.dram_tensor(name, shape, _mybir.dt.float32, kind="Internal").ap()
    t["out"] = nc.dram_tensor("out_dram", (B, S, D), _mybir.dt.float32, kind="ExternalOutput").ap()
    build(nc, t)
    r = _run(nc, [arrays], core_ids=[0])
    return r.results[0]["out_dram"]
```

```python
from contextlib import ExitStack

import numpy as np

import concourse.bass as bass
from concourse import mybir

ALU = mybir.AluOpType
ACT = mybir.ActivationFunctionType
F32 = mybir.dt.float32
F16 = mybir.dt.float16
BF16 = mybir.dt.bfloat16
U32 = mybir.dt.uint32
AX = mybir.AxisListType
P = 128
BF_NP = mybir.dt.np(BF16)

B, S, D = 8, 256, 256
L = 1601
ST = S // P
NT = B * ST
DK = D // P
H0, K0, DC, DCQ, R0 = 16, 128, 64, 192, 64
LT = -(-L // P)
LLAST = L - (LT - 1) * P
HALF = DCQ // 2
EPS = 1e-5

QK_TOP = 2.0 ** 14
SHIFT_ONE = 2.0 ** 15
SHIFT_ROWS = 16
SHIFT_MUL = 1.0 / (SHIFT_ONE * SHIFT_ROWS)
LN_1024 = float(np.log(1024.0))


LIVE = []


def new_semaphore(nc, name):
    LIVE.append(nc.alloc_semaphore(name))
    return LIVE[-1]


def clear_semaphores(nc):
    nc.all_engine_barrier()
    nc.clear_and_free_semaphores(list(LIVE))
    nc.all_engine_barrier()
    LIVE.clear()


def layer_norm_stats(dve, nc, link, x, stats, agg, n):
    for j in range(n):
        link(nc.vector.bn_stats(stats[:, j, :], x[:, j, :]))
        link(nc.vector.bn_aggr(agg[:, j, :], stats[:, j, :]))


def rstd_refined(nc, link, rstd, root, agg, tmp):
    var = agg[:, :, 1]
    link(nc.vector.reciprocal(rstd, root))
    link(nc.vector.tensor_tensor(tmp, rstd, rstd, ALU.mult))
    link(nc.vector.scalar_tensor_tensor(out=tmp, in0=var, scalar=EPS, in1=tmp, op0=ALU.add, op1=ALU.mult))
    link(nc.vector.tensor_scalar(tmp, tmp, -0.5, 1.5, ALU.mult, ALU.add))
    link(nc.vector.tensor_tensor(rstd, rstd, tmp, ALU.mult))


def phase_weights(nc, ctx, t, keep):
    def sb(name, shape, dt=F32):
        return ctx.enter_context(nc.sbuf_tensor(name, shape, dt))

    def sem(name):
        return new_semaphore(nc, name)

    wq = sb("a_wq", [P, H0, D])
    wkcq = sb("a_wkcq", [P, H0, DCQ])
    wqr = sb("a_wqr", [HALF, H0, 2, R0])
    wkr = sb("a_wkr", [DC, H0, R0])
    wkckv = sb("a_wkckv", [P, H0, DC])
    wo = sb("a_wo", [P, DK, H0 * K0])
    x = sb("a_x", [P, NT, D])
    w2 = sb("a_w2", [P, H0, DK * DCQ])
    rT = sb("a_rT", [R0, H0, DCQ + DC])
    m = sb("a_m", [HALF, H0, 2, DC])
    m2 = sb("a_m2", [HALF, H0, 2, 2, DC])
    woT = sb("a_woT", [P, H0, D])
    wvo = sb("a_wvo", [P, H0 // 2, D])
    junk = sb("a_junk", [P, DK * DCQ])
    norms = sb("a_norms", [P, 2 * H0])
    nsum = sb("a_nsum", [P, 2 * H0])
    bound = sb("a_bound", [P, H0])
    stats = sb("a_stats", [P, NT, 6])
    agg = sb("a_agg", [P, NT, 2])
    root = sb("a_root", [P, NT])
    rstd = sb("a_rstd", [P, NT])
    tmp = sb("a_tmp", [P, NT])
    ones = sb("a_ones", [P, P])
    eps = sb("a_eps", [P, 1])
    ident = sb("a_ident", [P, P])
    psA = [ctx.enter_context(nc.psum_tensor(f"a_psA{i}", [P, 512], F32)) for i in range(4)]
    psD = [ctx.enter_context(nc.psum_tensor(f"a_psD{i}", [P, 512], F32)) for i in range(4)]

    in_q, in_r, in_o, in_x = sem("in_q"), sem("in_r"), sem("in_o"), sem("in_x")
    a_full, a_done = sem("a_full"), sem("a_done")
    d_full, d_done = sem("d_full"), sem("d_done")
    chain = sem("a_chain")
    consts = sem("a_consts")
    var_ready, root_ready, xln_ready = sem("var_ready"), sem("root_ready"), sem("xln_ready")
    norms_ready, b2_ready, bound_ready = sem("norms_ready"), sem("b2_ready"), sem("bound_ready")
    m2_ready, sq_done, stored = sem("m2_ready"), sem("sq_done"), sem("a_stored")

    N_A = H0 + H0 // 2 + H0 // 2
    N_M, N_VO, N_XT = H0 // 2, H0 // 4, NT // 2
    A_RT, A_WOT = H0, H0 + H0 // 2

    with nc.Block() as block:
        @block.sync
        def _(sp):
            sp.dma_start(wq[:], t["L0_xattn_Wq"].rearrange("(h k) d -> k h d", h=H0)).then_inc(in_q, 16)
            sp.dma_start(wkcq[:], t["L0_xattn_w_kc_q"].rearrange("h k q -> k h q")).then_inc(in_q, 16)
            sp.dma_start(ident[:], t["ident"]).then_inc(in_r, 16)
            sp.dma_start(wqr[:], t["L0_xattn_W_qr"].rearrange("h (e q) r -> q h e r", e=2)).then_inc(in_r, 16)
            sp.dma_start(wkr[:], t["L0_xattn_W_kr"].rearrange("h d r -> d h r")).then_inc(in_r, 16)
            sp.dma_start(wo[:], t["L0_xattn_Wo"].rearrange("(c e) k -> e c k", e=P)).then_inc(in_o, 16)
            sp.dma_start(wkckv[:], t["L0_xattn_w_kc_kv"].rearrange("h k d -> k h d")).then_inc(in_o, 16)
            sp.wait_ge(a_done, H0)
            sp.dma_start(t["w2_scr"].rearrange("h p c -> p h c"), w2[:]).then_inc(stored, 16)
            sp.wait_ge(d_done, N_M + N_VO)
            sp.dma_start(t["wvo_scr"], wvo[:]).then_inc(stored, 16)
            sp.wait_ge(m2_ready, 2)
            sp.dma_start(t["m_scr"].rearrange("h p c -> p h c"),
                         m2[:].rearrange("p h a b d -> p h (a b d)")).then_inc(stored, 16)
            sp.wait_ge(stored, 48)

        @block.tensor
        def _(pe):
            pe.wait_ge(in_q, 32)
            for h in range(H0):
                if h >= 4:
                    pe.wait_ge(a_done, h - 3)
                for c in range(DK):
                    mm = pe.matmul(psA[h % 4][:, c * DCQ:(c + 1) * DCQ], wq[:, h, c * P:(c + 1) * P],
                                   wkcq[:, h, :], start=True, stop=True)
                mm.then_inc(a_full, 1)
            pe.wait_ge(in_r, 48)
            for g in range(H0 // 2):
                n = A_RT + g
                pe.wait_ge(a_done, n - 3)
                for u in range(2):
                    h, o = 2 * g + u, u * (DCQ + DC)
                    for e in range(2):
                        pe.transpose(psA[n % 4][0:R0, o + e * HALF:o + (e + 1) * HALF], wqr[:, h, e, :],
                                     ident[0:HALF, 0:HALF])
                    mm = pe.transpose(psA[n % 4][0:R0, o + DCQ:o + DCQ + DC], wkr[:, h, :], ident[0:DC, 0:DC])
                mm.then_inc(a_full, 1)
            pe.wait_ge(in_o, 32)
            for g in range(H0 // 2):
                n = A_WOT + g
                pe.wait_ge(a_done, n - 3)
                for u in range(2):
                    for c in range(DK):
                        mm = pe.transpose(psA[n % 4][:, u * D + c * P:u * D + (c + 1) * P],
                                          wo[:, c, (2 * g + u) * P:(2 * g + u + 1) * P], ident[:])
                mm.then_inc(a_full, 1)
            for g in range(N_M):
                pe.wait_ge(a_done, A_RT + g + 1)
                if g >= 4:
                    pe.wait_ge(d_done, g - 3)
                for u in range(2):
                    h = 2 * g + u
                    for e in range(2):
                        mm = pe.matmul(psD[g % 4][0:HALF, (2 * u + e) * DC:(2 * u + e + 1) * DC],
                                       rT[:, h, e * HALF:(e + 1) * HALF], rT[:, h, DCQ:DCQ + DC],
                                       start=True, stop=True)
                mm.then_inc(d_full, 1)
            for g in range(N_VO):
                n = N_M + g
                pe.wait_ge(a_done, A_WOT + 2 * g + 2)
                pe.wait_ge(d_done, n - 3)
                for u in range(2):
                    for k in range(2):
                        h = 4 * g + 2 * u + k
                        mm = pe.matmul(psD[n % 4][k * DC:(k + 1) * DC, u * D:(u + 1) * D], wkckv[:, h, :],
                                       woT[:, h, :], start=True, stop=True)
                mm.then_inc(d_full, 1)
            pe.wait_ge(norms_ready, 2 * H0)
            pe.wait_ge(consts, 2)
            n = N_M + N_VO
            pe.wait_ge(d_done, n - 3)
            pe.matmul(psD[n % 4][:, 0:2 * H0], ones[:], norms[:], start=True, stop=True).then_inc(d_full, 1)
            for g in range(N_XT):
                n = N_M + N_VO + 1 + g
                pe.wait_ge(xln_ready, 2 * g + 2)
                pe.wait_ge(d_done, n - 3)
                for c in range(DK):
                    for u in range(2):
                        mm = pe.transpose(psD[n % 4][:, c * 256 + u * P:c * 256 + (u + 1) * P],
                                          x[:, 2 * g + u, c * P:(c + 1) * P], ident[:])
                mm.then_inc(d_full, 1)

        @block.scalar
        def _(act):
            act.dma_start(x[:], t["x"].rearrange("b (s p) d -> p (b s) d", p=P)).then_inc(in_x, 16)
            for h in range(H0):
                act.wait_ge(a_full, h + 1)
                nc.scalar.activation(w2[:, h, :], psA[h % 4][:, 0:DK * DCQ], ACT.Copy).then_inc(a_done, 1)
            act.wait_ge(consts, 1)
            act.wait_ge(var_ready, 1)
            nc.scalar.activation(root[:], agg[:, :, 1], ACT.Sqrt, bias=eps[:, 0:1]).then_inc(root_ready, 1)
            for g in range(H0 // 2):
                n = A_RT + g
                act.wait_ge(a_full, n + 1)
                nc.scalar.activation(rT[:, 2 * g:2 * g + 2, :].rearrange("r h c -> r (h c)"),
                                     psA[n % 4][0:R0, :], ACT.Copy).then_inc(a_done, 1)
            for g in range(H0 // 2):
                n = A_WOT + g
                act.wait_ge(a_full, n + 1)
                nc.scalar.activation(woT[:, 2 * g:2 * g + 2, :].rearrange("k h e -> k (h e)"),
                                     psA[n % 4][:, :], ACT.Copy).then_inc(a_done, 1)
            for h in range(H0):
                if h == 0:
                    act.wait_ge(a_done, H0)
                    act.wait_ge(consts, 3)
                else:
                    act.wait_ge(norms_ready, h)
                nc.scalar.activation(junk[:], w2[:, h, :], ACT.Square,
                                     accum_out=norms[:, h:h + 1]).then_inc(norms_ready, 1)
            act.wait_ge(d_done, N_M)
            for h in range(H0):
                act.wait_ge(norms_ready, H0 + h)
                nc.scalar.activation(junk[0:HALF, 0:2 * DC], m[:, h, :, :].rearrange("p e d -> p (e d)"),
                                     ACT.Square,
                                     accum_out=norms[0:HALF, H0 + h:H0 + h + 1]).then_inc(norms_ready, 1)
            act.wait_ge(b2_ready, 1)
            nc.scalar.activation(bound[:], bound[:], ACT.Sqrt).then_inc(bound_ready, 1)

        @block.vector
        def _(dve):
            count = [0]

            def link(ins):
                count[0] += 1
                ins.then_inc(chain, 1)
                dve.wait_ge(chain, count[0])

            link(nc.vector.memset(keep["ln1024"][:], LN_1024))
            nc.vector.memset(eps[:], EPS).then_inc(consts, 1)
            nc.vector.memset(ones[:], 1.0).then_inc(consts, 1)
            nc.vector.memset(norms[:], 0.0).then_inc(consts, 1)
            dve.wait_ge(in_x, 16)
            layer_norm_stats(dve, nc, link, x, stats, agg, NT)
            dve.sem_inc(var_ready, 1)

            def drain_m():
                for g in range(N_M):
                    dve.wait_ge(d_full, g + 1)
                    nc.vector.tensor_copy(m[:, 2 * g:2 * g + 2, :, :].rearrange("p h e d -> p (h e d)"),
                                          psD[g % 4][0:HALF, 0:4 * DC]).then_inc(d_done, 1)

            drain_m()
            dve.wait_ge(root_ready, 1)
            rstd_refined(nc, link, rstd[:], root[:], agg, tmp[:])
            for j in range(NT):
                nc.vector.tensor_scalar(x[:, j, :], x[:, j, :], agg[:, j, 0:1], rstd[:, j:j + 1],
                                        ALU.subtract, ALU.mult).then_inc(xln_ready, 1)
            for g in range(N_VO):
                n = N_M + g
                dve.wait_ge(d_full, n + 1)
                nc.vector.tensor_copy(wvo[:, 2 * g:2 * g + 2, :].rearrange("p g e -> p (g e)"),
                                      psD[n % 4][:, :]).then_inc(d_done, 1)
            n = N_M + N_VO
            dve.wait_ge(d_full, n + 1)
            nc.vector.tensor_copy(nsum[:], psD[n % 4][:, 0:2 * H0]).then_inc(d_done, 1)
            dve.wait_ge(d_done, n + 1)
            link(nc.vector.tensor_tensor(bound[:], nsum[:, 0:H0], nsum[:, H0:2 * H0], ALU.mult))
            link(nc.vector.tensor_scalar(bound[:], bound[:], 4.0 * D, 1e-30, ALU.mult, ALU.add))
            dve.sem_inc(b2_ready, 1)
            dve.wait_ge(bound_ready, 1)
            link(nc.vector.reciprocal(bound[:], bound[:]))
            link(nc.vector.tensor_scalar(keep["qscale"][:], bound[:], QK_TOP, None, ALU.mult))
            for k in range(2):
                nc.vector.tensor_tensor(
                    m2[:, :, :, k, :], m[:],
                    keep["qscale"][0:HALF, :].unsqueeze(2).unsqueeze(3).broadcast_to([HALF, H0, 2, DC]),
                    ALU.mult).then_inc(m2_ready, 1)
            for g in range(N_XT):
                n = N_M + N_VO + 1 + g
                dve.wait_ge(d_full, n + 1)
                nc.vector.tensor_copy(keep["xT"][:, :, 256 * g:256 * (g + 1)],
                                      psD[n % 4][:].rearrange("p (c s) -> p c s", c=DK)).then_inc(d_done, 1)


def phase_context(nc, ctx, t, keep):
    def sb(name, shape, dt=F32):
        return ctx.enter_context(nc.sbuf_tensor(name, shape, dt))

    def sem(name):
        return new_semaphore(nc, name)

    kv = sb("b_kv", [P, B, LT, DC])
    rot = sb("b_rot", [P, B, LT, DC])
    cosk = sb("b_cosk", [P, LT, DC])
    sink = sb("b_sink", [P, LT, DC])
    amax = sb("b_amax", [P, B])
    aall = sb("b_aall", [P, B])
    ktop = sb("b_ktop", [P, 1])
    kscale = sb("b_kscale", [P, 1])
    ps = [ctx.enter_context(nc.psum_tensor(f"b_ps{i}", [P, 1024], F16)) for i in range(8)]
    in_t, in_ident, zeroed = sem("in_t"), sem("in_ident"), sem("b_zeroed")
    in_k = [sem(f"in_k{b}") for b in range(B)]
    rotated, roped, chain = sem("rotated"), sem("roped"), sem("b_chain")
    amax_ready, aall_ready = sem("amax_ready"), sem("aall_ready")
    v_ready, kt_full, k1_done, k2_done = sem("v_ready"), sem("kt_full"), sem("k1_done"), sem("k2_done")
    filled = sem("b_filled")
    V, KK1, KK2 = keep["V"], keep["KK1"], keep["KK2"]
    FIRST = 7
    jobs = [(b, lo, hi) for b in range(B) for lo, hi in ((0, FIRST), (FIRST, LT))]

    with nc.Block() as block:
        @block.sync
        def _(sp):
            sp.dma_start(cosk[:], t["cosk"]).then_inc(in_t, 16)
            sp.dma_start(sink[:], t["sink"]).then_inc(in_t, 16)
            sp.wait_ge(zeroed, 1)
            for b in range(B):
                sp.dma_start(kv[:, b, 0:LT - 1, :],
                             t["ctx_512"][b, 0:(LT - 1) * P, :].rearrange("(t p) d -> p t d", p=P)
                             ).then_inc(in_k[b], 16)
                sp.dma_start(kv[0:LLAST, b, LT - 1, :], t["ctx_512"][b, (LT - 1) * P:L, :]).then_inc(in_k[b], 16)

        @block.gpsimd
        def _(pool):
            nc.gpsimd.memset(kv[:, :, LT - 1, :], 0.0).then_inc(zeroed, 1)
            pool.wait_ge(in_t, 32)
            h = DC // 2
            for b in range(B):
                pool.wait_ge(in_k[b], 32)
                nc.gpsimd.tensor_tensor(rot[:, b, :, 0:h], kv[:, b, :, h:DC], sink[:, :, 0:h],
                                        ALU.mult).then_inc(rotated, 1)
                nc.gpsimd.tensor_tensor(rot[:, b, :, h:DC], kv[:, b, :, 0:h], sink[:, :, h:DC],
                                        ALU.mult).then_inc(rotated, 1)
            pool.wait_ge(amax_ready, B)
            nc.gpsimd.partition_all_reduce(aall[:], amax[:], P, bass.bass_isa.ReduceOp.max
                                           ).then_inc(aall_ready, 1)
            pool.wait_ge(aall_ready, 1)
            nc.gpsimd.memset(KK2[0:2 * SHIFT_ROWS, :], SHIFT_ONE).then_inc(filled, 1)
            pool.wait_ge(filled, 1)
            nc.gpsimd.memset(KK2[2 * SHIFT_ROWS:DC, :], 0.0).then_inc(filled, 1)
            pool.wait_ge(filled, 2)

        @block.vector
        def _(dve):
            count = [0]

            def link(ins):
                count[0] += 1
                ins.then_inc(chain, 1)
                dve.wait_ge(chain, count[0])

            def drain(b):
                for k in range(2):
                    n = 2 * b + k
                    _, lo, hi = jobs[n]
                    w = min(hi * P, L) - lo * P
                    dve.wait_ge(k1_done, n + 1)
                    nc.vector.tensor_copy(KK2[DC:P, b * L + lo * P:b * L + lo * P + w],
                                          KK1[DC:P, b * L + lo * P:b * L + lo * P + w]).then_inc(k2_done, 1)

            for b in range(B):
                nc.vector.memset(V[:, b, :, 2 * DC:2 * DC + 1], 1.0).then_inc(v_ready, 1)
            dve.wait_ge(in_t, 32)
            for b in range(B):
                dve.wait_ge(rotated, 2 * (b + 1))
                dve.wait_ge(in_k[b], 32)
                link(nc.vector.tensor_tensor(kv[:, b], kv[:, b], cosk[:], ALU.mult))
                nc.vector.tensor_tensor(kv[:, b], kv[:, b], rot[:, b], ALU.add).then_inc(roped, 1)
                dve.wait_ge(roped, b + 1)
                nc.vector.tensor_reduce(amax[:, b:b + 1], kv[:, b], AX.XY, ALU.max,
                                        apply_absolute_value=True).then_inc(amax_ready, 1)
            dve.wait_ge(aall_ready, 1)
            link(nc.vector.tensor_reduce(ktop[:], aall[:], AX.X, ALU.max))
            link(nc.vector.tensor_scalar(ktop[:], ktop[:], 1e-30, 1.0 / QK_TOP, ALU.add, ALU.mult))
            link(nc.vector.reciprocal(kscale[:], ktop[:]))
            link(nc.vector.tensor_scalar(keep["qk_scale"][:], keep["qscale"][:], kscale[:, 0:1], None, ALU.mult))
            link(nc.vector.reciprocal(keep["qk_scale"][:], keep["qk_scale"][:]))
            link(nc.vector.tensor_copy(keep["k_unscale"][:], ktop[:]))
            for b in range(B):
                link(nc.vector.tensor_scalar(V[:, b, :, DC:2 * DC], kv[:, b], kscale[:, 0:1], None, ALU.mult))
                nc.vector.scalar_tensor_tensor(out=V[:, b, :, 0:DC], in0=kv[:, b], scalar=kscale[:, 0:1],
                                               in1=V[:, b, :, DC:2 * DC], op0=ALU.mult,
                                               op1=ALU.subtract).then_inc(v_ready, 1)
                if b >= 1:
                    drain(b - 1)
            drain(B - 1)

        @block.tensor
        def _(pe):
            pe.wait_ge(in_ident, 16)
            for n, (b, lo, hi) in enumerate(jobs):
                pe.wait_ge(v_ready, B + b + 1)
                if n >= 8:
                    pe.wait_ge(k1_done, n - 7)
                for i in range(lo, hi):
                    r = P if i < LT - 1 else LLAST
                    mm = pe.transpose(ps[n % 8][:, (i - lo) * P:(i - lo) * P + r], V[0:r, b, i, 0:2 * DC],
                                      keep["ident16"][0:r, 0:r])
                mm.then_inc(kt_full, 1)

        @block.scalar
        def _(act):
            act.dma_start(keep["ident16"][:], t["ident16"]).then_inc(in_ident, 16)
            for n, (b, lo, hi) in enumerate(jobs):
                w = min(hi * P, L) - lo * P
                act.wait_ge(kt_full, n + 1)
                nc.scalar.activation(KK1[:, b * L + lo * P:b * L + lo * P + w], ps[n % 8][:, 0:w],
                                     ACT.Copy).then_inc(k1_done, 1)


def phase_attention0(nc, ctx, t, keep):
    def sb(name, shape, dt=F32):
        return ctx.enter_context(nc.sbuf_tensor(name, shape, dt))

    def sem(name):
        return new_semaphore(nc, name)

    HALF_L = 400
    TAIL = L - 3 * HALF_L
    AHEAD = 4
    V, KK1, KK2, xT = keep["V"], keep["KK1"], keep["KK2"], keep["xT"]
    kk1 = sb("c_kk1", [P, L], F16)
    kk2 = sb("c_kk2", [P, L], F16)
    kkm = [sb(f"c_kkm{i}", [P, 2 * TAIL], F16) for i in range(2)]
    vb = sb("c_vb", [P, LT, 2 * DC + 1], F16)
    xb = sb("c_xb", [P, DK, S])
    ident16 = keep["ident16"]
    tabA = sb("c_tabA", [HALF, 2 * S])
    tabB = sb("c_tabB", [HALF, 2 * S])
    w2s = sb("c_w2s", [P, DK * DCQ])
    ms = sb("c_ms", [HALF, 2, P])
    ropeA = sb("c_ropeA", [HALF, 2, S])
    ropeB = sb("c_ropeB", [HALF, 2, S])
    roped = sb("c_roped", [HALF, 2, S])
    q1 = [sb(f"c_q1_{i}", [P, S], F16) for i in range(AHEAD)]
    q2 = [sb(f"c_q2_{i}", [P, S], F16) for i in range(AHEAD)]
    prob = [sb(f"c_prob{i}", [P, 4 * S if i < 3 else S]) for i in range(4)]
    rest = [sb(f"c_rest{i}", [P, 4 * S if i < 3 else S], F16) for i in range(4)]
    mxp = sb("c_mxp", [P, ST, 2])
    mx = sb("c_mx", [P, ST])
    mcol = sb("c_mcol", [P, ST, DC], F16)
    exp_scale = [sb(f"c_exp_scale{i}", [P, 1]) for i in range(AHEAD)]
    W = 2 * DC + 1
    acc = [sb(f"c_acc{i}", [P, ST, W]) for i in range(2)]
    psS = [ctx.enter_context(nc.psum_tensor(f"c_psS{i}", [P, 1024], F32)) for i in range(2)]
    psM = ctx.enter_context(nc.psum_tensor("c_psM", [P, 2, 512], F32))
    psQ = ctx.enter_context(nc.psum_tensor("c_psQ", [P, 512], F32))
    psV = ctx.enter_context(nc.psum_tensor("c_psV", [P, 512], F32))
    shiftT = psM[0:DC, :, HALF_L:HALF_L + DC].bitcast(F16)

    in_tab, in_w2, in_m = sem("in_tab"), sem("in_w2"), sem("in_m")
    qb_full, rope_done, qk_full = sem("qb_full"), sem("rope_done"), sem("qk_full")
    rope_added = sem("rope_added")
    qh_done, ql_done = sem("qh_done"), sem("ql_done")
    mx_full, mx_done, mx_joined, mcol_done = sem("mx_full"), sem("mx_done"), sem("mx_joined"), sem("mcol_done")
    shift_full, shift_done = sem("shift_full"), sem("shift_done")
    s_full, exp_done = sem("s_full"), sem("exp_done")
    rest_dve, rest_pool = sem("rest_dve"), sem("rest_pool")
    pv_done = sem("pv_done")
    pv_drained = sem("pv_drained")
    sent = [sem(f"sent{i}") for i in range(2)]
    zeroed = sem("c_zeroed")
    in_kk = [sem(f"in_kk{g}") for g in range(4)]
    in_v = [sem(f"in_v{g}") for g in range(4)]
    in_kkm = [sem(f"in_kkm{i}") for i in range(2)]
    in_xb = sem("in_xb")

    N = B * H0
    GROUPS = [(0, 4), (4, 8), (8, 12), (12, 13)]
    CHUNKS = [((0, HALF_L), (HALF_L, HALF_L)), ((L - 2 * TAIL, TAIL), (L - TAIL, TAIL))]
    POOL_COLS = 704

    def head(n):
        return n % H0

    with nc.Block() as block:
        @block.sync
        def _(sp):
            sp.dma_start(tabA[:], t["tabA"]).then_inc(in_tab, 16)
            sp.dma_start(tabB[:], t["tabB"]).then_inc(in_tab, 16)

            def load_w2(n):
                sp.dma_start(w2s[:], t["w2_scr"][head(n)]).then_inc(in_w2, 16)

            def load_m(n):
                sp.dma_start(ms[:], t["m_scr"][head(n)].rearrange("p (a b) -> p a b", a=2)).then_inc(in_m, 16)

            def refill_x(b):
                sp.dma_start(xb[:], xT[:, :, bass.ds(b * S, S)]).then_inc(in_xb, 16)

            def refill_maxima(b, half):
                c0, w = CHUNKS[half][0][0], 2 * CHUNKS[half][0][1]
                sp.dma_start(kkm[half][:, 0:w], KK1[:, bass.ds(b * L + c0, w)]).then_inc(in_kkm[half], 16)

            def refill_scores(b, g):
                c0, c1 = GROUPS[g][0] * P, min(GROUPS[g][1] * P, L)
                for part, whole in ((kk1, KK1), (kk2, KK2)):
                    sp.dma_start(part[:, c0:c1], whole[:, bass.ds(b * L + c0, c1 - c0)]).then_inc(in_kk[g], 16)

            def refill_values(b, g):
                lo, hi = GROUPS[g]
                sp.dma_start(vb[:, lo:hi, :], V[:, bass.ds(b, 1), lo:hi, :].rearrange("p o t w -> p (o t) w")
                             ).then_inc(in_v[g], 16)

            refill_x(0)
            load_w2(0)
            load_m(0)
            for half in range(2):
                refill_maxima(0, half)
            for g in range(4):
                refill_scores(0, g)
            for g in range(4):
                refill_values(0, g)
            for n in range(AHEAD - 1):
                sp.wait_ge(qb_full, n + 1)
                load_w2(n + 1)
                sp.wait_ge(qk_full, n + 1)
                load_m(n + 1)
            sp.sem_inc(sent[0], 16)
            sp.sem_inc(sent[1], 16)

            def step(n, u, b=None):
                if b is not None and u == 3:
                    sp.wait_ge(s_full, 4 * n + 2)
                    refill_scores(b, 1)
                    sp.wait_ge(s_full, 4 * n + 3)
                    refill_scores(b, 2)
                    sp.wait_ge(pv_done, 4 * n + 5)
                    refill_values(b, 0)
                sp.wait_ge(qb_full, n + 4)
                if b is not None and u == 0:
                    refill_x(b)
                    sp.wait_ge(in_xb, 16 * (b_count(n) + 2))
                load_w2(n + 4)
                if b is not None and u == 3:
                    sp.wait_ge(s_full, 4 * n + 4)
                    refill_scores(b, 3)
                    sp.wait_ge(pv_done, 4 * n + 6)
                    refill_values(b, 1)
                if b is not None and u == 2:
                    sp.wait_ge(mx_full, 4 * (n + 1) + 4)
                    refill_maxima(b, 1)
                    sp.wait_ge(s_full, 4 * (n + 1) + 1)
                    refill_scores(b, 0)
                sp.wait_ge(qk_full, n + 4)
                load_m(n + 4)
                if b is not None and u == 1:
                    sp.wait_ge(mx_full, 4 * (n + 2) + 3)
                    refill_maxima(b, 0)
                if b is not None and u == 3:
                    sp.wait_ge(pv_done, 4 * n + 7)
                    refill_values(b, 2)
                sp.wait_ge(pv_drained, n + 2)
                sp.dma_start(t["acc_scr"][n], acc[u % 2][:]).then_inc(sent[u % 2], 16)
                if b is not None and u == 3:
                    refill_values(b, 3)

            def b_count(n):
                return n // H0

            with sp.Fori(0, B) as b:
                with sp.Fori(0, H0 // AHEAD - 1) as j:
                    for u in range(AHEAD):
                        step(b * H0 + j * AHEAD + u, u)
                for u in range(AHEAD):
                    step(b * H0 + (H0 - AHEAD + u), u, (b + 1) % B)
            for u in range(2):
                sp.wait_ge(sent[u], 16 + 16 * (N // 2))
            sp.wait_ge(in_w2, 16 * (N + 4))
            for g in range(4):
                sp.wait_ge(in_kk[g], 32 * (B + 1))
                sp.wait_ge(in_v[g], 16 * (B + 1))
            for half in range(2):
                sp.wait_ge(in_kkm[half], 16 * (B + 1))
            sp.wait_ge(in_xb, 16 * (B + 1))
            sp.wait_ge(in_m, 16 * (N + 4))

        @block.tensor
        def _(pe):
            def q_big(n, e, cs=tuple(range(DK))):
                if e == 0 and cs[0] == 0:
                    pe.wait_ge(in_w2, 16 * (n + 1))
                for c in cs:
                    mm = pe.matmul(psQ[0:HALF, e * S:(e + 1) * S],
                                   w2s[:, c * DCQ + e * HALF:c * DCQ + (e + 1) * HALF],
                                   xb[:, c, :], start=(c == 0), stop=(c == DK - 1))
                if e == 1 and cs[-1] == DK - 1:
                    mm.then_inc(qb_full, 1)

            def q_lat(n):
                pe.wait_ge(rope_added, n + 1)
                pe.wait_ge(in_m, 16 * (n + 1))
                for e in range(2):
                    mm = pe.matmul(psQ[:, 0:S], ms[:, e, :], roped[:, e, :], start=(e == 0), stop=(e == 1))
                mm.then_inc(qk_full, 1)

            def maxima(n, k, slot):
                st, half = divmod(k, 2)
                if k == 0 and not (isinstance(n, int) and n == 0):
                    pe.wait_ge(shift_done, n)
                if not (isinstance(n, int) and n == 0 and k == 0):
                    pe.wait_ge(mx_done, 4 * n + k)
                for i, (c0, w) in enumerate(CHUNKS[half]):
                    mm = pe.matmul(psM[:, i, 0:w], q1[slot][:, st * P:(st + 1) * P],
                                   kkm[half][:, i * w:(i + 1) * w], start=True, stop=True)
                mm.then_inc(mx_full, 1)

            def shift(n):
                for st in range(ST):
                    mm = pe.transpose(shiftT[:, st, :], mcol[:, st, :], ident16[:])
                mm.then_inc(shift_full, 1)

            def scores(n, g, slot, part=None):
                lo, hi = GROUPS[g]
                k0, k1 = part or (0, 2 * (hi - lo))
                if k0 == 0:
                    pe.wait_ge(exp_done, 4 * n + g + 1)
                for k in range(k0, k1):
                    one, i = divmod(k, hi - lo)
                    src, mov = ((kk1, q1), (kk2, q2))[one]
                    r = P if lo + i < LT - 1 else LLAST
                    mm = pe.matmul(psS[g % 2][0:r, i * S:(i + 1) * S],
                                   src[:, (lo + i) * P:(lo + i) * P + r], mov[slot][:, :],
                                   start=(one == 0 and i % 2 == 0), stop=(one == 1), skip_group_check=True)
                if k1 == 2 * (hi - lo):
                    mm.then_inc(s_full, 1)

            def values(n, g, part=None):
                lo, hi = GROUPS[g]
                t0, t1 = part or (0, hi - lo)
                if g == 0:
                    pe.wait_ge(pv_drained, n + 1)
                if t0 == 0:
                    if g < 3:
                        pe.wait_ge(rest_pool, 3 * n + g + 1)
                    pe.wait_ge(rest_dve, 4 * n + g + 1)
                high = prob[g][:].bitcast(BF16).rearrange("p (c t) -> p c t", t=2)[:, :, 1]
                for i in range(lo + t0, lo + t1):
                    r = P if i < LT - 1 else LLAST
                    for st in range(ST):
                        c0 = (i - lo) * S + st * P
                        pe.matmul(psV[:, st * W:(st + 1) * W], high[0:r, c0:c0 + P],
                                  vb[0:r, i, :],
                                  start=(i == 0 and st == 0), stop=False, skip_group_check=True)
                        mm = pe.matmul(psV[:, st * W + DC:(st + 1) * W], rest[g][0:r, c0:c0 + P],
                                       vb[0:r, i, DC:W],
                                       start=False, stop=(i == LT - 1), skip_group_check=True)
                if lo + t1 == hi:
                    mm.then_inc(pv_done, 1)

            pe.sem_inc(pv_done, 4)
            pe.wait_ge(in_xb, 16)
            q_big(0, 0)
            q_big(0, 1)
            q_lat(0)
            for n in range(2):
                pe.wait_ge(qh_done, n + 1)
                if n == 0:
                    for i in range(2):
                        pe.wait_ge(in_kkm[i], 16)
                maxima(n, 0, n)
                pe.wait_ge(ql_done, n + 1)
                q_big(n + 1, 0)
                q_big(n + 1, 1)
                for k in range(1, 4 - n):
                    maxima(n, k, n)
                if n == 0:
                    pe.wait_ge(mcol_done, 2)
                    shift(0)
                q_lat(n + 1)
            pe.wait_ge(shift_done, 1)
            for g in range(4):
                pe.wait_ge(in_kk[g], 32)
                pe.wait_ge(in_v[g], 16)
            scores(0, 0, 0)
            with pe.Fori(0, N // AHEAD) as j:
                for u in range(AHEAD):
                    n = AHEAD * j + u
                    s1, s2 = (u + 1) % AHEAD, (u + 2) % AHEAD
                    scores(n, 1, u)
                    maxima(n + 1, 3, s1)
                    for i in range(4):
                        scores(n, 2, u, (2 * i, 2 * i + 2))
                        values(n, 0, (i, i + 1))
                    pe.wait_ge(ql_done, n + 3)
                    q_big(n + 3, 0)
                    q_big(n + 3, 1, (0,))
                    pe.wait_ge(mcol_done, 2 * n + 4)
                    q_big(n + 3, 1, (1,))
                    shift(n + 1)
                    scores(n, 3, u)
                    maxima(n + 2, 0, s2)
                    for i in range(4):
                        scores(n + 1, 0, s1, (2 * i, 2 * i + 2))
                        values(n, 1, (i, i + 1))
                    maxima(n + 2, 1, s2)
                    q_lat(n + 3)
                    values(n, 2)
                    maxima(n + 2, 2, s2)
                    values(n, 3)

        @block.scalar
        def _(act):
            def q_high(n, slot):
                act.wait_ge(qk_full, n + 1)
                nc.scalar.activation(q1[slot][:], psQ[:, 0:S], ACT.Copy).then_inc(qh_done, 1)

            def shift_copy(n, slot):
                act.wait_ge(shift_full, n + 1)
                nc.scalar.activation(q2[slot][0:DC, :].rearrange("p (s c) -> p s c", s=ST), shiftT, ACT.Copy).then_inc(shift_done, 1)

            def exp(n, g, slot):
                lo, hi = GROUPS[g]
                r = P if hi < LT else LLAST
                w = (hi - lo) * S
                act.wait_ge(s_full, 4 * n + g + 1)
                act.wait_ge(in_kk[(g + 2) % 4], 32 * ((n + (g + 2) // 4) // H0) + 32)
                act.wait_ge(pv_done, 4 * n + g + 1)
                nc.scalar.activation(prob[g][0:r, 0:w], psS[g % 2][0:r, 0:w], ACT.Exp, bias=keep["ln1024"][0:r, :],
                                     scale=exp_scale[slot][0:r, :]).then_inc(exp_done, 1)

            act.sem_inc(exp_done, 2)
            act.sem_inc(pv_drained, 1)
            q_high(0, 0)
            shift_copy(0, 0)
            q_high(1, 1)
            q_high(2, 2)
            exp(0, 0, 0)
            with act.Fori(0, N // AHEAD) as j:
                for u in range(AHEAD):
                    n = AHEAD * j + u
                    exp(n, 1, u)
                    exp(n, 2, u)
                    shift_copy(n + 1, (u + 1) % AHEAD)
                    exp(n, 3, u)
                    exp(n + 1, 0, (u + 1) % AHEAD)
                    q_high(n + 3, (u + 3) % AHEAD)
                    act.wait_ge(pv_done, 4 * n + 8)
                    act.wait_ge(sent[u % 2], 16 * (2 * j + u // 2) + 16)
                    nc.scalar.activation(acc[u % 2][:].rearrange("p s w -> p (s w)"), psV[:, 0:ST * W],
                                         ACT.Copy).then_inc(pv_drained, 1)

        @block.vector
        def _(dve):
            def rope(n):
                dve.wait_ge(qb_full, n + 1)
                if not isinstance(n, int) or n > 0:
                    dve.wait_ge(qk_full, n)
                nc.vector.tensor_tensor(ropeA[:].rearrange("p e s -> p (e s)"), psQ[0:HALF, :], tabA[:],
                                        ALU.mult).then_inc(rope_done, 1)
                for e in range(2):
                    nc.vector.tensor_tensor(ropeB[:, 1 - e, :], psQ[0:HALF, e * S:(e + 1) * S],
                                            tabB[:, e * S:(e + 1) * S], ALU.mult).then_inc(rope_done, 1)

            def q_low(n, slot):
                dve.wait_ge(qh_done, n + 1)
                nc.vector.tensor_tensor(q2[slot][DC:P, :], psQ[DC:P, 0:S], q1[slot][DC:P, :],
                                        ALU.subtract).then_inc(ql_done, 1)

            def reduce_max(n, k):
                st, half = divmod(k, 2)
                dve.wait_ge(mx_full, 4 * n + k + 1)
                dve.wait_ge(in_kkm[(k + 1) % 2], 16 * ((n + (k + 1) // 4) // H0) + 16)
                w = CHUNKS[half][0][1]
                nc.vector.tensor_reduce(mxp[:, st, half:half + 1], psM[:, :, 0:w], AX.XY,
                                        ALU.max).then_inc(mx_done, 1)

            def join(n, slot):
                dve.wait_ge(mx_done, 4 * n + 4)
                nc.vector.tensor_scalar(exp_scale[slot][:], keep["qk_scale"][:, bass.ds(head(n), 1)], 1.0, None,
                                        ALU.mult).then_inc(mx_joined, 1)
                nc.vector.tensor_reduce(mx[:], mxp[:], AX.X, ALU.max).then_inc(mx_joined, 1)
                dve.wait_ge(mx_joined, 2 * n + 2)
                if not isinstance(n, int) or n > 0:
                    dve.wait_ge(shift_full, n)
                m = mx[:].unsqueeze(2).broadcast_to([P, ST, SHIFT_ROWS])
                nc.vector.tensor_scalar(mcol[:, :, 0:SHIFT_ROWS], m, -SHIFT_MUL, None,
                                        ALU.mult).then_inc(mcol_done, 1)
                dve.wait_ge(mcol_done, 2 * n + 1)
                nc.vector.scalar_tensor_tensor(out=mcol[:, :, SHIFT_ROWS:2 * SHIFT_ROWS], in0=m,
                                               scalar=-SHIFT_MUL, in1=mcol[:, :, 0:SHIFT_ROWS],
                                               op0=ALU.mult, op1=ALU.subtract).then_inc(mcol_done, 1)

            def rest_of(n, g):
                lo, hi = GROUPS[g]
                r = P if hi < LT else LLAST
                c0, c1 = (POOL_COLS if g < 3 else 0), (hi - lo) * S
                dve.wait_ge(exp_done, 4 * n + g + 3)
                dve.wait_ge(in_v[g], 16 * (n // H0) + 16)
                high = prob[g][:].bitcast(BF16).rearrange("p (c t) -> p c t", t=2)[:, :, 1]
                nc.vector.tensor_tensor(rest[g][0:r, c0:c1], prob[g][0:r, c0:c1], high[0:r, c0:c1],
                                        ALU.subtract).then_inc(rest_dve, 1)

            nc.vector.memset(mcol[:], 0.0).then_inc(zeroed, 1)
            dve.wait_ge(zeroed, 1)
            dve.wait_ge(in_tab, 32)
            rope(0)
            q_low(0, 0)
            for n in range(2):
                reduce_max(n, 0)
                rope(n + 1)
                reduce_max(n, 1)
                reduce_max(n, 2)
                if n == 0:
                    reduce_max(0, 3)
                    join(0, 0)
                q_low(n + 1, n + 1)
            rest_of(0, 0)
            with dve.Fori(0, N // AHEAD) as j:
                for u in range(AHEAD):
                    n = AHEAD * j + u
                    reduce_max(n + 1, 3)
                    join(n + 1, (u + 1) % AHEAD)
                    rest_of(n, 1)
                    rest_of(n, 2)
                    rope(n + 3)
                    reduce_max(n + 2, 0)
                    rest_of(n, 3)
                    reduce_max(n + 2, 1)
                    rest_of(n + 1, 0)
                    reduce_max(n + 2, 2)
                    q_low(n + 3, (u + 3) % AHEAD)

        @block.gpsimd
        def _(pool):
            def rope_sum(n):
                pool.wait_ge(rope_done, 3 * n + 3)
                if not isinstance(n, int) or n > 0:
                    pool.wait_ge(qk_full, n)
                nc.gpsimd.tensor_tensor(roped[:], ropeA[:], ropeB[:], ALU.add).then_inc(rope_added, 1)

            def rest_of(n, g):
                pool.wait_ge(exp_done, 4 * n + g + 3)
                high = prob[g][:].bitcast(BF16).rearrange("p (c t) -> p c t", t=2)[:, :, 1]
                nc.gpsimd.tensor_tensor(rest[g][:, 0:POOL_COLS], prob[g][:, 0:POOL_COLS],
                                        high[:, 0:POOL_COLS], ALU.subtract).then_inc(rest_pool, 1)

            for n in range(3):
                rope_sum(n)
            rest_of(0, 0)
            with pool.Fori(0, N // AHEAD) as j:
                for u in range(AHEAD):
                    n = AHEAD * j + u
                    rest_of(n, 1)
                    rest_of(n, 2)
                    rope_sum(n + 3)
                    rest_of(n + 1, 0)


def phase_project0(nc, ctx, t, keep, x):
    def sb(name, shape, dt=F32):
        return ctx.enter_context(nc.sbuf_tensor(name, shape, dt))

    def sem(name):
        return new_semaphore(nc, name)

    W = 2 * DC + 1
    G = H0 // 2
    wvo = sb("d_wvo", [P, G, D])
    ident = sb("d_ident", [P, P])
    acc = [sb(f"d_acc{i}", [P, H0, ST, W]) for i in range(2)]
    cs = [sb(f"d_cs{i}", [P, ST, H0, DC]) for i in range(2)]
    rec = sb("d_rec", [P, H0, ST])
    cT = [sb(f"d_cT{i}", [P, G, P]) for i in range(2)]
    psT = [ctx.enter_context(nc.psum_tensor(f"d_psT{i}", [P, 512], F32)) for i in range(4)]
    psO = [ctx.enter_context(nc.psum_tensor(f"d_psO{i}", [P, 512], F32)) for i in range(2)]
    in_c = sem("d_in_c")
    in_x = sem("d_in_x")
    in_acc = [sem(f"d_in_acc{i}") for i in range(2)]
    chain, cs_ready, cs_read = sem("d_chain"), sem("cs_ready"), sem("cs_read")
    t_full, t_done, o_full, o_done = sem("d_t_full"), sem("d_t_done"), sem("d_o_full"), sem("d_o_done")

    with nc.Block() as block:
        @block.sync
        def _(sp):
            with sp.Fori(0, B // 2) as j:
                for u in range(2):
                    b = 2 * j + u
                    sp.wait_ge(cs_read, b + 1)
                    sp.dma_start(acc[u][:].rearrange("p h s w -> p h (s w)"),
                                 t["acc_scr"][bass.ds(b * H0, H0)].rearrange("h p s w -> p h (s w)")
                                 ).then_inc(in_acc[u], 16)

        @block.vector
        def _(dve):
            def combine(b, u, j):
                dve.wait_ge(in_acc[u], 16 * j + 16)
                dve.wait_ge(t_full, 4 * b + 1)
                nc.vector.reciprocal(rec[:], acc[u][:, :, :, 2 * DC]).then_inc(chain, 1)
                nc.vector.tensor_tensor(cs[u][:].rearrange("p s h d -> p h s d"), acc[u][:, :, :, 0:DC],
                                        acc[u][:, :, :, DC:2 * DC], ALU.add).then_inc(chain, 1)
                dve.wait_ge(chain, 4 * b + 2)
                dve.sem_inc(cs_read, 1)
                nc.vector.tensor_scalar(rec[:], rec[:], keep["k_unscale"][:, 0:1], None,
                                        ALU.mult).then_inc(chain, 1)
                dve.wait_ge(chain, 4 * b + 3)
                nc.vector.tensor_tensor(cs[u][:].rearrange("p s h d -> p h s d"),
                                        cs[u][:].rearrange("p s h d -> p h s d"),
                                        rec[:].unsqueeze(3).broadcast_to([P, H0, ST, DC]),
                                        ALU.mult).then_inc(chain, 1)
                dve.wait_ge(chain, 4 * b + 4)
                dve.sem_inc(cs_ready, 1)

            def add_rows(b):
                for s in range(ST):
                    dve.wait_ge(o_full, 2 * b + s + 3)
                    xt = x[:, bass.ds(2 * b + s, 1), :].rearrange("p o d -> p (o d)")
                    nc.vector.tensor_tensor(xt, xt, psO[s][:, 0:D], ALU.add).then_inc(o_done, 1)

            dve.sem_inc(cs_read, 2)
            dve.sem_inc(o_done, 2)
            combine(0, 0, 0)
            dve.wait_ge(in_x, 16)
            with dve.Fori(0, B // 2 - 1) as j:
                combine(2 * j + 1, 1, j)
                add_rows(2 * j)
                combine(2 * j + 2, 0, j + 1)
                add_rows(2 * j + 1)
            combine(B - 1, 1, B // 2 - 1)
            add_rows(B - 2)
            add_rows(B - 1)

        @block.tensor
        def _(pe):
            pe.wait_ge(in_c, 32)
            pe.sem_inc(t_full, 8)
            pe.sem_inc(o_full, 2)
            with pe.Fori(0, B // 2) as j:
                for u in range(2):
                    b = 2 * j + u
                    pe.wait_ge(cs_ready, b + 1)
                    for s in range(ST):
                        for half in range(2):
                            pe.wait_ge(t_done, 4 * b + 2 * s + half + 1)
                            for g in range(4):
                                h = 2 * (4 * half + g)
                                mm = pe.transpose(psT[2 * s + half][:, g * P:(g + 1) * P],
                                                  cs[u][:, s, h:h + 2, :].rearrange("p h d -> p (h d)"), ident[:])
                            mm.then_inc(t_full, 1)
                    for s in range(ST):
                        pe.wait_ge(t_done, 4 * b + 2 * s + 6)
                        pe.wait_ge(o_done, 2 * b + s + 1)
                        for g in range(G):
                            mm = pe.matmul(psO[s][:, 0:D], cT[s][:, g, :], wvo[:, g, :],
                                           start=(g == 0), stop=(g == G - 1))
                        mm.then_inc(o_full, 1)

        @block.scalar
        def _(act):
            act.dma_start(ident[:], t["ident"]).then_inc(in_c, 16)
            act.dma_start(wvo[:], t["wvo_scr"]).then_inc(in_c, 16)
            act.dma_start(x[:], t["x"].rearrange("b (s p) d -> p (b s) d", p=P)).then_inc(in_x, 16)
            act.sem_inc(t_done, 4)
            with act.Fori(0, B // 2) as j:
                for u in range(2):
                    b = 2 * j + u
                    for s in range(ST):
                        for half in range(2):
                            act.wait_ge(t_full, 4 * b + 2 * s + half + 9)
                            if half == 0:
                                act.wait_ge(o_full, 2 * b + s + 1)
                            nc.scalar.activation(
                                cT[s][:, 4 * half:4 * half + 4, :].rearrange("p g c -> p (g c)"),
                                psT[2 * s + half][:], ACT.Copy).then_inc(t_done, 1)


def phase_norm(nc, ctx, t, x, xn, xT, tag):
    def sb(name, shape, dt=F32):
        return ctx.enter_context(nc.sbuf_tensor(tag + name, shape, dt))

    def sem(name):
        return new_semaphore(nc, tag + name)

    ident = sb("ident", [P, P])
    stats = sb("stats", [P, NT, 6])
    agg = sb("agg", [P, NT, 2])
    root = sb("root", [P, NT])
    rstd = sb("rstd", [P, NT])
    tmp = sb("tmp", [P, NT])
    eps = sb("eps", [P, 1])
    ps = [ctx.enter_context(nc.psum_tensor(f"{tag}ps{i}", [P, 512], F32)) for i in range(8)]
    in_c, chain, var_ready, root_ready = sem("in_c"), sem("chain"), sem("var"), sem("root_ready")
    xn_ready, full, done = sem("xn_ready"), sem("full"), sem("done")

    with nc.Block() as block:
        @block.sync
        def _(sp):
            sp.dma_start(ident[:], t["ident"]).then_inc(in_c, 16)

        @block.vector
        def _(dve):
            count = [0]

            def link(ins):
                count[0] += 1
                ins.then_inc(chain, 1)
                dve.wait_ge(chain, count[0])

            link(nc.vector.memset(eps[:], EPS))
            layer_norm_stats(dve, nc, link, x, stats, agg, NT)
            dve.sem_inc(var_ready, 1)
            dve.wait_ge(root_ready, 1)
            rstd_refined(nc, link, rstd[:], root[:], agg, tmp[:])
            for j in range(NT):
                nc.vector.tensor_scalar(xn[:, j, :], x[:, j, :], agg[:, j, 0:1], rstd[:, j:j + 1],
                                        ALU.subtract, ALU.mult).then_inc(xn_ready, 1)

        @block.tensor
        def _(pe):
            pe.wait_ge(in_c, 16)
            for g in range(NT // 2):
                pe.wait_ge(xn_ready, 2 * g + 2)
                for c in range(DK):
                    for u in range(2):
                        mm = pe.transpose(ps[g][:, c * 256 + u * P:c * 256 + (u + 1) * P],
                                          xn[:, 2 * g + u, c * P:(c + 1) * P], ident[:])
                mm.then_inc(full, 1)

        @block.scalar
        def _(act):
            act.wait_ge(var_ready, 1)
            nc.scalar.activation(root[:], agg[:, :, 1], ACT.Sqrt, bias=eps[:, 0:1]).then_inc(root_ready, 1)
            for g in range(NT // 2):
                act.wait_ge(full, g + 1)
                nc.scalar.activation(xT[:, :, 256 * g:256 * (g + 1)],
                                     ps[g][:].rearrange("p (c s) -> p c s", c=DK), ACT.Copy).then_inc(done, 1)


CAP = 64
DFF = 1024
FT = DFF // P
NSEL = B * CAP
SEL_T = NSEL // P
OUT_OF_RANGE = 16384.0


def phase_ffn0(nc, ctx, t, x, xn, xT):
    def sb(name, shape, dt=F32):
        return ctx.enter_context(nc.sbuf_tensor("e_" + name, shape, dt))

    def sem(name):
        return new_semaphore(nc, "e_" + name)

    ident = sb("ident", [P, P])
    upper = sb("upper", [P, P], BF16)
    onesb = sb("ones", [P, P], BF16)
    wr = sb("wr", [P, DK])
    wrb = sb("wrb", [P, DK, P])
    onesf = sb("onesf", [P, P])
    br = sb("br", [P, 1])
    b1 = sb("b1", [P, FT])
    b2 = sb("b2", [P, D])
    w1 = sb("w1", [P, DK, DFF])
    w2 = sb("w2", [P, FT, D])
    rows = sb("rows", [P, NT * P])
    diag = sb("diag", [P, NT, P])
    wcol = sb("wcol", [P, NT])
    ge = sb("ge", [P, S])
    cnt = sb("cnt", [P, NT])
    sel = sb("sel", [P, NT])
    selb = sb("selb", [P, NT], BF16)
    slot = sb("slot", [P, NT])
    base = sb("base", [P, NT])
    s_idx = sb("s_idx", [P, NT], U32)
    g_idx = sb("g_idx", [P, NT], U32)
    gate = sb("gate", [P, NT])
    left = sb("left", [P, NT])
    zero = sb("zero", [P, SEL_T, D])
    xg = sb("xg", [P, SEL_T, D])
    xgT = sb("xgT", [P, DK, NSEL])
    hT = sb("hT", [P, FT, NSEL])
    y = sb("y", [P, SEL_T, D])
    back = sb("back", [P, NT, D])
    ps = [ctx.enter_context(nc.psum_tensor(f"e_ps{i}", [P, 512], F32)) for i in range(8)]
    in_c, in_w, in_z = sem("in_c"), sem("in_w"), sem("in_z")
    made, wrb_made, chain = sem("made"), sem("wrb_made"), sem("chain")
    r_full, r_done, sel_ready, cum_full, idx_ready = (sem("r_full"), sem("r_done"), sem("sel_ready"),
                                                      sem("cum_full"), sem("idx_ready"))
    scattered, in_xg, t_full, t_done = sem("scattered"), sem("in_xg"), sem("t_full"), sem("t_done")
    h_full, h_done, y_full, y_done = sem("h_full"), sem("h_done"), sem("y_full"), sem("y_done")
    stored, gathered = sem("stored"), sem("gathered")
    NB = NT * P // 512

    with nc.Block() as block:
        @block.sync
        def _(sp):
            sp.dma_start(ident[:], t["ident"]).then_inc(in_c, 16)
            sp.dma_start(upper[:], t["upper"]).then_inc(in_c, 16)
            sp.dma_start(base[:], t["cap_base"]).then_inc(in_c, 16)
            sp.dma_start(wr[:], t["L0_ffn_W_r"].rearrange("(c d) o -> d (c o)", d=P),
                         allow_slow_non_contiguous=True).then_inc(in_c, 16)
            sp.dma_start(br[:], t["L0_ffn_b_r"].partition_broadcast(P)).then_inc(in_c, 16)
            sp.dma_start(b1[:], t["L0_ffn_b1"].rearrange("(f p) -> p f", p=P),
                         allow_slow_non_contiguous=True).then_inc(in_w, 16)
            sp.dma_start(b2[:], t["L0_ffn_b2"].partition_broadcast(P)).then_inc(in_w, 16)
            sp.dma_start(w1[:], t["L0_ffn_W1"].rearrange("(c d) f -> d c f", d=P)).then_inc(in_w, 16)
            sp.dma_start(w2[:], t["L0_ffn_W2"].rearrange("(f p) d -> p f d", p=P)).then_inc(in_w, 16)
            sp.wait_ge(made, 1)
            sp.dma_start(t["xg_scr"].rearrange("(t p) d -> p t d", p=P), zero[:]).then_inc(in_z, 16)
            sp.wait_ge(scattered, 16 * NT)
            sp.dma_start(xg[:], t["xg_scr"].rearrange("(t p) d -> p t d", p=P)).then_inc(in_xg, 16)
            sp.wait_ge(y_done, SEL_T)
            sp.dma_start(t["y_scr"].rearrange("(t p) d -> p t d", p=P), y[:]).then_inc(stored, 16)
            sp.wait_ge(stored, 16)

        @block.gpsimd
        def _(pool):
            nc.gpsimd.memset(zero[:], 0.0).then_inc(made, 1)
            pool.wait_ge(in_z, 16)
            pool.wait_ge(idx_ready, 1)
            for j in range(NT):
                nc.gpsimd.indirect_dma_start(
                    out=t["xg_scr"], out_offset=bass.IndirectOffsetOnAxis(ap=s_idx[:, j:j + 1], axis=0),
                    in_=xn[:, j, :], in_offset=None, bounds_check=NSEL - 1, oob_is_err=False
                ).then_inc(scattered, 16)
            pool.wait_ge(stored, 16)
            for j in range(NT):
                nc.gpsimd.indirect_dma_start(
                    out=back[:, j, :], out_offset=None, in_=t["y_scr"],
                    in_offset=bass.IndirectOffsetOnAxis(ap=g_idx[:, j:j + 1], axis=0),
                    bounds_check=NSEL - 1, oob_is_err=False).then_inc(gathered, 16)
            pool.wait_ge(gathered, 16 * NT)

        @block.vector
        def _(dve):
            count = [0]

            def link(ins):
                count[0] += 1
                ins.then_inc(chain, 1)
                dve.wait_ge(chain, count[0])

            link(nc.vector.memset(onesf[:], 1.0))
            link(nc.vector.memset(onesb[:], 1.0))
            dve.wait_ge(in_c, 80)
            for c in range(DK):
                link(nc.vector.tensor_scalar(wrb[:, c, :], onesf[:], wr[:, c:c + 1], None, ALU.mult))
            dve.sem_inc(wrb_made, 1)
            for k in range(NB):
                dve.wait_ge(r_full, k + 1)
                nc.vector.tensor_scalar(rows[:, k * 512:(k + 1) * 512], ps[k][:], br[:, 0:1], None,
                                        ALU.add).then_inc(r_done, 1)
            dve.wait_ge(r_done, NB)
            link(nc.vector.tensor_tensor(diag[:], rows[:].rearrange("p (t q) -> p t q", t=NT),
                                         ident[:].unsqueeze(1).broadcast_to([P, NT, P]), ALU.mult))
            link(nc.vector.tensor_reduce(wcol[:], diag[:], AX.X, ALU.add))
            for j in range(NT):
                b = j // ST
                link(nc.vector.tensor_scalar(ge[:], rows[:, b * S:(b + 1) * S], wcol[:, j:j + 1], None,
                                             ALU.is_ge))
                link(nc.vector.tensor_reduce(cnt[:, j:j + 1], ge[:], AX.X, ALU.add))
            link(nc.vector.tensor_scalar(sel[:], cnt[:], CAP - 0.5, None, ALU.is_lt))
            nc.vector.tensor_copy(selb[:], sel[:]).then_inc(sel_ready, 1)
            dve.wait_ge(cum_full, 1)
            link(nc.vector.tensor_tensor(slot[:], ps[4][:, 0:NT], base[:], ALU.add))
            link(nc.vector.tensor_tensor(slot[:], slot[:], sel[:], ALU.mult))
            link(nc.vector.tensor_copy(g_idx[:], slot[:]))
            link(nc.vector.tensor_scalar(left[:], sel[:], -1.0, 1.0, ALU.mult, ALU.add))
            link(nc.vector.scalar_tensor_tensor(out=slot[:], in0=left[:], scalar=OUT_OF_RANGE, in1=slot[:],
                                                op0=ALU.mult, op1=ALU.add))
            nc.vector.tensor_copy(s_idx[:], slot[:]).then_inc(idx_ready, 1)
            link(nc.vector.tensor_tensor(gate[:], wcol[:], sel[:], ALU.mult))
            for k in range(2):
                dve.wait_ge(t_full, k + 1)
                nc.vector.tensor_copy(xgT[:, :, 256 * k:256 * (k + 1)],
                                      ps[k][:].rearrange("p (c s) -> p c s", c=DK)).then_inc(t_done, 1)
            for k in range(SEL_T):
                dve.wait_ge(y_full, k + 1)
                nc.vector.tensor_tensor(y[:, k, :], ps[k][:, 0:D], b2[:], ALU.add).then_inc(y_done, 1)
            for j in range(NT):
                link(nc.vector.scalar_tensor_tensor(out=x[:, j, :], in0=xn[:, j, :], scalar=left[:, j:j + 1],
                                                    in1=x[:, j, :], op0=ALU.mult, op1=ALU.add))
            dve.wait_ge(gathered, 16 * NT)
            for j in range(NT):
                link(nc.vector.scalar_tensor_tensor(out=x[:, j, :], in0=back[:, j, :], scalar=gate[:, j:j + 1],
                                                    in1=x[:, j, :], op0=ALU.mult, op1=ALU.add))

        @block.tensor
        def _(pe):
            pe.wait_ge(wrb_made, 1)
            for k in range(NB):
                for c in range(DK):
                    mm = pe.matmul(ps[k][:], wrb[:, c, :], xT[:, c, k * 512:(k + 1) * 512],
                                   start=(c == 0), stop=(c == DK - 1))
                mm.then_inc(r_full, 1)
            pe.wait_ge(in_c, 80)
            pe.wait_ge(sel_ready, 1)
            pe.matmul(ps[4][:, 0:NT:2], upper[:], selb[:, 0:NT:2], start=True, stop=True)
            pe.matmul(ps[4][:, 1:NT:2], upper[:], selb[:, 1:NT:2], start=True, stop=False)
            pe.matmul(ps[4][:, 1:NT:2], onesb[:], selb[:, 0:NT:2], start=False,
                      stop=True).then_inc(cum_full, 1)
            pe.wait_ge(in_xg, 16)
            for k in range(2):
                for c in range(DK):
                    for u in range(2):
                        mm = pe.transpose(ps[k][:, c * 256 + u * P:c * 256 + (u + 1) * P],
                                          xg[:, 2 * k + u, c * P:(c + 1) * P], ident[:])
                mm.then_inc(t_full, 1)
            pe.wait_ge(in_w, 64)
            pe.wait_ge(t_done, 2)
            for f in range(FT):
                if f >= 4:
                    pe.wait_ge(h_done, f - 3)
                for c in range(DK):
                    mm = pe.matmul(ps[4 + f % 4][:], w1[:, c, f * P:(f + 1) * P], xgT[:, c, :],
                                   start=(c == 0), stop=(c == DK - 1))
                mm.then_inc(h_full, 1)
            for k in range(SEL_T):
                pe.wait_ge(h_done, FT)
                for f in range(FT):
                    mm = pe.matmul(ps[k][:, 0:D], hT[:, f, k * P:(k + 1) * P], w2[:, f, :],
                                   start=(f == 0), stop=(f == FT - 1))
                mm.then_inc(y_full, 1)

        @block.scalar
        def _(act):
            act.wait_ge(in_w, 64)
            for f in range(FT):
                act.wait_ge(h_full, f + 1)
                nc.scalar.activation(hT[:, f, :], ps[4 + f % 4][:], ACT.Gelu_apprx_tanh,
                                     bias=b1[:, f:f + 1]).then_inc(h_done, 1)


H1, HD = 16, 16
SCALE1 = 1.0 / float(np.sqrt(HD))
NH = P // HD
HH = H1 // NH
VROW = P + HD
MASKED = -3.0e38


def phase_qkv1(nc, ctx, t, xT, qT, kT, v):
    def sb(name, shape, dt=F32):
        return ctx.enter_context(nc.sbuf_tensor("f_" + name, shape, dt))

    def sem(name):
        return new_semaphore(nc, "f_" + name)

    ident = sb("ident", [P, P])
    wq = sb("wq", [P, DK, D])
    wkv = sb("wkv", [P, 2 * DK, DC])
    c = sb("c", [P, NT, DC])
    wqT = sb("wqT", [P, DK, D])
    wkvT = sb("wkvT", [DC, 2 * D])
    cT = sb("cT", [DC, NT * P])
    psA = [ctx.enter_context(nc.psum_tensor(f"f_psA{i}", [P, 512], F32)) for i in range(4)]
    psD = [ctx.enter_context(nc.psum_tensor(f"f_psD{i}", [P, 512], F32)) for i in range(4)]
    in_c = sem("in_c")
    a_full, a_done, d_full, d_done = sem("a_full"), sem("a_done"), sem("d_full"), sem("d_done")
    NQ = B * S // 512

    with nc.Block() as block:
        @block.sync
        def _(sp):
            sp.dma_start(ident[:], t["ident"]).then_inc(in_c, 16)
            sp.dma_start(wq[:], t["L1_xattn_Wq"].rearrange("(c e) d -> e c d", e=P)).then_inc(in_c, 16)
            sp.dma_start(wkv[:], t["L1_xattn_Wkv_expand"].rearrange("(c e) d -> e c d", e=P)).then_inc(in_c, 16)
            for b in range(B):
                sp.dma_start(c[:, b * ST:(b + 1) * ST, :],
                             t["ctx_512"][b, 0:S, :].rearrange("(s p) d -> p s d", p=P)).then_inc(in_c, 16)

        @block.tensor
        def _(pe):
            pe.wait_ge(in_c, 16 * (3 + B))
            for dk in range(DK):
                for ec in range(DK):
                    mm = pe.transpose(psA[0][:, dk * D + ec * P:dk * D + (ec + 1) * P],
                                      wq[:, ec, dk * P:(dk + 1) * P], ident[:])
            mm.then_inc(a_full, 1)
            for ec in range(2 * DK):
                mm = pe.transpose(psA[1][0:DC, ec * P:(ec + 1) * P], wkv[:, ec, :], ident[:])
            mm.then_inc(a_full, 1)
            for g in range(NQ):
                n = 2 + g
                if n >= 4:
                    pe.wait_ge(a_done, n - 3)
                for i in range(4):
                    mm = pe.transpose(psA[n % 4][0:DC, i * P:(i + 1) * P], c[:, 4 * g + i, :], ident[:])
                mm.then_inc(a_full, 1)
            pe.wait_ge(a_done, 1)
            for e in range(DK):
                for g in range(NQ):
                    n = e * NQ + g
                    if n >= 4:
                        pe.wait_ge(d_done, n - 3)
                    for dk in range(DK):
                        mm = pe.matmul(psD[n % 4][:], wqT[:, dk, e * P:(e + 1) * P],
                                       xT[:, dk, g * 512:(g + 1) * 512], start=(dk == 0), stop=(dk == DK - 1))
                    mm.then_inc(d_full, 1)
            for e in range(DK):
                for g in range(NQ):
                    n = 2 + NQ + e * NQ + g
                    pe.wait_ge(a_done, max(n - 3, 2 + NQ))
                    pe.matmul(psA[n % 4][:], wkvT[:, e * P:(e + 1) * P], cT[:, g * 512:(g + 1) * 512],
                              start=True, stop=True).then_inc(a_full, 1)
            for g in range(NT // 2):
                n = 2 * NQ + g
                pe.wait_ge(d_done, n - 3)
                for u in range(2):
                    i = 2 * g + u
                    mm = pe.matmul(psD[n % 4][:, u * D:(u + 1) * D], cT[:, i * P:(i + 1) * P],
                                   wkvT[:, D:2 * D], start=True, stop=True)
                mm.then_inc(d_full, 1)

        @block.scalar
        def _(act):
            act.wait_ge(a_full, 1)
            nc.scalar.activation(wqT[:].rearrange("p c e -> p (c e)"), psA[0][:], ACT.Copy).then_inc(a_done, 1)
            act.wait_ge(a_full, 2)
            nc.scalar.activation(wkvT[:], psA[1][0:DC, :], ACT.Copy).then_inc(a_done, 1)
            for g in range(NQ):
                act.wait_ge(a_full, 3 + g)
                nc.scalar.activation(cT[:, g * 512:(g + 1) * 512], psA[(2 + g) % 4][0:DC, :],
                                     ACT.Copy).then_inc(a_done, 1)
            for e in range(DK):
                for g in range(NQ):
                    n = 2 + NQ + e * NQ + g
                    act.wait_ge(a_full, n + 1)
                    nc.scalar.activation(kT[:, e, g * 512:(g + 1) * 512], psA[n % 4][:],
                                         ACT.Copy).then_inc(a_done, 1)

        @block.vector
        def _(dve):
            for e in range(DK):
                for g in range(NQ):
                    n = e * NQ + g
                    dve.wait_ge(d_full, n + 1)
                    nc.vector.tensor_copy(qT[:, e, g * 512:(g + 1) * 512], psD[n % 4][:]).then_inc(d_done, 1)
            for g in range(NT // 2):
                n = 2 * NQ + g
                dve.wait_ge(d_full, n + 1)
                nc.vector.tensor_copy(v[:, 2 * g:2 * g + 2, :].rearrange("p g e -> p (g e)"),
                                      psD[n % 4][:]).then_inc(d_done, 1)


def phase_attention1(nc, ctx, t, x, qT, kT, v):
    def sb(name, shape, dt=F32):
        return ctx.enter_context(nc.sbuf_tensor("g_" + name, shape, dt))

    def sem(name):
        return new_semaphore(nc, "g_" + name)

    ident = sb("ident", [P, P])
    identb = sb("identb", [P, P], BF16)
    causal = sb("causal", [P, P], BF16)
    hmask = sb("hmask", [P, NH])
    wo = sb("wo", [P, DK, D])
    woT = sb("woT", [P, DK, D])
    q = [sb(f"q{i}", [P, HH, S]) for i in range(2)]
    km = [sb(f"km{i}", [P, HH, NH, S]) for i in range(2)]
    vm = [sb(f"vm{i}", [P, ST * HH, NH * VROW]) for i in range(2)]
    prob = [sb(f"prob{i}", [P, 1024]) for i in range(2)]
    pT = [sb(f"pT{i}", [P, 1024]) for i in range(2)]
    mx = [sb(f"mx{i}", [P, NH]) for i in range(2)]
    bias = [sb(f"bias{i}", [P, NH]) for i in range(2)]
    sums = sb("sums", [P, HH, ST * NH])
    rec = sb("rec", [P, ST * NH])
    recx = sb("recx", [P, ST, NH, HD])
    rT = sb("rT", [P, S])
    oT = [sb(f"oT{i}", [P, S]) for i in range(HH)]
    psS = [ctx.enter_context(nc.psum_tensor(f"g_psS{i}", [P, 1024], F32)) for i in range(2)]
    psT = ctx.enter_context(nc.psum_tensor("g_psT", [P, 1024], F32))
    psO = ctx.enter_context(nc.psum_tensor("g_psO", [P, 512], F32))
    psX = ctx.enter_context(nc.psum_tensor("g_psX", [P, 512], F32))

    in_c, wo_full, wo_done = sem("in_c"), sem("wo_full"), sem("wo_done")
    zeroed, q_ready, km_ready, vm_ready = sem("zeroed"), sem("q_ready"), sem("km_ready"), sem("vm_ready")
    s_full = sem("s_full")
    mx_done, bias_ready = sem("mx_done"), sem("bias_ready")
    exp_done = sem("exp_done")
    t_full = sem("t_full")
    pt_done = sem("pt_done")
    pv_done = sem("pv_done")
    r_chain, r_ready, r_full = sem("r_chain"), sem("r_ready"), sem("r_full")
    r_copied = sem("r_copied")
    o_done = sem("o_done")
    p_full = sem("p_full")
    p_done = sem("p_done")
    UNITS = 3 * HH

    def heads(k):
        kind = k % 3
        return ((0, NH), P, 0) if kind == 0 else ((4 * (kind - 1), 4 * kind), S, 1)

    def nxt(b):
        return (b + 1) % B

    with nc.Block() as block:
        @block.sync
        def _(sp):
            sp.dma_start(ident[:], t["ident"]).then_inc(in_c, 16)
            sp.dma_start(identb[:], t["identb"]).then_inc(in_c, 16)
            sp.dma_start(causal[:], t["causal"]).then_inc(in_c, 16)
            sp.dma_start(hmask[:], t["hmask"]).then_inc(in_c, 16)
            sp.dma_start(wo[:], t["L1_xattn_Wout"].rearrange("(c e) d -> e c d", e=P)).then_inc(in_c, 16)

        @block.gpsimd
        def _(pool):
            def keys(b, u):
                for hh in range(HH):
                    ins = nc.gpsimd.tensor_tensor(
                        km[u][:, hh], kT[:, hh:hh + 1, bass.ds(b * S, S)].broadcast_to([P, NH, S]),
                        hmask[:].unsqueeze(2).broadcast_to([P, NH, S]), ALU.mult)
                ins.then_inc(km_ready, 1)

            def values(b, u):
                nc.gpsimd.tensor_copy(
                    vm[u][:].rearrange("p a (h w) -> p a h w", w=VROW)[:, :, :, 0:HD],
                    v[:, bass.ds(b * ST, ST), :].rearrange("p s (a h w) -> p (s a) h w", a=HH, h=NH)
                ).then_inc(vm_ready, 1)

            for u in range(2):
                nc.gpsimd.memset(vm[u][:], 0.0).then_inc(zeroed, 1)
            pool.wait_ge(zeroed, 2)
            pool.wait_ge(in_c, 80)
            keys(0, 0)
            values(0, 0)
            with pool.Fori(0, B // 2) as j:
                for u in range(2):
                    b = 2 * j + u
                    pool.wait_ge(s_full, UNITS * b + 1)
                    keys(nxt(b), 1 - u)
                    pool.wait_ge(pv_done, UNITS * b + 2)
                    values(nxt(b), 1 - u)

        @block.tensor
        def _(pe):
            def scores(b_count, k, u):
                (h0, h1), w, st = heads(k)
                hh = k // 3
                slot = psS[k % 2]
                if k == 0:
                    pe.wait_ge(q_ready, b_count + 1)
                    pe.wait_ge(km_ready, b_count + 1)
                per = 512 // w
                for half in range(2):
                    ha = h0 + half * per
                    bank = slot[:, half * 512:(half + 1) * 512]
                    pe.matmul(bank, q[u][:, hh, st * P:(st + 1) * P],
                              km[u][:, hh, ha:ha + per, 0:w], start=True, stop=True)
                    diag = bank.rearrange("p (h k) -> p h k", h=per)[:, :, w - P:w]
                    mm = pe.matmul(diag, identb[:], causal[:].unsqueeze(1).broadcast_to([P, per, P]),
                                   start=False, stop=True, skip_group_check=True)
                mm.then_inc(s_full, 1)

            def transposes(b, k):
                n = UNITS * b + k
                pe.wait_ge(exp_done, n + 2)
                pe.wait_ge(pt_done, n + 1)
                for i in range(8):
                    mm = pe.transpose(psT[:, i * P:(i + 1) * P], prob[k % 2][:, i * P:(i + 1) * P], ident[:])
                mm.then_inc(t_full, 1)

            def values(b, k, u):
                (h0, h1), w, st = heads(k)
                hh = k // 3
                n = UNITS * b + k
                pe.wait_ge(pt_done, n + 2)
                if k % 3 == 0:
                    pe.wait_ge(o_done, HH * b + hh + 1)
                    if hh == 0:
                        pe.wait_ge(vm_ready, b + 1)
                i = 0
                for h in range(h0, h1):
                    for kt in range(w // P):
                        mm = pe.matmul(psO[:, st * P:(st + 1) * P],
                                       vm[u][:, kt * HH + hh, h * P:(h + 1) * P],
                                       pT[k % 2][:, i * P:(i + 1) * P],
                                       start=(k % 3 == 0 and i == 0),
                                       stop=(k % 3 != 1 and i == 7), skip_group_check=True)
                        i += 1
                mm.then_inc(pv_done, 1)

            def reciprocals(b, hh):
                n = HH * b + hh
                pe.wait_ge(r_ready, n + 1)
                pe.wait_ge(r_copied, n + 1)
                pe.wait_ge(p_done, ST * b + 1)
                for st in range(ST):
                    mm = pe.transpose(psX[:, st * P:(st + 1) * P],
                                      recx[:, st].rearrange("p h w -> p (h w)"), ident[:])
                mm.then_inc(r_full, 1)

            def project(b):
                pe.wait_ge(o_done, HH * b + HH + 1)
                for st in range(ST):
                    pe.wait_ge(p_done, ST * b + st + 1)
                    for hh in range(HH):
                        mm = pe.matmul(psX[:, D:2 * D], oT[hh][:, st * P:(st + 1) * P], woT[:, hh, :],
                                       start=(hh == 0), stop=(hh == HH - 1))
                    mm.then_inc(p_full, 1)

            pe.wait_ge(in_c, 80)
            for dk in range(DK):
                for ec in range(DK):
                    mm = pe.transpose(psX[:, dk * D + ec * P:dk * D + (ec + 1) * P],
                                      wo[:, ec, dk * P:(dk + 1) * P], ident[:])
            mm.then_inc(wo_full, 1)
            pe.sem_inc(t_full, 1)
            pe.sem_inc(pv_done, 2)
            pe.wait_ge(wo_done, 1)
            scores(0, 0, 0)
            with pe.Fori(0, B // 2) as j:
                for u in range(2):
                    b = 2 * j + u
                    for k in range(UNITS):
                        pe.wait_ge(exp_done, UNITS * b + k + 1)
                        if k < UNITS - 1:
                            scores(b, k + 1, u)
                        else:
                            scores(b + 1, 0, 1 - u)
                        transposes(b, k)
                        if k >= 1:
                            values(b, k - 1, u)
                        if k == 3:
                            reciprocals(b, 0)
                    values(b, UNITS - 1, u)
                    reciprocals(b, 1)
                    project(b)

        @block.scalar
        def _(act):
            def exps(b, k):
                (h0, h1), w, st = heads(k)
                hh = k // 3
                n = UNITS * b + k
                act.wait_ge(bias_ready, n + 1)
                if not isinstance(n, int):
                    act.wait_ge(t_full, n)
                for h in range(h0, h1):
                    i = h - h0
                    ins = nc.scalar.activation(prob[k % 2][:, i * w:(i + 1) * w], psS[k % 2][:, i * w:(i + 1) * w],
                                               ACT.Exp, bias=bias[k % 2][:, i:i + 1], scale=SCALE1,
                                               accum_out=sums[:, hh, st * NH + h:st * NH + h + 1])
                ins.then_inc(exp_done, 1)

            def copy_r(b, hh):
                n = HH * b + hh
                act.wait_ge(r_full, n + 1)
                act.wait_ge(o_done, n + 1)
                nc.scalar.activation(rT[:], psX[:, 0:S], ACT.Copy).then_inc(r_copied, 1)

            act.sem_inc(exp_done, 1)
            act.sem_inc(r_copied, 1)
            exps(0, 0)
            with act.Fori(0, B // 2) as j:
                for u in range(2):
                    b = 2 * j + u
                    for k in range(UNITS):
                        if k < UNITS - 1:
                            exps(b, k + 1)
                        else:
                            exps(b + 1, 0)
                        if k == 3:
                            copy_r(b, 0)
                    copy_r(b, 1)

        @block.vector
        def _(dve):
            def maxima(b, k):
                (h0, h1), w, st = heads(k)
                n = UNITS * b + k
                dve.wait_ge(s_full, n + 1)
                nh = h1 - h0
                nc.vector.tensor_reduce(mx[k % 2][:, 0:nh], psS[k % 2][:].rearrange("p (h k) -> p h k", h=nh),
                                        AX.X, ALU.max).then_inc(mx_done, 1)
                dve.wait_ge(mx_done, n + 1)
                nc.vector.tensor_scalar(bias[k % 2][:, 0:nh], mx[k % 2][:, 0:nh], -SCALE1, None,
                                        ALU.mult).then_inc(bias_ready, 1)

            def drain_t(b, k):
                n = UNITS * b + k
                dve.wait_ge(t_full, n + 2)
                dve.wait_ge(pv_done, n + 1)
                nc.vector.tensor_copy(pT[k % 2][:], psT[:]).then_inc(pt_done, 1)

            def reciprocals(b, hh):
                n = HH * b + hh
                dve.wait_ge(exp_done, UNITS * b + 3 * hh + 4)
                nc.vector.reciprocal(rec[:], sums[:, hh, :]).then_inc(r_chain, 1)
                dve.wait_ge(r_chain, n + 1)
                nc.vector.tensor_copy(recx[:].rearrange("p s h w -> p (s h) w"),
                                      rec[:].unsqueeze(2).broadcast_to([P, ST * NH, HD])).then_inc(r_ready, 1)

            def normalise(b, hh):
                n = HH * b + hh
                dve.wait_ge(r_copied, n + 2)
                dve.wait_ge(pv_done, UNITS * b + 3 * hh + 5)
                nc.vector.tensor_tensor(oT[hh][:], psO[:, 0:S], rT[:], ALU.mult).then_inc(o_done, 1)

            def add(b):
                for st in range(ST):
                    dve.wait_ge(p_full, ST * b + st + 1)
                    xt = x[:, bass.ds(b * ST + st, 1), :].rearrange("p o d -> p (o d)")
                    nc.vector.tensor_tensor(xt, xt, psX[:, D:2 * D], ALU.add).then_inc(p_done, 1)

            def queries(b, u):
                nc.vector.tensor_copy(q[u][:], qT[:, :, bass.ds(b * S, S)]).then_inc(q_ready, 1)

            dve.wait_ge(wo_full, 1)
            nc.vector.tensor_copy(woT[:].rearrange("p c e -> p (c e)"), psX[:]).then_inc(wo_done, 1)
            dve.sem_inc(pt_done, 1)
            dve.sem_inc(o_done, 1)
            dve.sem_inc(p_done, 1)
            queries(0, 0)
            maxima(0, 0)
            with dve.Fori(0, B // 2) as j:
                for u in range(2):
                    b = 2 * j + u
                    dve.wait_ge(s_full, UNITS * b + 1)
                    queries(nxt(b), 1 - u)
                    for k in range(UNITS):
                        if k < UNITS - 1:
                            maxima(b, k + 1)
                        else:
                            maxima(b + 1, 0)
                        drain_t(b, k)
                        if k == 2:
                            reciprocals(b, 0)
                        if k == 3:
                            normalise(b, 0)
                    reciprocals(b, 1)
                    normalise(b, 1)
                    add(b)


E1, HID = 8, 352
CAP1 = B * S // E1
FT1 = [(0, 128), (128, 128), (256, 96)]


def phase_moe(nc, ctx, t, x, xn, xT):
    def sb(name, shape, dt=F32):
        return ctx.enter_context(nc.sbuf_tensor("m_" + name, shape, dt))

    def sem(name):
        return new_semaphore(nc, "m_" + name)

    FTN = len(FT1)
    ident = sb("ident", [P, P])
    upper = sb("upper", [P, P], BF16)
    onesb = sb("ones", [P, P], BF16)
    wg = sb("wg", [P, DK, E1])
    rank = sb("rank", [P, E1])
    ebase = sb("ebase", [P, E1])
    sw1 = sb("sw1", [P, DK, HID])
    sw3 = sb("sw3", [P, DK, HID])
    sw2 = sb("sw2", [P, FTN, D])
    w1 = [sb(f"w1_{i}", [P, DK, HID]) for i in range(2)]
    w3 = [sb(f"w3_{i}", [P, DK, HID]) for i in range(2)]
    w2 = [sb(f"w2_{i}", [P, FTN, D]) for i in range(2)]
    xt = [sb(f"xt{i}", [P, DK, CAP1]) for i in range(2)]
    xd = [sb(f"xd{i}", [P, 2, D]) for i in range(2)]
    act_s = [sb(f"s{i}", [P, FTN, CAP1]) for i in range(2)]
    g = [sb(f"g{i}", [P, FTN, CAP1]) for i in range(2)]
    yo = [sb(f"yo{i}", [P, 2, D]) for i in range(2)]
    zero = sb("zero", [P, NT * D // 4])
    logit = sb("logit", [P, NT, E1])
    top = sb("top", [P, NT])
    ex = sb("ex", [P, NT, E1])
    tot = sb("tot", [P, NT])
    val = sb("val", [P, NT, E1])
    oh = sb("oh", [P, NT, E1])
    ohb = sb("ohb", [P, NT, E1], BF16)
    cum = sb("cum", [P, NT, E1])
    pos = sb("pos", [P, NT])
    ebs = sb("ebs", [P, NT])
    keepm = sb("keepm", [P, NT])
    gate = sb("gate", [P, NT])
    slot = sb("slot", [P, NT])
    s_idx = sb("s_idx", [P, NT], U32)
    g_idx = sb("g_idx", [P, NT], U32)
    back = sb("back", [P, NT, D])
    psR = ctx.enter_context(nc.psum_tensor("m_psR", [P, 512], F32))
    psH = [ctx.enter_context(nc.psum_tensor(f"m_psH{i}", [P, 512], F32)) for i in range(4)]
    psY = [ctx.enter_context(nc.psum_tensor(f"m_psY{i}", [P, 512], F32)) for i in range(2)]

    in_c, in_s, in_z = sem("in_c"), sem("in_s"), sem("in_z")
    in_w = [sem(f"in_w{i}") for i in range(2)]
    in_xd = [sem(f"in_xd{i}") for i in range(2)]
    zeroed, chain, const = sem("zeroed"), sem("chain"), sem("const")
    l_full, l_done, ex_ready = sem("l_full"), sem("l_done"), sem("ex_ready")
    oh_ready, cum_full, idx_ready = sem("oh_ready"), sem("cum_full"), sem("idx_ready")
    scattered, gathered = sem("scattered"), sem("gathered")
    xt_full, xt_done = sem("xt_full"), sem("xt_done")
    h_full, silu_done, g_done = sem("h_full"), sem("silu_done"), sem("g_done")
    y_full, y_done = sem("y_full"), sem("y_done")
    stored = [sem(f"stored{i}") for i in range(2)]
    out_sent = sem("out_sent")
    x_final = sem("x_final")
    NS = B * S // CAP1

    def load_ffn(sp, s, d1, d3, d2, a1, a3, a2):
        sp.dma_start(d1[:], a1.rearrange("(c d) f -> d c f", d=P)).then_inc(s, 16)
        sp.dma_start(d3[:], a3.rearrange("(c d) f -> d c f", d=P)).then_inc(s, 16)
        sp.dma_start(d2[:, 0:2, :], a2[0:256, :].rearrange("(c f) d -> f c d", f=P)).then_inc(s, 16)
        sp.dma_start(d2[0:96, 2, :], a2[256:352, :]).then_inc(s, 16)

    with nc.Block() as block:
        @block.sync
        def _(sp):
            sp.dma_start(ident[:], t["ident"]).then_inc(in_c, 16)
            sp.dma_start(upper[:], t["upper"]).then_inc(in_c, 16)
            sp.dma_start(rank[:], t["rank"]).then_inc(in_c, 16)
            sp.dma_start(ebase[:], t["ebase"]).then_inc(in_c, 16)
            sp.dma_start(wg[:], t["L1_ffn_Wg"].rearrange("(c d) e -> d c e", d=P)).then_inc(in_c, 16)
            load_ffn(sp, in_s, sw1, sw3, sw2, t["L1_ffn_sw1"], t["L1_ffn_sw3"], t["L1_ffn_sw2"])
            sp.wait_ge(zeroed, 1)
            for k in range(4):
                sp.dma_start(t["xd_scr"].rearrange("(k p r) d -> k p (r d)", k=4, p=P)[k],
                             zero[:]).then_inc(in_z, 16)

            def weights(e, u):
                ap = [a[bass.ds(e, 1)].rearrange("o a b -> (o a) b")
                      for a in (t["L1_ffn_W1"], t["L1_ffn_W3"], t["L1_ffn_W2"])]
                load_ffn(sp, in_w[u], w1[u], w3[u], w2[u], *ap)

            for u in range(2):
                sp.sem_inc(stored[u], 16)
            weights(0, 0)
            weights(1, 1)
            sp.wait_ge(scattered, 16 * NT)
            for u in range(2):
                sp.dma_start(xd[u][:], t["xd_scr"][u * CAP1:(u + 1) * CAP1, :].rearrange("(c p) d -> p c d", p=P)
                             ).then_inc(in_xd[u], 16)
            with sp.Fori(0, E1 // 2) as j:
                for u in range(2):
                    e = 2 * j + u
                    sp.wait_ge(y_full, 2 * (NS + e) + 2)
                    weights((e + 2) % E1, u)
                    sp.dma_start(xd[u][:], t["xd_scr"][bass.ds(((e + 2) % E1) * CAP1, CAP1), :]
                                 .rearrange("(c p) d -> p c d", p=P)).then_inc(in_xd[u], 16)
                    sp.wait_ge(y_done, 2 * (NS + e) + 4)
                    sp.dma_start(t["oe_scr"][bass.ds(e * CAP1, CAP1), :].rearrange("(c p) d -> p c d", p=P),
                                 yo[u][:]).then_inc(stored[u], 16)
            for u in range(2):
                sp.wait_ge(in_w[u], 64 * (E1 // 2 + 1))
                sp.wait_ge(in_xd[u], 16 * (E1 // 2 + 1))
                sp.wait_ge(stored[u], 16 + 16 * (E1 // 2))
            for j in range(NT // 4):
                sp.wait_ge(x_final, 4 * j + 4)
                sp.dma_start(t["out"].rearrange("b (s p) d -> p (b s) d", p=P)[:, 4 * j:4 * j + 4, :],
                             x[:, 4 * j:4 * j + 4, :]).then_inc(out_sent, 16)
            sp.wait_ge(out_sent, 16 * (NT // 4))

        @block.gpsimd
        def _(pool):
            nc.gpsimd.memset(zero[:], 0.0).then_inc(zeroed, 1)
            pool.wait_ge(in_z, 64)
            pool.wait_ge(idx_ready, 1)
            for j in range(NT):
                nc.gpsimd.indirect_dma_start(
                    out=t["xd_scr"], out_offset=bass.IndirectOffsetOnAxis(ap=s_idx[:, j:j + 1], axis=0),
                    in_=xn[:, j, :], in_offset=None, bounds_check=E1 * CAP1 - 1, oob_is_err=False
                ).then_inc(scattered, 16)
            for u in range(2):
                pool.wait_ge(stored[u], 16 + 16 * (E1 // 2))
            for j in range(NT):
                nc.gpsimd.indirect_dma_start(
                    out=back[:, j, :], out_offset=None, in_=t["oe_scr"],
                    in_offset=bass.IndirectOffsetOnAxis(ap=g_idx[:, j:j + 1], axis=0),
                    bounds_check=E1 * CAP1 - 1, oob_is_err=False).then_inc(gathered, 16)
            pool.wait_ge(gathered, 16 * NT)

        @block.tensor
        def _(pe):
            def hidden(n, a1, a3, moving):
                for f, (f0, fw) in enumerate(FT1):
                    slot = psH[f]
                    pe.wait_ge(g_done, FTN * n + f + 1)
                    for k, a in enumerate((a1, a3)):
                        for c in range(DK):
                            mm = pe.matmul(slot[0:fw, k * CAP1:(k + 1) * CAP1], a[:, c, f0:f0 + fw],
                                           moving(c), start=(c == 0), stop=(c == DK - 1))
                    mm.then_inc(h_full, 1)

            def down(n, a2, u):
                for r in range(2):
                    if r == 0:
                        pe.wait_ge(g_done, FTN * n + 6)
                    pe.wait_ge(y_done, 2 * n + r + 1)
                    for f, (_, fw) in enumerate(FT1):
                        mm = pe.matmul(psY[r][:, 0:D], g[u][0:fw, f, r * P:(r + 1) * P], a2[0:fw, f, :],
                                       start=(f == 0), stop=(f == FTN - 1))
                    mm.then_inc(y_full, 1)

            pe.wait_ge(in_c, 80)
            for j in range(NT):
                for c in range(DK):
                    mm = pe.matmul(psR[:, j * E1:(j + 1) * E1], xT[:, c, j * P:(j + 1) * P], wg[:, c, :],
                                   start=(c == 0), stop=(c == DK - 1))
            mm.then_inc(l_full, 1)
            pe.wait_ge(in_s, 64)
            for n in range(2):
                hidden(n, sw1, sw3, lambda c: xT[:, c, n * CAP1:(n + 1) * CAP1])
                down(n, sw2, n)
            pe.wait_ge(oh_ready, 1)
            pe.wait_ge(const, 1)
            w = NT * E1
            pe.matmul(psR[:, 0:w], upper[:], ohb[:].rearrange("p t e -> p (t e)"), start=True, stop=True)
            for j in range(NT - 1):
                left = NT - 1 - j
                mm = pe.matmul(psR[:, (j + 1) * E1:w], onesb[:],
                               ohb[:, j:j + 1, :].broadcast_to([P, left, E1]),
                               start=False, stop=True, skip_group_check=True)
            mm.then_inc(cum_full, 1)
            with pe.Fori(1, NS // 2) as j:
                for u in range(2):
                    n = 2 * j + u
                    hidden(n, sw1, sw3, lambda c: xT[:, c, bass.ds(n * CAP1, CAP1)])
                    down(n, sw2, u)
            with pe.Fori(0, E1 // 2) as j:
                for u in range(2):
                    e = 2 * j + u
                    pe.wait_ge(in_xd[u], 16 * j + 16)
                    pe.wait_ge(xt_done, e + 1)
                    for c in range(DK):
                        for r in range(2):
                            mm = pe.transpose(psH[3][:, c * 256 + r * P:c * 256 + (r + 1) * P],
                                              xd[u][:, r, c * P:(c + 1) * P], ident[:])
                    mm.then_inc(xt_full, 1)
                    pe.wait_ge(in_w[u], 64 * j + 64)
                    pe.wait_ge(xt_done, e + 2)
                    hidden(NS + e, w1[u], w3[u], lambda c: xt[u][:, c, :])
                    down(NS + e, w2[u], u)

        @block.scalar
        def _(act):
            def silu(n, u):
                for f, (_, fw) in enumerate(FT1):
                    act.wait_ge(h_full, FTN * n + f + 1)
                    act.wait_ge(g_done, FTN * n + f + 1)
                    nc.scalar.activation(act_s[u][0:fw, f, :], psH[f][0:fw, 0:CAP1], ACT.Silu
                                         ).then_inc(silu_done, 1)

            act.wait_ge(l_done, 2)
            nc.scalar.activation(ex[:], ex[:], ACT.Exp).then_inc(ex_ready, 1)
            with act.Fori(0, NS // 2) as j:
                for u in range(2):
                    silu(2 * j + u, u)
            act.sem_inc(xt_done, 1)
            with act.Fori(0, E1 // 2) as j:
                for u in range(2):
                    e = 2 * j + u
                    act.wait_ge(xt_full, e + 1)
                    nc.scalar.activation(xt[u][:].rearrange("p c s -> p (c s)"), psH[3][:],
                                         ACT.Copy).then_inc(xt_done, 1)
                    silu(NS + e, u)
                    for r in range(2):
                        if r == 0:
                            act.wait_ge(stored[u], 16 * j + 16)
                        act.wait_ge(y_full, 2 * (NS + e) + r + 1)
                        nc.scalar.activation(yo[u][:, r, :], psY[r][:, 0:D], ACT.Copy).then_inc(y_done, 1)

        @block.vector
        def _(dve):
            count = [0]

            def link(ins):
                count[0] += 1
                ins.then_inc(chain, 1)
                dve.wait_ge(chain, count[0])

            def gated(n, u):
                for f, (_, fw) in enumerate(FT1):
                    dve.wait_ge(silu_done, FTN * n + f + 1)
                    nc.vector.tensor_tensor(g[u][0:fw, f, :], act_s[u][0:fw, f, :],
                                            psH[f][0:fw, CAP1:2 * CAP1], ALU.mult).then_inc(g_done, 1)

            def add_shared(n, dyn):
                for r in range(2):
                    dve.wait_ge(y_full, 2 * n + r + 1)
                    row = x[:, bass.ds(2 * n + r, 1), :].rearrange("p o d -> p (o d)")
                    nc.vector.tensor_tensor(row, row, psY[r][:, 0:D], ALU.add).then_inc(y_done, 1)

            nc.vector.memset(onesb[:], 1.0).then_inc(const, 1)
            dve.sem_inc(g_done, FTN)
            dve.sem_inc(y_done, 2)
            dve.wait_ge(in_c, 80)
            dve.wait_ge(l_full, 1)
            nc.vector.tensor_copy(logit[:].rearrange("p t e -> p (t e)"), psR[:, 0:NT * E1]).then_inc(l_done, 1)
            dve.wait_ge(l_done, 1)
            link(nc.vector.tensor_reduce(top[:], logit[:], AX.X, ALU.max))
            nc.vector.tensor_tensor(ex[:], logit[:], top[:].unsqueeze(2).broadcast_to([P, NT, E1]),
                                    ALU.subtract).then_inc(l_done, 1)
            dve.wait_ge(ex_ready, 1)
            link(nc.vector.tensor_reduce(tot[:], ex[:], AX.X, ALU.add))
            link(nc.vector.tensor_reduce(top[:], ex[:], AX.X, ALU.max))
            link(nc.vector.tensor_tensor(val[:], ex[:], top[:].unsqueeze(2).broadcast_to([P, NT, E1]), ALU.is_ge))
            link(nc.vector.tensor_tensor(val[:], val[:], rank[:].unsqueeze(1).broadcast_to([P, NT, E1]), ALU.mult))
            link(nc.vector.tensor_reduce(pos[:], val[:], AX.X, ALU.max))
            link(nc.vector.tensor_tensor(oh[:], val[:], pos[:].unsqueeze(2).broadcast_to([P, NT, E1]),
                                         ALU.is_equal))
            nc.vector.tensor_copy(ohb[:], oh[:]).then_inc(oh_ready, 1)
            link(nc.vector.reciprocal(tot[:], tot[:]))
            link(nc.vector.tensor_tensor(gate[:], tot[:], top[:], ALU.mult))
            link(nc.vector.tensor_tensor(val[:], oh[:], ebase[:].unsqueeze(1).broadcast_to([P, NT, E1]), ALU.mult))
            link(nc.vector.tensor_reduce(ebs[:], val[:], AX.X, ALU.add))
            for n in range(2):
                gated(n, n)
                add_shared(n, False)
            dve.wait_ge(cum_full, 1)
            link(nc.vector.tensor_tensor(cum[:].rearrange("p t e -> p (t e)"), psR[:, 0:NT * E1],
                                         oh[:].rearrange("p t e -> p (t e)"), ALU.mult))
            link(nc.vector.tensor_reduce(pos[:], cum[:], AX.X, ALU.add))
            link(nc.vector.tensor_scalar(keepm[:], pos[:], CAP1 + 0.5, None, ALU.is_lt))
            link(nc.vector.scalar_tensor_tensor(out=slot[:], in0=pos[:], scalar=-1.0, in1=ebs[:],
                                                op0=ALU.add, op1=ALU.add))
            link(nc.vector.tensor_tensor(slot[:], slot[:], keepm[:], ALU.mult))
            link(nc.vector.tensor_copy(g_idx[:], slot[:]))
            link(nc.vector.tensor_tensor(gate[:], gate[:], keepm[:], ALU.mult))
            link(nc.vector.tensor_scalar(keepm[:], keepm[:], -OUT_OF_RANGE, OUT_OF_RANGE, ALU.mult, ALU.add))
            link(nc.vector.tensor_tensor(slot[:], slot[:], keepm[:], ALU.add))
            nc.vector.tensor_copy(s_idx[:], slot[:]).then_inc(idx_ready, 1)
            with dve.Fori(1, NS // 2) as j:
                for u in range(2):
                    gated(2 * j + u, u)
                    add_shared(2 * j + u, True)
            with dve.Fori(0, E1 // 2) as j:
                for u in range(2):
                    gated(NS + 2 * j + u, u)
            dve.wait_ge(y_done, 2 * NS + 2)
            dve.wait_ge(gathered, 16 * NT)
            for j in range(NT):
                nc.vector.scalar_tensor_tensor(out=x[:, j, :], in0=back[:, j, :], scalar=gate[:, j:j + 1],
                                               in1=x[:, j, :], op0=ALU.mult, op1=ALU.add).then_inc(x_final, 1)


SCRATCH = {
    "w2_scr": (H0, P, DK * DCQ),
    "m_scr": (H0, HALF, 4 * DC),
    "wvo_scr": (P, H0 // 2, D),
    "acc_scr": (B * H0, P, ST, 2 * DC + 1),
    "xg_scr": (NSEL, D),
    "y_scr": (NSEL, D),
    "xd_scr": (E1 * CAP1, D),
    "oe_scr": (E1 * CAP1, D),
}


def tables():
    def rope(length, dim):
        e = np.arange(0, dim, 2, dtype=np.float32) / np.float32(dim)
        inv = (np.float32(1.0) / np.power(10000.0, e.astype(np.float64)).astype(np.float32)).astype(np.float32)
        f = (np.arange(length, dtype=np.float32)[:, None] * inv[None, :]).astype(np.float64)
        return (np.repeat(np.sin(f), 2, axis=1).astype(np.float32),
                np.repeat(np.cos(f), 2, axis=1).astype(np.float32))

    sin_q, cos_q = rope(S, DCQ)
    sin_k, cos_k = rope(L, DC)
    sq, cq = sin_q.T, cos_q.T
    tabs = {
        "tabA": np.concatenate([cq[:HALF], cq[HALF:]], axis=1),
        "tabB": np.concatenate([sq[HALF:], -sq[:HALF]], axis=1),
    }
    sgn = np.concatenate([-sin_k[:, :DC // 2], sin_k[:, DC // 2:]], axis=1)
    for name, tab in (("cosk", cos_k), ("sink", sgn)):
        full = np.zeros((LT * P, DC), np.float32)
        full[:L] = tab
        tabs[name] = full.reshape(LT, P, DC).transpose(1, 0, 2)
    tabs["ident"] = np.eye(P, dtype=np.float32)
    tabs["upper"] = np.triu(np.ones((P, P), np.float32)).astype(BF_NP)
    first = np.repeat(np.arange(B, dtype=np.float32) * CAP - 1.0, ST)
    tabs["cap_base"] = np.broadcast_to(first, (P, NT))
    tabs["identb"] = np.eye(P, dtype=np.float32).astype(BF_NP)
    tabs["causal"] = np.where(np.tril(np.ones((P, P), bool)), 0.0, MASKED).astype(np.float32).astype(BF_NP)
    tabs["hmask"] = np.repeat(np.eye(NH, dtype=np.float32), HD, axis=0)
    tabs["rank"] = np.broadcast_to(np.arange(E1, 0, -1, dtype=np.float32), (P, E1))
    tabs["ebase"] = np.broadcast_to(np.arange(E1, dtype=np.float32) * CAP1, (P, E1))
    tabs["ident16"] = np.eye(P, dtype=np.float16)
    return {k: np.ascontiguousarray(v) for k, v in tabs.items()}


def build(nc, t):
    LIVE.clear()
    with ExitStack() as whole:
        def sb(ctx, name, shape, dt=F32):
            return ctx.enter_context(nc.sbuf_tensor(name, shape, dt))

        k_unscale = sb(whole, "k_unscale", [P, 1])
        layer0 = whole.enter_context(ExitStack())
        keep = {
            "qscale": sb(layer0, "qscale", [P, H0]),
            "qk_scale": sb(layer0, "qk_scale", [P, H0]),
            "k_unscale": k_unscale,
            "ln1024": sb(layer0, "ln1024", [P, 1]),
            "ident16": sb(layer0, "ident16_sb", [P, P], F16),
            "xT": sb(layer0, "xT", [P, DK, B * S]),
        }
        with ExitStack() as ctx:
            phase_weights(nc, ctx, t, keep)
        keep["V"] = sb(layer0, "V", [P, B, LT, 2 * DC + 1], F16)
        keep["KK1"] = sb(layer0, "KK1", [P, B * L], F16)
        keep["KK2"] = sb(layer0, "KK2", [P, B * L], F16)
        with ExitStack() as ctx:
            phase_context(nc, ctx, t, keep)
        with ExitStack() as ctx:
            phase_attention0(nc, ctx, t, keep)
        layer0.close()
        x = sb(whole, "x_rows", [P, NT, D])
        xn = sb(whole, "xn_rows", [P, NT, D])
        xT = sb(whole, "xT_rows", [P, DK, B * S])
        with ExitStack() as ctx:
            phase_project0(nc, ctx, t, keep, x)
        with ExitStack() as ctx:
            phase_norm(nc, ctx, t, x, xn, xT, "n1_")
        with ExitStack() as ctx:
            phase_ffn0(nc, ctx, t, x, xn, xT)
        clear_semaphores(nc)
        with ExitStack() as ctx:
            phase_norm(nc, ctx, t, x, xn, xT, "n2_")
        with ExitStack() as layer1:
            qT = sb(layer1, "qT", [P, DK, B * S])
            kT = sb(layer1, "kT", [P, DK, B * S])
            v = sb(layer1, "v", [P, NT, D])
            with ExitStack() as ctx:
                phase_qkv1(nc, ctx, t, xT, qT, kT, v)
            with ExitStack() as ctx:
                phase_attention1(nc, ctx, t, x, qT, kT, v)
        with ExitStack() as ctx:
            phase_norm(nc, ctx, t, x, xn, xT, "n3_")
        with ExitStack() as ctx:
            phase_moe(nc, ctx, t, x, xn, xT)


_INS = ["x", "ctx_512", "L0_xattn_Wq", "L0_xattn_w_kc_q", "L0_xattn_w_kc_kv", "L0_xattn_W_qr", "L0_xattn_W_kr",
        "L0_xattn_Wo", "L0_ffn_W_r", "L0_ffn_b_r", "L0_ffn_W1", "L0_ffn_b1", "L0_ffn_W2", "L0_ffn_b2",
        "L1_xattn_Wq", "L1_xattn_Wkv_expand", "L1_xattn_Wout", "L1_ffn_Wg", "L1_ffn_W1", "L1_ffn_W3",
        "L1_ffn_W2", "L1_ffn_sw1", "L1_ffn_sw3", "L1_ffn_sw2"]


def kernel(**inputs):
    import numpy as _np
    import concourse.bacc as _bacc
    from concourse import mybir as _mybir
    from concourse.bass_utils import run_bass_kernel_spmd as _run

    nc = _bacc.Bacc("TRN2", target_bir_lowering=False, num_devices=1)
    arrays, t = {}, {}
    given = {name: _np.ascontiguousarray(inputs[name]) for name in _INS}
    for name, a in {**given, **tables()}.items():
        arrays[f"in_{name}"] = a
        t[name] = nc.dram_tensor(f"in_{name}", a.shape, _mybir.dt.from_np(a.dtype), kind="ExternalInput").ap()
    for name, shape in SCRATCH.items():
        t[name] = nc.dram_tensor(name, shape, _mybir.dt.float32, kind="Internal").ap()
    t["out"] = nc.dram_tensor("out_dram", (B, S, D), _mybir.dt.float32, kind="ExternalOutput").ap()
    build(nc, t)
    r = _run(nc, [arrays], core_ids=[0])
    return r.results[0]["out_dram"]
```

```python
from contextlib import ExitStack

import numpy as np

import concourse.bass as bass
from concourse import mybir

ALU = mybir.AluOpType
ACT = mybir.ActivationFunctionType
F32 = mybir.dt.float32
F16 = mybir.dt.float16
BF16 = mybir.dt.bfloat16
U32 = mybir.dt.uint32
AX = mybir.AxisListType
P = 128
BF_NP = mybir.dt.np(BF16)

B, S, D = 8, 256, 256
L = 1601
ST = S // P
NT = B * ST
DK = D // P
H0, K0, DC, DCQ, R0 = 16, 128, 64, 192, 64
LT = -(-L // P)
LLAST = L - (LT - 1) * P
HALF = DCQ // 2
EPS = 1e-5

QK_TOP = 2.0 ** 14
W_TOP = 2.0 ** 12
SHIFT_ONE = 2.0 ** 15
SHIFT_ROWS = 16
SHIFT_MUL = 1.0 / (SHIFT_ONE * SHIFT_ROWS)
LN_1024 = float(np.log(1024.0))


LIVE = []


def new_semaphore(nc, name):
    LIVE.append(nc.alloc_semaphore(name))
    return LIVE[-1]


def clear_semaphores(nc):
    nc.all_engine_barrier()
    nc.clear_and_free_semaphores(list(LIVE))
    nc.all_engine_barrier()
    LIVE.clear()


def layer_norm_stats(dve, nc, done, x, stats, agg, n):
    for j in range(n):
        nc.vector.bn_stats(stats[:, j, :], x[:, j, :]).then_inc(done, 1)
    dve.wait_ge(done, n)
    for j in range(n):
        nc.vector.bn_aggr(agg[:, j, :], stats[:, j, :]).then_inc(done, 1)
    dve.wait_ge(done, 2 * n)


def rstd_refined(nc, link, rstd, root, agg, tmp):
    var = agg[:, :, 1]
    link(nc.vector.reciprocal(rstd, root))
    link(nc.vector.tensor_tensor(tmp, rstd, rstd, ALU.mult))
    link(nc.vector.scalar_tensor_tensor(out=tmp, in0=var, scalar=EPS, in1=tmp, op0=ALU.add, op1=ALU.mult))
    link(nc.vector.tensor_scalar(tmp, tmp, -0.5, 1.5, ALU.mult, ALU.add))
    link(nc.vector.tensor_tensor(rstd, rstd, tmp, ALU.mult))


def phase_weights(nc, ctx, t, keep):
    def sb(name, shape, dt=F32):
        return ctx.enter_context(nc.sbuf_tensor(name, shape, dt))

    def sem(name):
        return new_semaphore(nc, name)

    wqk = sb("a_wqk", [P, H0 * (D + DCQ)])
    wq = wqk[:, 0:H0 * D].rearrange("p (h d) -> p h d", h=H0)
    wkcq = wqk[:, H0 * D:H0 * (D + DCQ)].rearrange("p (h q) -> p h q", h=H0)
    w2p = wqk[:, 0:H0 * DK * DCQ].bitcast(F16).rearrange("p (h t q) -> p h t q", h=H0, t=2)
    wqr = sb("a_wqr", [HALF, H0, 2, R0])
    wkr = sb("a_wkr", [DC, H0, R0])
    wkckv = sb("a_wkckv", [P, H0, DC])
    wo = sb("a_wo", [P, DK, H0 * K0])
    x = sb("a_x", [P, NT, D])
    w2 = sb("a_w2", [P, H0, DK * DCQ])
    rT = sb("a_rT", [R0, H0, DCQ + DC])
    m = sb("a_m", [HALF, H0, 2, DC])
    m2 = w2[0:HALF].rearrange("p h q -> p (h q)")[:, 0:H0 * 4 * DC].rearrange("p (h a b d) -> p h a b d",
                                                                            h=H0, a=2, b=2)
    woT = sb("a_woT", [P, H0, D])
    wvo = sb("a_wvo", [P, H0 // 2, D])
    rot = [sb(f"a_rot{i}", [P, LT, DC]) for i in range(2)]
    cosk = sb("a_cosk", [P, LT, DC])
    sink = sb("a_sink", [P, LT, DC])
    kv = keep["kv"]
    junk = sb("a_junk", [P, DK * DCQ])
    norms = sb("a_norms", [P, 2 * H0])
    nsum = sb("a_nsum", [P, 2 * H0])
    w_norm = sb("a_w_norm", [P, H0])
    w_scale = sb("a_w_scale", [P, H0])
    m_scale = sb("a_m_scale", [P, H0])
    bound = sb("a_bound", [P, H0])
    stats = sb("a_stats", [P, NT, 6])
    agg = sb("a_agg", [P, NT, 2])
    root = sb("a_root", [P, NT])
    rstd = sb("a_rstd", [P, NT])
    tmp = sb("a_tmp", [P, NT])
    ones = sb("a_ones", [P, P])
    eps = sb("a_eps", [P, 1])
    ident = sb("a_ident", [P, P])
    psA = [ctx.enter_context(nc.psum_tensor(f"a_psA{i}", [P, 512], F32)) for i in range(4)]
    psD = [ctx.enter_context(nc.psum_tensor(f"a_psD{i}", [P, 512], F32)) for i in range(4)]

    in_q = [sem(f"in_q{g}") for g in range(H0 // 4)]
    in_r, in_o, in_x = sem("in_r"), sem("in_o"), sem("in_x")
    a_full, a_done = sem("a_full"), sem("a_done")
    d_full, d_done = sem("d_full"), sem("d_done")
    chain = sem("a_chain")
    consts, agg_done = sem("a_consts"), sem("a_agg_done")
    var_ready, root_ready, xln_ready = sem("var_ready"), sem("root_ready"), sem("xln_ready")
    norms_ready, b2_ready, bound_ready = sem("norms_ready"), sem("b2_ready"), sem("bound_ready")
    m2_ready, stored = sem("m2_ready"), sem("a_stored")
    wsum_ready, wnorm_ready, w2p_done, xh_done = (sem("wsum_ready"), sem("wnorm_ready"), sem("w2p_done"),
                                                  sem("xh_done"))

    in_t, kv_zeroed, rotated, kv_turned, roped = (sem("in_t"), sem("kv_zeroed"), sem("rotated"),
                                                  sem("kv_turned"), sem("roped"))
    amax_ready = sem("amax_ready")
    POOL_SUMS = B - 2
    in_k = [sem(f"in_k{b}") for b in range(B)]

    N_A = H0 + H0 // 2 + H0 // 2
    N_M, N_VO, N_XT = H0 // 2, H0 // 4, NT // 2
    A_RT, A_WOT = H0, H0 + H0 // 2
    D_M, D_VO, D_NM, D_XT = 1, 1 + N_M, 1 + N_M + N_VO, 2 + N_M + N_VO

    with nc.Block() as block:
        @block.sync
        def _(sp):
            for g in range(H0 // 4):
                heads = slice(4 * g, 4 * g + 4)
                sp.dma_start(wq[:, heads], t["L0_xattn_Wq"].rearrange("(h k) d -> k h d", h=H0)[:, heads]
                             ).then_inc(in_q[g], 16)
                sp.dma_start(wkcq[:, heads], t["L0_xattn_w_kc_q"].rearrange("h k q -> k h q")[:, heads]
                             ).then_inc(in_q[g], 16)
            sp.dma_start(ident[:], t["ident"]).then_inc(in_r, 16)
            sp.dma_start(wqr[:], t["L0_xattn_W_qr"].rearrange("h (e q) r -> q h e r", e=2)).then_inc(in_r, 16)
            sp.dma_start(wkr[:], t["L0_xattn_W_kr"].rearrange("h d r -> d h r")).then_inc(in_r, 16)
            sp.dma_start(cosk[:], t["cosk"]).then_inc(in_t, 16)
            sp.dma_start(sink[:], t["sink"]).then_inc(in_t, 16)
            sp.wait_ge(kv_zeroed, 1)

            def load_context(b):
                sp.dma_start(kv[:, b, 0:LT - 1, :],
                             t["ctx_512"][b, 0:(LT - 1) * P, :].rearrange("(t p) d -> p t d", p=P)
                             ).then_inc(in_k[b], 16)
                sp.dma_start(kv[0:LLAST, b, LT - 1, :], t["ctx_512"][b, (LT - 1) * P:L, :]).then_inc(in_k[b], 16)

            load_context(0)
            sp.dma_start(wo[:], t["L0_xattn_Wo"].rearrange("(c e) k -> e c k", e=P)).then_inc(in_o, 16)
            sp.dma_start(wkckv[:], t["L0_xattn_w_kc_kv"].rearrange("h k d -> k h d")).then_inc(in_o, 16)
            for b in range(1, B):
                load_context(b)
            sp.wait_ge(w2p_done, 2 * H0)
            sp.dma_start(t["w2_scr"].rearrange("h p c -> p h c"),
                         wqk[:, 0:H0 * DK * DCQ].rearrange("p (h c) -> p h c", h=H0)).then_inc(stored, 16)
            sp.wait_ge(d_done, D_NM)
            sp.dma_start(t["wvo_scr"], wvo[:]).then_inc(stored, 16)
            sp.wait_ge(m2_ready, 2)
            sp.dma_start(t["m_scr"].rearrange("h p c -> p h c"),
                         m2.rearrange("p h a b d -> p h (a b d)")).then_inc(stored, 16)
            sp.wait_ge(stored, 48)

        @block.gpsimd
        def _(pool):
            nc.gpsimd.memset(kv[:, :, LT - 1, :], 0.0).then_inc(kv_zeroed, 1)
            pool.wait_ge(in_t, 32)
            h = DC // 2
            for b in range(B):
                r = rot[b % 2]
                pool.wait_ge(in_k[b], 32)
                if b >= 2:
                    pool.wait_ge(roped, b - 1)
                nc.gpsimd.tensor_tensor(r[:, :, 0:h], kv[:, b, :, h:DC], sink[:, :, 0:h],
                                        ALU.mult).then_inc(rotated, 1)
                nc.gpsimd.tensor_tensor(r[:, :, h:DC], kv[:, b, :, 0:h], sink[:, :, h:DC],
                                        ALU.mult).then_inc(rotated, 1)
                pool.wait_ge(rotated, 2 * b + 2)
                nc.gpsimd.tensor_tensor(kv[:, b], kv[:, b], cosk[:], ALU.mult).then_inc(kv_turned, 1)
                pool.wait_ge(kv_turned, b + 1)
                if b < POOL_SUMS:
                    nc.gpsimd.tensor_tensor(kv[:, b], kv[:, b], r[:], ALU.add).then_inc(roped, 1)

        @block.tensor
        def _(pe):
            for h in range(H0):
                if h % 4 == 0:
                    pe.wait_ge(in_q[h // 4], 32)
                if h >= 4:
                    pe.wait_ge(a_done, h - 3)
                for c in range(DK):
                    mm = pe.matmul(psA[h % 4][:, c * DCQ:(c + 1) * DCQ], wq[:, h, c * P:(c + 1) * P],
                                   wkcq[:, h, :], start=True, stop=True)
                mm.then_inc(a_full, 1)
            pe.wait_ge(in_r, 48)
            pe.wait_ge(consts, 3)
            pe.wait_ge(norms_ready, H0)
            pe.matmul(psD[0][:, 0:H0], ones[:], norms[:, 0:H0], start=True, stop=True).then_inc(d_full, 1)
            for g in range(H0 // 2):
                n = A_RT + g
                pe.wait_ge(a_done, n - 3)
                for u in range(2):
                    h, o = 2 * g + u, u * (DCQ + DC)
                    for e in range(2):
                        pe.transpose(psA[n % 4][0:R0, o + e * HALF:o + (e + 1) * HALF], wqr[:, h, e, :],
                                     ident[0:HALF, 0:HALF])
                    mm = pe.transpose(psA[n % 4][0:R0, o + DCQ:o + DCQ + DC], wkr[:, h, :], ident[0:DC, 0:DC])
                mm.then_inc(a_full, 1)
            pe.wait_ge(in_o, 32)
            for g in range(H0 // 2):
                n = A_WOT + g
                pe.wait_ge(a_done, n - 3)
                for u in range(2):
                    for c in range(DK):
                        mm = pe.transpose(psA[n % 4][:, u * D + c * P:u * D + (c + 1) * P],
                                          wo[:, c, (2 * g + u) * P:(2 * g + u + 1) * P], ident[:])
                mm.then_inc(a_full, 1)
            for g in range(N_M):
                n = D_M + g
                pe.wait_ge(a_done, A_RT + g + 1)
                if n >= 4:
                    pe.wait_ge(d_done, n - 3)
                for u in range(2):
                    h = 2 * g + u
                    for e in range(2):
                        mm = pe.matmul(psD[n % 4][0:HALF, (2 * u + e) * DC:(2 * u + e + 1) * DC],
                                       rT[:, h, e * HALF:(e + 1) * HALF], rT[:, h, DCQ:DCQ + DC],
                                       start=True, stop=True)
                mm.then_inc(d_full, 1)
            for g in range(N_VO):
                n = D_VO + g
                pe.wait_ge(a_done, A_WOT + 2 * g + 2)
                pe.wait_ge(d_done, n - 3)
                for u in range(2):
                    for k in range(2):
                        h = 4 * g + 2 * u + k
                        mm = pe.matmul(psD[n % 4][k * DC:(k + 1) * DC, u * D:(u + 1) * D], wkckv[:, h, :],
                                       woT[:, h, :], start=True, stop=True)
                mm.then_inc(d_full, 1)
            pe.wait_ge(norms_ready, 2 * H0)
            n = D_NM
            pe.wait_ge(d_done, n - 3)
            pe.matmul(psD[n % 4][:, 0:H0], ones[:], norms[:, H0:2 * H0], start=True, stop=True).then_inc(d_full, 1)
            for g in range(N_XT):
                n = D_XT + g
                pe.wait_ge(xln_ready, 2 * g + 2)
                pe.wait_ge(d_done, n - 3)
                for c in range(DK):
                    for u in range(2):
                        mm = pe.transpose(psD[n % 4][:, c * 256 + u * P:c * 256 + (u + 1) * P],
                                          x[:, 2 * g + u, c * P:(c + 1) * P], ident[:])
                mm.then_inc(d_full, 1)

        @block.scalar
        def _(act):
            act.dma_start(x[:], t["x"].rearrange("b (s p) d -> p (b s) d", p=P)).then_inc(in_x, 16)
            act.wait_ge(consts, 3)
            for h in range(H0):
                act.wait_ge(a_full, h + 1)
                if h >= 1:
                    act.wait_ge(norms_ready, h)
                nc.scalar.activation(junk[:], psA[h % 4][:, 0:DK * DCQ], ACT.Square,
                                     accum_out=norms[:, h:h + 1]).then_inc(norms_ready, 1)
                nc.scalar.activation(w2[:, h, :], psA[h % 4][:, 0:DK * DCQ], ACT.Copy).then_inc(a_done, 1)
                if h == H0 // 2:
                    act.wait_ge(var_ready, 1)
                    nc.scalar.activation(root[:], agg[:, :, 1], ACT.Sqrt, bias=eps[:, 0:1]).then_inc(root_ready, 1)
            act.wait_ge(wsum_ready, 1)
            nc.scalar.activation(w_norm[:], nsum[:, 0:H0], ACT.Sqrt).then_inc(wnorm_ready, 1)
            for g in range(H0 // 2):
                n = A_RT + g
                act.wait_ge(a_full, n + 1)
                nc.scalar.activation(rT[:, 2 * g:2 * g + 2, :].rearrange("r h c -> r (h c)"),
                                     psA[n % 4][0:R0, :], ACT.Copy).then_inc(a_done, 1)
            for g in range(H0 // 2):
                n = A_WOT + g
                act.wait_ge(a_full, n + 1)
                nc.scalar.activation(woT[:, 2 * g:2 * g + 2, :].rearrange("k h e -> k (h e)"),
                                     psA[n % 4][:, :], ACT.Copy).then_inc(a_done, 1)
            act.wait_ge(d_done, D_M + N_M)
            for h in range(H0):
                act.wait_ge(norms_ready, H0 + h)
                nc.scalar.activation(junk[0:HALF, 0:2 * DC], m[:, h, :, :].rearrange("p e d -> p (e d)"),
                                     ACT.Square,
                                     accum_out=norms[0:HALF, H0 + h:H0 + h + 1]).then_inc(norms_ready, 1)
            act.wait_ge(b2_ready, 1)
            nc.scalar.activation(bound[:], bound[:], ACT.Sqrt).then_inc(bound_ready, 1)
            for g in range(N_XT):
                n = D_XT + g
                act.wait_ge(d_full, n + 1)
                nc.scalar.activation(keep["xh"][:, :, 256 * g:256 * (g + 1)],
                                     psD[n % 4][:].rearrange("p (c s) -> p c s", c=DK), ACT.Copy
                                     ).then_inc(xh_done, 1)

        @block.vector
        def _(dve):
            count = [0]

            def link(ins):
                count[0] += 1
                ins.then_inc(chain, 1)
                dve.wait_ge(chain, count[0])

            link(nc.vector.memset(keep["ln1024"][:], LN_1024))
            nc.vector.memset(eps[:], EPS).then_inc(consts, 1)
            nc.vector.memset(ones[:], 1.0).then_inc(consts, 1)
            nc.vector.memset(norms[:], 0.0).then_inc(consts, 1)
            dve.wait_ge(in_x, 16)
            layer_norm_stats(dve, nc, agg_done, x, stats, agg, NT)
            dve.sem_inc(var_ready, 1)

            dve.wait_ge(root_ready, 1)
            rstd_refined(nc, link, rstd[:], root[:], agg, tmp[:])
            for j in range(NT):
                nc.vector.tensor_scalar(x[:, j, :], x[:, j, :], agg[:, j, 0:1], rstd[:, j:j + 1],
                                        ALU.subtract, ALU.mult).then_inc(xln_ready, 1)
            dve.wait_ge(d_full, 1)
            nc.vector.tensor_scalar(nsum[:, 0:H0], psD[0][:, 0:H0], 1e-30, None, ALU.add).then_inc(d_done, 1)
            dve.wait_ge(d_done, 1)
            dve.sem_inc(wsum_ready, 1)
            dve.wait_ge(wnorm_ready, 1)
            link(nc.vector.reciprocal(w_scale[:], w_norm[:]))
            link(nc.vector.tensor_scalar(w_scale[:], w_scale[:], W_TOP, None, ALU.mult))
            dve.wait_ge(a_done, H0)

            def split(h):
                nc.vector.tensor_scalar(w2p[:, h, 0, :], w2[:, h, :], w_scale[:, h:h + 1], None,
                                        ALU.mult).then_inc(w2p_done, 1)

            def split_rest(h):
                dve.wait_ge(w2p_done, H0 + h)
                nc.vector.scalar_tensor_tensor(out=w2p[:, h, 1, :], in0=w2[:, h, :], scalar=w_scale[:, h:h + 1],
                                               in1=w2p[:, h, 0, :], op0=ALU.mult,
                                               op1=ALU.subtract).then_inc(w2p_done, 1)

            for h in range(H0):
                split(h)
            for g in range(N_M):
                n = D_M + g
                split_rest(2 * g)
                split_rest(2 * g + 1)
                dve.wait_ge(d_full, n + 1)
                nc.vector.tensor_copy(m[:, 2 * g:2 * g + 2, :, :].rearrange("p h e d -> p (h e d)"),
                                      psD[n % 4][0:HALF, 0:4 * DC]).then_inc(d_done, 1)
            for g in range(N_VO):
                n = D_VO + g
                dve.wait_ge(d_full, n + 1)
                nc.vector.tensor_copy(wvo[:, 2 * g:2 * g + 2, :].rearrange("p g e -> p (g e)"),
                                      psD[n % 4][:, :]).then_inc(d_done, 1)
            n = D_NM
            dve.wait_ge(d_full, n + 1)
            nc.vector.tensor_copy(nsum[:, H0:2 * H0], psD[n % 4][:, 0:H0]).then_inc(d_done, 1)
            dve.wait_ge(d_done, n + 1)
            link(nc.vector.tensor_tensor(bound[:], nsum[:, 0:H0], nsum[:, H0:2 * H0], ALU.mult))
            link(nc.vector.tensor_scalar(bound[:], bound[:], 4.0 * D, 1e-30, ALU.mult, ALU.add))
            dve.sem_inc(b2_ready, 1)
            dve.wait_ge(bound_ready, 1)
            link(nc.vector.reciprocal(bound[:], bound[:]))
            link(nc.vector.tensor_scalar(keep["qscale"][:], bound[:], QK_TOP, None, ALU.mult))
            link(nc.vector.tensor_tensor(m_scale[:], keep["qscale"][:], w_norm[:], ALU.mult))
            link(nc.vector.tensor_scalar(m_scale[:], m_scale[:], 1.0 / W_TOP, None, ALU.mult))
            for k in range(2):
                nc.vector.tensor_tensor(
                    m2[:, :, :, k, :], m[:],
                    m_scale[0:HALF, :].unsqueeze(2).unsqueeze(3).broadcast_to([HALF, H0, 2, DC]),
                    ALU.mult).then_inc(m2_ready, 1)
            for g in range(N_XT):
                n = D_XT + g
                dve.wait_ge(xh_done, g + 1)
                nc.vector.tensor_tensor(keep["xl"][:, :, 256 * g:256 * (g + 1)],
                                        psD[n % 4][:].rearrange("p (c s) -> p c s", c=DK),
                                        keep["xh"][:, :, 256 * g:256 * (g + 1)], ALU.subtract).then_inc(d_done, 1)
            for b in range(B):
                if b < POOL_SUMS:
                    dve.wait_ge(roped, b + 1)
                else:
                    dve.wait_ge(kv_turned, b + 1)
                    link(nc.vector.tensor_tensor(kv[:, b], kv[:, b], rot[b % 2][:], ALU.add))
                nc.vector.tensor_reduce(keep["amax"][:, b:b + 1], kv[:, b], AX.XY, ALU.max,
                                        apply_absolute_value=True).then_inc(amax_ready, 1)
            dve.wait_ge(amax_ready, B)


def phase_context(nc, ctx, t, keep):
    def sb(name, shape, dt=F32):
        return ctx.enter_context(nc.sbuf_tensor(name, shape, dt))

    def sem(name):
        return new_semaphore(nc, name)

    kv = keep["kv"]
    amax = keep["amax"]
    aall = sb("b_aall", [P, B])
    ktop = sb("b_ktop", [P, 1])
    kscale = sb("b_kscale", [P, 1])
    ps = [ctx.enter_context(nc.psum_tensor(f"b_ps{i}", [P, 1024], F16)) for i in range(8)]
    in_ident, chain = sem("in_ident"), sem("b_chain")
    aall_ready = sem("aall_ready")
    v_ready, kt_full, k1_done, k2_done = sem("v_ready"), sem("kt_full"), sem("k1_done"), sem("k2_done")
    filled, high_copied = sem("b_filled"), sem("high_copied")
    V, KK1, KK2 = keep["V"], keep["KK1"], keep["KK2"]
    FIRST = 7
    jobs = [(b, lo, hi) for b in range(B) for lo, hi in ((0, FIRST), (FIRST, LT))]

    with nc.Block() as block:
        @block.sync
        def _(sp):
            for i, part in enumerate((keep["xh"], keep["xl"])):
                sp.dma_start(keep["xb"][:, i], part[:, :, 0:S]).then_inc(keep["in_xb"], 16)
            sp.dma_start(keep["w2s"][:], t["w2_scr"][0]).then_inc(keep["in_w2"], 16)
            sp.dma_start(keep["ms"][:], t["m_scr"][0].rearrange("p (a b) -> p a b", a=2)).then_inc(keep["in_m"], 16)
            sp.dma_start(keep["tabA"][:], t["tabA"]).then_inc(keep["in_tab"], 16)
            sp.dma_start(keep["tabB"][:], t["tabB"]).then_inc(keep["in_tab"], 16)

        @block.gpsimd
        def _(pool):
            nc.gpsimd.partition_all_reduce(aall[:], amax[:], P, bass.bass_isa.ReduceOp.max
                                           ).then_inc(aall_ready, 1)
            pool.wait_ge(aall_ready, 1)
            nc.gpsimd.memset(KK2[0:2 * SHIFT_ROWS, :], SHIFT_ONE).then_inc(filled, 1)
            pool.wait_ge(filled, 1)
            nc.gpsimd.memset(KK2[2 * SHIFT_ROWS:DC, :], 0.0).then_inc(filled, 1)
            pool.wait_ge(filled, 2)

        @block.vector
        def _(dve):
            count = [0]

            def link(ins):
                count[0] += 1
                ins.then_inc(chain, 1)
                dve.wait_ge(chain, count[0])

            def copy_high(b):
                dve.wait_ge(k1_done, 2 * b + 2)
                nc.vector.tensor_copy(KK2[DC:P, b * L:(b + 1) * L], KK1[DC:P, b * L:(b + 1) * L]
                                      ).then_inc(high_copied, 1)

            for b in range(B):
                nc.vector.memset(V[:, b, :, 2 * DC:2 * DC + 1], 1.0).then_inc(v_ready, 1)
            dve.wait_ge(aall_ready, 1)
            link(nc.vector.tensor_reduce(ktop[:], aall[:], AX.X, ALU.max))
            link(nc.vector.tensor_scalar(ktop[:], ktop[:], 1e-30, 1.0 / QK_TOP, ALU.add, ALU.mult))
            link(nc.vector.reciprocal(kscale[:], ktop[:]))
            link(nc.vector.tensor_scalar(keep["qk_scale"][:], keep["qscale"][:], kscale[:, 0:1], None, ALU.mult))
            link(nc.vector.reciprocal(keep["qk_scale"][:], keep["qk_scale"][:]))
            link(nc.vector.tensor_copy(keep["k_unscale"][:], ktop[:]))
            for b in range(B):
                link(nc.vector.tensor_scalar(V[:, b, :, DC:2 * DC], kv[:, b], kscale[:, 0:1], None, ALU.mult))
                nc.vector.scalar_tensor_tensor(out=V[:, b, :, 0:DC], in0=kv[:, b], scalar=kscale[:, 0:1],
                                               in1=V[:, b, :, DC:2 * DC], op0=ALU.mult,
                                               op1=ALU.subtract).then_inc(v_ready, 1)
                if b % 2 == 0 and b > 0:
                    copy_high(b - 1)
            copy_high(B - 1)

        @block.tensor
        def _(pe):
            pe.wait_ge(in_ident, 16)
            for n, (b, lo, hi) in enumerate(jobs):
                pe.wait_ge(v_ready, B + b + 1)
                if n >= 8:
                    pe.wait_ge(k1_done, n - 7)
                for i in range(lo, hi):
                    r = P if i < LT - 1 else LLAST
                    mm = pe.transpose(ps[n % 8][:, (i - lo) * P:(i - lo) * P + r], V[0:r, b, i, 0:2 * DC],
                                      keep["ident16"][0:r, 0:r])
                mm.then_inc(kt_full, 1)

        @block.scalar
        def _(act):
            act.dma_start(keep["ident16"][:], t["ident16"]).then_inc(in_ident, 16)
            for n, (b, lo, hi) in enumerate(jobs):
                w = min(hi * P, L) - lo * P
                act.wait_ge(kt_full, n + 1)
                if b % 2 == 0:
                    nc.scalar.activation(KK2[DC:P, b * L + lo * P:b * L + lo * P + w], ps[n % 8][DC:P, 0:w],
                                         ACT.Copy).then_inc(k2_done, 1)
                nc.scalar.activation(KK1[:, b * L + lo * P:b * L + lo * P + w], ps[n % 8][:, 0:w],
                                     ACT.Copy).then_inc(k1_done, 1)


def phase_attention0(nc, ctx, t, keep):
    def sb(name, shape, dt=F32):
        return ctx.enter_context(nc.sbuf_tensor(name, shape, dt))

    def sem(name):
        return new_semaphore(nc, name)

    HALF_L = 400
    TAIL = L - 3 * HALF_L
    AHEAD = 4
    V, KK1, KK2, xh, xl = keep["V"], keep["KK1"], keep["KK2"], keep["xh"], keep["xl"]
    kk1 = sb("c_kk1", [P, L], F16)
    kk2 = sb("c_kk2", [P, L], F16)
    kkm = [sb(f"c_kkm{i}", [P, 2 * TAIL], F16) for i in range(2)]
    vb = sb("c_vb", [P, LT, 2 * DC + 1], F16)
    ident16 = keep["ident16"]
    tabA, tabB, w2s, ms, xb = (keep[name] for name in ("tabA", "tabB", "w2s", "ms", "xb"))
    in_tab, in_w2, in_m, in_xb = (keep[name] for name in ("in_tab", "in_w2", "in_m", "in_xb"))
    w2p = w2s[:].bitcast(F16).rearrange("p (t c) -> p t c", t=2)
    ropeA = sb("c_ropeA", [HALF, 2, S])
    ropeB = sb("c_ropeB", [HALF, 2, S])
    roped = sb("c_roped", [HALF, 2, S])
    q1 = [sb(f"c_q1_{i}", [P, S], F16) for i in range(AHEAD)]
    q2 = [sb(f"c_q2_{i}", [P, S], F16) for i in range(AHEAD)]
    prob = [sb(f"c_prob{i}", [P, 4 * S if i < 3 else S]) for i in range(4)]
    rest = [sb(f"c_rest{i}", [P, 4 * S if i < 3 else S], F16) for i in range(4)]
    mxp = sb("c_mxp", [P, ST, 2])
    mx = sb("c_mx", [P, ST])
    mcol = sb("c_mcol", [P, ST, DC], F16)
    exp_scale = [sb(f"c_exp_scale{i}", [P, 1]) for i in range(AHEAD)]
    W = 2 * DC + 1
    acc = [sb(f"c_acc{i}", [P, ST, W]) for i in range(2)]
    psS = [ctx.enter_context(nc.psum_tensor(f"c_psS{i}", [P, 1024], F32)) for i in range(2)]
    psM = ctx.enter_context(nc.psum_tensor("c_psM", [P, 2, 512], F32))
    psQ = ctx.enter_context(nc.psum_tensor("c_psQ", [P, 512], F32))
    psV = ctx.enter_context(nc.psum_tensor("c_psV", [P, 512], F32))
    shiftT = psM[0:DC, :, HALF_L:HALF_L + DC].bitcast(F16)

    qb_full, rope_done, qk_full = sem("qb_full"), sem("rope_done"), sem("qk_full")
    rope_added = sem("rope_added")
    qh_done, ql_done = sem("qh_done"), sem("ql_done")
    mx_full, mx_done, mx_joined, mcol_done = sem("mx_full"), sem("mx_done"), sem("mx_joined"), sem("mcol_done")
    shift_full, shift_done = sem("shift_full"), sem("shift_done")
    s_full, exp_done = sem("s_full"), sem("exp_done")
    rest_dve, rest_pool = sem("rest_dve"), sem("rest_pool")
    pv_done = sem("pv_done")
    pv_drained = sem("pv_drained")
    sent = [sem(f"sent{i}") for i in range(2)]
    zeroed = sem("c_zeroed")
    in_kk = [sem(f"in_kk{g}") for g in range(4)]
    in_v = [sem(f"in_v{g}") for g in range(4)]
    in_kkm = [sem(f"in_kkm{i}") for i in range(2)]

    N = B * H0
    GROUPS = [(0, 4), (4, 8), (8, 12), (12, 13)]
    CHUNKS = [((0, HALF_L), (HALF_L, HALF_L)), ((L - 2 * TAIL, TAIL), (L - TAIL, TAIL))]
    POOL_COLS = 704

    def head(n):
        return n % H0

    def refill_x(queue, b):
        for i, part in enumerate((xh, xl)):
            queue.dma_start(xb[:, i], part[:, :, bass.ds(b * S, S)]).then_inc(in_xb, 16)

    def refill_maxima(queue, b, half):
        c0, w = CHUNKS[half][0][0], 2 * CHUNKS[half][0][1]
        queue.dma_start(kkm[half][:, 0:w], KK1[:, bass.ds(b * L + c0, w)]).then_inc(in_kkm[half], 16)

    def refill_scores(queue, b, g):
        c0, c1 = GROUPS[g][0] * P, min(GROUPS[g][1] * P, L)
        for part, whole in ((kk1, KK1), (kk2, KK2)):
            queue.dma_start(part[:, c0:c1], whole[:, bass.ds(b * L + c0, c1 - c0)]).then_inc(in_kk[g], 16)

    def refill_values(queue, b, g):
        lo, hi = GROUPS[g]
        queue.dma_start(vb[:, lo:hi, :], V[:, bass.ds(b, 1), lo:hi, :].rearrange("p o t w -> p (o t) w")
                     ).then_inc(in_v[g], 16)

    with nc.Block() as block:
        @block.sync
        def _(sp):
            def load_w2(n):
                sp.dma_start(w2s[:], t["w2_scr"][head(n)]).then_inc(in_w2, 16)

            def load_m(n):
                sp.dma_start(ms[:], t["m_scr"][head(n)].rearrange("p (a b) -> p a b", a=2)).then_inc(in_m, 16)

            for half in range(2):
                refill_maxima(sp, 0, half)
            for n in range(AHEAD - 1):
                sp.wait_ge(qb_full, n + 1)
                load_w2(n + 1)
                sp.wait_ge(qk_full, n + 1)
                load_m(n + 1)
            sp.sem_inc(sent[0], 16)
            sp.sem_inc(sent[1], 16)

            def step(n, u, b=None):
                if b is not None and u == 2:
                    sp.wait_ge(mx_full, 4 * (n + 1) + 4)
                    refill_maxima(sp, b, 1)
                if b is not None and u == 3:
                    sp.wait_ge(s_full, 4 * n + 2)
                    refill_scores(sp, b, 1)
                    sp.wait_ge(s_full, 4 * n + 3)
                    refill_scores(sp, b, 2)
                    sp.wait_ge(pv_done, 4 * n + 5)
                    refill_values(sp, b, 0)
                sp.wait_ge(qb_full, n + 4)
                if b is not None and u == 0:
                    refill_x(sp, b)
                load_w2(n + 4)
                if b is not None and u == 3:
                    sp.wait_ge(s_full, 4 * n + 4)
                    refill_scores(sp, b, 3)
                    sp.wait_ge(pv_done, 4 * n + 6)
                    refill_values(sp, b, 1)
                if b is not None and u == 2:
                    sp.wait_ge(s_full, 4 * (n + 1) + 1)
                    refill_scores(sp, b, 0)
                sp.wait_ge(qk_full, n + 4)
                load_m(n + 4)
                if b is not None and u == 1:
                    sp.wait_ge(mx_full, 4 * (n + 2) + 3)
                    refill_maxima(sp, b, 0)
                if b is not None and u == 3:
                    sp.wait_ge(pv_done, 4 * n + 7)
                    refill_values(sp, b, 2)
                sp.wait_ge(pv_drained, n + 2)
                sp.dma_start(t["acc_scr"][n], acc[u % 2][:]).then_inc(sent[u % 2], 16)
                if b is not None and u == 3:
                    refill_values(sp, b, 3)

            def batch_steps(b, following):
                with sp.Fori(0, H0 // AHEAD - 1) as j:
                    for u in range(AHEAD):
                        step(b * H0 + j * AHEAD + u, u)
                for u in range(AHEAD):
                    step(b * H0 + (H0 - AHEAD + u), u, following)

            with sp.Fori(0, B - 1) as b:
                batch_steps(b, b + 1)
            for u in range(2):
                sp.wait_ge(sent[u], 16 + 16 * (H0 // 2))
            sp.dma_start(keep["wvo"], t["wvo_scr"]).then_inc(keep["in_wvo"], 16)
            sp.dma_start(keep["acc0"].rearrange("p h s w -> p h (s w)"),
                         t["acc_scr"][0:H0].rearrange("h p s w -> p h (s w)")).then_inc(keep["in_acc0"], 16)
            batch_steps(B - 1, 0)
            for u in range(2):
                sp.wait_ge(sent[u], 16 + 16 * (N // 2))
            sp.wait_ge(in_w2, 16 * (N + 4))
            for g in range(4):
                sp.wait_ge(in_kk[g], 32 * (B + 1))
                sp.wait_ge(in_v[g], 16 * (B + 1))
            for half in range(2):
                sp.wait_ge(in_kkm[half], 16 * (B + 1))
            sp.wait_ge(in_xb, 32 * (B + 1))
            sp.wait_ge(in_m, 16 * (N + 4))

        @block.tensor
        def _(pe):
            def q_big(n, e, cs=tuple(range(DK))):
                if e == 0 and cs[0] == 0:
                    pe.wait_ge(in_w2, 16 * (n + 1))
                for c in cs:
                    cols = slice(c * DCQ + e * HALF, c * DCQ + (e + 1) * HALF)
                    for i, (w, x) in enumerate(((0, 0), (0, 1), (1, 0))):
                        mm = pe.matmul(psQ[0:HALF, e * S:(e + 1) * S], w2p[:, w, cols], xb[:, x, c, :],
                                       start=(c == 0 and i == 0), stop=(c == DK - 1 and i == 2))
                if e == 1 and cs[-1] == DK - 1:
                    mm.then_inc(qb_full, 1)

            def q_lat(n):
                pe.wait_ge(rope_added, n + 1)
                pe.wait_ge(in_m, 16 * (n + 1))
                for e in range(2):
                    mm = pe.matmul(psQ[:, 0:S], ms[:, e, :], roped[:, e, :], start=(e == 0), stop=(e == 1))
                mm.then_inc(qk_full, 1)

            def maxima(n, k, slot):
                st, half = divmod(k, 2)
                if k == 0 and not (isinstance(n, int) and n == 0):
                    pe.wait_ge(shift_done, n)
                if not (isinstance(n, int) and n == 0 and k == 0):
                    pe.wait_ge(mx_done, 4 * n + k)
                for i, (c0, w) in enumerate(CHUNKS[half]):
                    mm = pe.matmul(psM[:, i, 0:w], q1[slot][:, st * P:(st + 1) * P],
                                   kkm[half][:, i * w:(i + 1) * w], start=True, stop=True)
                mm.then_inc(mx_full, 1)

            def shift(n):
                for st in range(ST):
                    mm = pe.transpose(shiftT[:, st, :], mcol[:, st, :], ident16[:])
                mm.then_inc(shift_full, 1)

            def scores(n, g, slot, part=None):
                lo, hi = GROUPS[g]
                k0, k1 = part or (0, 2 * (hi - lo))
                if k0 == 0:
                    pe.wait_ge(exp_done, 4 * n + g + 1)
                for k in range(k0, k1):
                    one, i = divmod(k, hi - lo)
                    src, mov = ((kk1, q1), (kk2, q2))[one]
                    r = P if lo + i < LT - 1 else LLAST
                    mm = pe.matmul(psS[g % 2][0:r, i * S:(i + 1) * S],
                                   src[:, (lo + i) * P:(lo + i) * P + r], mov[slot][:, :],
                                   start=(one == 0 and i % 2 == 0), stop=(one == 1), skip_group_check=True)
                if k1 == 2 * (hi - lo):
                    mm.then_inc(s_full, 1)

            def values(n, g, part=None):
                lo, hi = GROUPS[g]
                t0, t1 = part or (0, hi - lo)
                if g == 0:
                    pe.wait_ge(pv_drained, n + 1)
                if t0 == 0:
                    if g < 3:
                        pe.wait_ge(rest_pool, 3 * n + g + 1)
                    pe.wait_ge(rest_dve, 4 * n + g + 1)
                high = prob[g][:].bitcast(BF16).rearrange("p (c t) -> p c t", t=2)[:, :, 1]
                for i in range(lo + t0, lo + t1):
                    r = P if i < LT - 1 else LLAST
                    for st in range(ST):
                        c0 = (i - lo) * S + st * P
                        pe.matmul(psV[:, st * W:(st + 1) * W], high[0:r, c0:c0 + P],
                                  vb[0:r, i, :],
                                  start=(i == 0 and st == 0), stop=False, skip_group_check=True)
                        mm = pe.matmul(psV[:, st * W + DC:(st + 1) * W], rest[g][0:r, c0:c0 + P],
                                       vb[0:r, i, DC:W],
                                       start=False, stop=(i == LT - 1), skip_group_check=True)
                if lo + t1 == hi:
                    mm.then_inc(pv_done, 1)

            pe.sem_inc(pv_done, 4)
            pe.wait_ge(in_xb, 32)
            q_big(0, 0)
            q_big(0, 1)
            q_lat(0)
            for n in range(2):
                pe.wait_ge(qh_done, n + 1)
                if n == 0:
                    for i in range(2):
                        pe.wait_ge(in_kkm[i], 16)
                maxima(n, 0, n)
                pe.wait_ge(ql_done, n + 1)
                q_big(n + 1, 0)
                q_big(n + 1, 1)
                for k in range(1, 4 - n):
                    maxima(n, k, n)
                if n == 0:
                    pe.wait_ge(mcol_done, 2)
                    shift(0)
                q_lat(n + 1)
            pe.wait_ge(shift_done, 1)
            for g in range(4):
                pe.wait_ge(in_kk[g], 32)
                pe.wait_ge(in_v[g], 16)
            scores(0, 0, 0)
            with pe.Fori(0, N // AHEAD) as j:
                for u in range(AHEAD):
                    n = AHEAD * j + u
                    s1, s2 = (u + 1) % AHEAD, (u + 2) % AHEAD
                    scores(n, 1, u)
                    for i in range(4):
                        if i == 1:
                            maxima(n + 1, 3, s1)
                        scores(n, 2, u, (2 * i, 2 * i + 2))
                        values(n, 0, (i, i + 1))
                    pe.wait_ge(ql_done, n + 3)
                    q_big(n + 3, 0)
                    q_big(n + 3, 1, (0,))
                    pe.wait_ge(mcol_done, 2 * n + 4)
                    q_big(n + 3, 1, (1,))
                    shift(n + 1)
                    scores(n, 3, u)
                    for i in range(4):
                        if i == 2:
                            maxima(n + 2, 0, s2)
                        scores(n + 1, 0, s1, (2 * i, 2 * i + 2))
                        values(n, 1, (i, i + 1))
                    values(n, 2)
                    maxima(n + 2, 1, s2)
                    q_lat(n + 3)
                    values(n, 3)
                    maxima(n + 2, 2, s2)

        @block.scalar
        def _(act):
            def q_high(n, slot):
                act.wait_ge(qk_full, n + 1)
                nc.scalar.activation(q1[slot][:], psQ[:, 0:S], ACT.Copy).then_inc(qh_done, 1)

            def shift_copy(n, slot):
                act.wait_ge(shift_full, n + 1)
                nc.scalar.activation(q2[slot][0:DC, :].rearrange("p (s c) -> p s c", s=ST), shiftT, ACT.Copy).then_inc(shift_done, 1)

            def exp(n, g, slot):
                lo, hi = GROUPS[g]
                r = P if hi < LT else LLAST
                w = (hi - lo) * S
                act.wait_ge(s_full, 4 * n + g + 1)
                act.wait_ge(in_kk[(g + 2) % 4], 32 * ((n + (g + 2) // 4) // H0) + 32)
                act.wait_ge(pv_done, 4 * n + g + 1)
                nc.scalar.activation(prob[g][0:r, 0:w], psS[g % 2][0:r, 0:w], ACT.Exp, bias=keep["ln1024"][0:r, :],
                                     scale=exp_scale[slot][0:r, :]).then_inc(exp_done, 1)

            for g in range(4):
                refill_scores(act, 0, g)
            for g in range(4):
                refill_values(act, 0, g)
            act.sem_inc(exp_done, 2)
            act.sem_inc(pv_drained, 1)
            q_high(0, 0)
            shift_copy(0, 0)
            q_high(1, 1)
            q_high(2, 2)
            exp(0, 0, 0)
            with act.Fori(0, N // AHEAD) as j:
                for u in range(AHEAD):
                    n = AHEAD * j + u
                    exp(n, 1, u)
                    exp(n, 2, u)
                    shift_copy(n + 1, (u + 1) % AHEAD)
                    exp(n, 3, u)
                    exp(n + 1, 0, (u + 1) % AHEAD)
                    q_high(n + 3, (u + 3) % AHEAD)
                    act.wait_ge(pv_done, 4 * n + 8)
                    act.wait_ge(sent[u % 2], 16 * (2 * j + u // 2) + 16)
                    nc.scalar.activation(acc[u % 2][:].rearrange("p s w -> p (s w)"), psV[:, 0:ST * W],
                                         ACT.Copy).then_inc(pv_drained, 1)

        @block.vector
        def _(dve):
            def rope(n):
                dve.wait_ge(qb_full, n + 1)
                if not isinstance(n, int) or n > 0:
                    dve.wait_ge(qk_full, n)
                nc.vector.tensor_tensor(ropeA[:].rearrange("p e s -> p (e s)"), psQ[0:HALF, :], tabA[:],
                                        ALU.mult).then_inc(rope_done, 1)
                for e in range(2):
                    nc.vector.tensor_tensor(ropeB[:, 1 - e, :], psQ[0:HALF, e * S:(e + 1) * S],
                                            tabB[:, e * S:(e + 1) * S], ALU.mult).then_inc(rope_done, 1)

            def q_low(n, slot):
                dve.wait_ge(qh_done, n + 1)
                dve.wait_ge(in_xb, 32 * ((n + 1) // H0) + 32)
                nc.vector.tensor_tensor(q2[slot][DC:P, :], psQ[DC:P, 0:S], q1[slot][DC:P, :],
                                        ALU.subtract).then_inc(ql_done, 1)

            def reduce_max(n, k):
                st, half = divmod(k, 2)
                dve.wait_ge(mx_full, 4 * n + k + 1)
                dve.wait_ge(in_kkm[(k + 1) % 2], 16 * ((n + (k + 1) // 4) // H0) + 16)
                w = CHUNKS[half][0][1]
                nc.vector.tensor_reduce(mxp[:, st, half:half + 1], psM[:, :, 0:w], AX.XY,
                                        ALU.max).then_inc(mx_done, 1)

            def join(n, slot):
                dve.wait_ge(mx_done, 4 * n + 4)
                nc.vector.tensor_scalar(exp_scale[slot][:], keep["qk_scale"][:, bass.ds(head(n), 1)], 1.0, None,
                                        ALU.mult).then_inc(mx_joined, 1)
                nc.vector.tensor_reduce(mx[:], mxp[:], AX.X, ALU.max).then_inc(mx_joined, 1)
                dve.wait_ge(mx_joined, 2 * n + 2)
                if not isinstance(n, int) or n > 0:
                    dve.wait_ge(shift_full, n)
                m = mx[:].unsqueeze(2).broadcast_to([P, ST, SHIFT_ROWS])
                nc.vector.tensor_scalar(mcol[:, :, 0:SHIFT_ROWS], m, -SHIFT_MUL, None,
                                        ALU.mult).then_inc(mcol_done, 1)
                dve.wait_ge(mcol_done, 2 * n + 1)
                nc.vector.scalar_tensor_tensor(out=mcol[:, :, SHIFT_ROWS:2 * SHIFT_ROWS], in0=m,
                                               scalar=-SHIFT_MUL, in1=mcol[:, :, 0:SHIFT_ROWS],
                                               op0=ALU.mult, op1=ALU.subtract).then_inc(mcol_done, 1)

            def rest_of(n, g):
                lo, hi = GROUPS[g]
                r = P if hi < LT else LLAST
                c0, c1 = (POOL_COLS if g < 3 else 0), (hi - lo) * S
                dve.wait_ge(exp_done, 4 * n + g + 3)
                dve.wait_ge(in_v[g], 16 * (n // H0) + 16)
                high = prob[g][:].bitcast(BF16).rearrange("p (c t) -> p c t", t=2)[:, :, 1]
                nc.vector.tensor_tensor(rest[g][0:r, c0:c1], prob[g][0:r, c0:c1], high[0:r, c0:c1],
                                        ALU.subtract).then_inc(rest_dve, 1)

            nc.vector.memset(mcol[:], 0.0).then_inc(zeroed, 1)
            dve.wait_ge(zeroed, 1)
            dve.wait_ge(in_tab, 32)
            rope(0)
            q_low(0, 0)
            for n in range(2):
                reduce_max(n, 0)
                rope(n + 1)
                reduce_max(n, 1)
                reduce_max(n, 2)
                if n == 0:
                    reduce_max(0, 3)
                    join(0, 0)
                q_low(n + 1, n + 1)
            rest_of(0, 0)
            with dve.Fori(0, N // AHEAD) as j:
                for u in range(AHEAD):
                    n = AHEAD * j + u
                    reduce_max(n + 1, 3)
                    join(n + 1, (u + 1) % AHEAD)
                    rest_of(n, 1)
                    rest_of(n, 2)
                    rope(n + 3)
                    reduce_max(n + 2, 0)
                    rest_of(n, 3)
                    reduce_max(n + 2, 1)
                    rest_of(n + 1, 0)
                    reduce_max(n + 2, 2)
                    q_low(n + 3, (u + 3) % AHEAD)

        @block.gpsimd
        def _(pool):
            def rope_sum(n):
                pool.wait_ge(rope_done, 3 * n + 3)
                if not isinstance(n, int) or n > 0:
                    pool.wait_ge(qk_full, n)
                nc.gpsimd.tensor_tensor(roped[:], ropeA[:], ropeB[:], ALU.add).then_inc(rope_added, 1)

            def rest_of(n, g):
                pool.wait_ge(exp_done, 4 * n + g + 3)
                high = prob[g][:].bitcast(BF16).rearrange("p (c t) -> p c t", t=2)[:, :, 1]
                nc.gpsimd.tensor_tensor(rest[g][:, 0:POOL_COLS], prob[g][:, 0:POOL_COLS],
                                        high[:, 0:POOL_COLS], ALU.subtract).then_inc(rest_pool, 1)

            for n in range(3):
                rope_sum(n)
            rest_of(0, 0)
            with pool.Fori(0, N // AHEAD) as j:
                for u in range(AHEAD):
                    n = AHEAD * j + u
                    rest_of(n, 1)
                    rest_of(n, 2)
                    rope_sum(n + 3)
                    rest_of(n + 1, 0)


def phase_project0(nc, ctx, t, keep, x):
    def sb(name, shape, dt=F32):
        return ctx.enter_context(nc.sbuf_tensor(name, shape, dt))

    def sem(name):
        return new_semaphore(nc, name)

    W = 2 * DC + 1
    G = H0 // 2
    wvo = keep["wvo"]
    ident = sb("d_ident", [P, P])
    acc = [keep["acc0"], sb("d_acc1", [P, H0, ST, W])]
    cs = [sb(f"d_cs{i}", [P, ST, H0, DC]) for i in range(2)]
    rec = sb("d_rec", [P, H0, ST])
    cT = [sb(f"d_cT{i}", [P, G, P]) for i in range(2)]
    psT = [ctx.enter_context(nc.psum_tensor(f"d_psT{i}", [P, 512], F32)) for i in range(4)]
    psO = [ctx.enter_context(nc.psum_tensor(f"d_psO{i}", [P, 512], F32)) for i in range(2)]
    in_c = sem("d_in_c")
    in_x = sem("d_in_x")
    in_acc = [keep["in_acc0"], sem("d_in_acc1")]
    chain, cs_ready, cs_read = sem("d_chain"), sem("cs_ready"), sem("cs_read")
    t_full, t_done, o_full, o_done = sem("d_t_full"), sem("d_t_done"), sem("d_o_full"), sem("d_o_done")

    with nc.Block() as block:
        @block.sync
        def _(sp):
            def load(b, u):
                sp.wait_ge(cs_read, b + 1)
                sp.dma_start(acc[u].rearrange("p h s w -> p h (s w)") if u == 0 else
                             acc[u][:].rearrange("p h s w -> p h (s w)"),
                             t["acc_scr"][bass.ds(b * H0, H0)].rearrange("h p s w -> p h (s w)")
                             ).then_inc(in_acc[u], 16)

            load(1, 1)
            with sp.Fori(1, B // 2) as j:
                for u in range(2):
                    load(2 * j + u, u)

        @block.vector
        def _(dve):
            def combine(b, u, j):
                dve.wait_ge(in_acc[u], 16 * j + 16)
                dve.wait_ge(t_full, 4 * b + 1)
                nc.vector.reciprocal(rec[:], acc[u][:, :, :, 2 * DC]).then_inc(chain, 1)
                nc.vector.tensor_tensor(cs[u][:].rearrange("p s h d -> p h s d"), acc[u][:, :, :, 0:DC],
                                        acc[u][:, :, :, DC:2 * DC], ALU.add).then_inc(chain, 1)
                dve.wait_ge(chain, 4 * b + 2)
                dve.sem_inc(cs_read, 1)
                nc.vector.tensor_scalar(rec[:], rec[:], keep["k_unscale"][:, 0:1], None,
                                        ALU.mult).then_inc(chain, 1)
                dve.wait_ge(chain, 4 * b + 3)
                nc.vector.tensor_tensor(cs[u][:].rearrange("p s h d -> p h s d"),
                                        cs[u][:].rearrange("p s h d -> p h s d"),
                                        rec[:].unsqueeze(3).broadcast_to([P, H0, ST, DC]),
                                        ALU.mult).then_inc(chain, 1)
                dve.wait_ge(chain, 4 * b + 4)
                dve.sem_inc(cs_ready, 1)

            def add_rows(b):
                for s in range(ST):
                    dve.wait_ge(o_full, 2 * b + s + 3)
                    xt = x[:, bass.ds(2 * b + s, 1), :].rearrange("p o d -> p (o d)")
                    nc.vector.tensor_tensor(xt, xt, psO[s][:, 0:D], ALU.add).then_inc(o_done, 1)

            dve.sem_inc(cs_read, 2)
            dve.sem_inc(o_done, 2)
            combine(0, 0, 0)
            dve.wait_ge(in_x, 16)
            with dve.Fori(0, B // 2 - 1) as j:
                combine(2 * j + 1, 1, j)
                add_rows(2 * j)
                combine(2 * j + 2, 0, j + 1)
                add_rows(2 * j + 1)
            combine(B - 1, 1, B // 2 - 1)
            add_rows(B - 2)
            add_rows(B - 1)

        @block.tensor
        def _(pe):
            pe.wait_ge(in_c, 16)
            pe.wait_ge(keep["in_wvo"], 16)
            pe.sem_inc(t_full, 8)
            pe.sem_inc(o_full, 2)
            with pe.Fori(0, B // 2) as j:
                for u in range(2):
                    b = 2 * j + u
                    pe.wait_ge(cs_ready, b + 1)
                    for s in range(ST):
                        for half in range(2):
                            pe.wait_ge(t_done, 4 * b + 2 * s + half + 1)
                            for g in range(4):
                                h = 2 * (4 * half + g)
                                mm = pe.transpose(psT[2 * s + half][:, g * P:(g + 1) * P],
                                                  cs[u][:, s, h:h + 2, :].rearrange("p h d -> p (h d)"), ident[:])
                            mm.then_inc(t_full, 1)
                    for s in range(ST):
                        pe.wait_ge(t_done, 4 * b + 2 * s + 6)
                        pe.wait_ge(o_done, 2 * b + s + 1)
                        for g in range(G):
                            mm = pe.matmul(psO[s][:, 0:D], cT[s][:, g, :], wvo[:, g, :],
                                           start=(g == 0), stop=(g == G - 1))
                        mm.then_inc(o_full, 1)

        @block.scalar
        def _(act):
            act.dma_start(ident[:], t["ident"]).then_inc(in_c, 16)
            act.dma_start(x[:], t["x"].rearrange("b (s p) d -> p (b s) d", p=P)).then_inc(in_x, 16)
            act.sem_inc(t_done, 4)
            with act.Fori(0, B // 2) as j:
                for u in range(2):
                    b = 2 * j + u
                    for s in range(ST):
                        for half in range(2):
                            act.wait_ge(t_full, 4 * b + 2 * s + half + 9)
                            if half == 0:
                                act.wait_ge(o_full, 2 * b + s + 1)
                            nc.scalar.activation(
                                cT[s][:, 4 * half:4 * half + 4, :].rearrange("p g c -> p (g c)"),
                                psT[2 * s + half][:], ACT.Copy).then_inc(t_done, 1)


class Norm:
    POOL_TILES = 3

    def __init__(self, nc, ctx, t, x, xn, xT, tag, banks):
        def sb(name, shape, dt=F32):
            return ctx.enter_context(nc.sbuf_tensor(tag + name, shape, dt))

        def sem(name):
            return new_semaphore(nc, tag + name)

        self.nc, self.t, self.x, self.xn, self.xT, self.banks = nc, t, x, xn, xT, banks
        self.ident = sb("n_ident", [P, P])
        self.stats = sb("n_stats", [P, NT, 6])
        self.agg = sb("n_agg", [P, NT, 2])
        self.root, self.rstd, self.tmp = sb("n_root", [P, NT]), sb("n_rstd", [P, NT]), sb("n_tmp", [P, NT])
        self.eps = sb("n_eps", [P, 1])
        self.in_ident, self.chain, self.agg_done = sem("n_in_ident"), sem("n_chain"), sem("n_agg_done")
        self.var_ready, self.root_ready = sem("n_var"), sem("n_root_ready")
        self.rstd_ready = sem("n_rstd_ready")
        self.rows_done, self.pool_rows = sem("n_rows_done"), sem("n_pool_rows")
        self.full, self.done = sem("n_full"), sem("n_done")

    def wait_rows(self, engine):
        engine.wait_ge(self.rows_done, NT - self.POOL_TILES)
        engine.wait_ge(self.pool_rows, self.POOL_TILES)

    def wait_columns(self, engine):
        engine.wait_ge(self.done, NT // 2)

    def sync(self, sp):
        sp.dma_start(self.ident[:], self.t["ident"]).then_inc(self.in_ident, 16)

    def scale_rows(self, compute, j, signal):
        compute.tensor_scalar(self.xn[:, j, :], self.x[:, j, :], self.agg[:, j, 0:1], self.rstd[:, j:j + 1],
                              ALU.subtract, ALU.mult).then_inc(signal, 1)

    def vector(self, dve):
        nc = self.nc
        count = [0]

        def link(ins):
            count[0] += 1
            ins.then_inc(self.chain, 1)
            dve.wait_ge(self.chain, count[0])

        link(nc.vector.memset(self.eps[:], EPS))
        layer_norm_stats(dve, nc, self.agg_done, self.x, self.stats, self.agg, NT)
        dve.sem_inc(self.var_ready, 1)
        dve.wait_ge(self.root_ready, 1)
        rstd_refined(nc, link, self.rstd[:], self.root[:], self.agg, self.tmp[:])
        dve.sem_inc(self.rstd_ready, 1)
        for j in range(NT - self.POOL_TILES):
            self.scale_rows(nc.vector, j, self.rows_done)

    def gpsimd(self, pool):
        pool.wait_ge(self.rstd_ready, 1)
        for j in range(NT - self.POOL_TILES, NT):
            self.scale_rows(self.nc.gpsimd, j, self.pool_rows)

    def tensor(self, pe):
        pe.wait_ge(self.in_ident, 16)
        for g in range(NT // 2):
            bank = self.banks[g % len(self.banks)]
            if g >= len(self.banks):
                pe.wait_ge(self.done, g + 1 - len(self.banks))
            mine = min(2 * g + 2, NT - self.POOL_TILES)
            pe.wait_ge(self.rows_done, mine)
            if 2 * g + 2 > mine:
                pe.wait_ge(self.pool_rows, 2 * g + 2 - mine)
            for c in range(DK):
                for u in range(2):
                    mm = pe.transpose(bank[:, c * 256 + u * P:c * 256 + (u + 1) * P],
                                      self.xn[:, 2 * g + u, c * P:(c + 1) * P], self.ident[:])
            mm.then_inc(self.full, 1)

    def scalar_root(self, act):
        nc = self.nc
        act.wait_ge(self.var_ready, 1)
        nc.scalar.activation(self.root[:], self.agg[:, :, 1], ACT.Sqrt,
                             bias=self.eps[:, 0:1]).then_inc(self.root_ready, 1)

    def scalar_columns(self, act):
        nc = self.nc
        for g in range(NT // 2):
            act.wait_ge(self.full, g + 1)
            nc.scalar.activation(self.xT[:, :, 256 * g:256 * (g + 1)],
                                 self.banks[g % len(self.banks)][:].rearrange("p (c s) -> p c s", c=DK),
                                 ACT.Copy).then_inc(self.done, 1)


CAP = 64
DFF = 1024
FT = DFF // P
NSEL = B * CAP
SEL_T = NSEL // P
TPS = NT // SEL_T
OUT_OF_RANGE = 16384.0


def phase_ffn0(nc, ctx, t, x, xn, xT):
    def sb(name, shape, dt=F32):
        return ctx.enter_context(nc.sbuf_tensor("e_" + name, shape, dt))

    def sem(name):
        return new_semaphore(nc, "e_" + name)

    upper = sb("upper", [P, P], BF16)
    onesb = sb("ones", [P, P], BF16)
    iota = sb("iota", [P, P])
    wr = sb("wr", [P, DK])
    wrb = sb("wrb", [P, DK, P])
    onesf = sb("onesf", [P, P])
    br = sb("br", [P, 1])
    b1 = sb("b1", [P, FT])
    b2 = sb("b2", [P, D])
    w1 = sb("w1", [P, DK, DFF])
    w2 = sb("w2", [P, FT, D])
    rows = sb("rows", [P, NT * P])
    diag = sb("diag", [P, NT, P])
    wcol = sb("wcol", [P, NT])
    le = sb("le", [P, NT, S], BF16)
    sel = sb("sel", [P, NT])
    selb = sb("selb", [P, NT], BF16)
    slot = sb("slot", [P, NT])
    base = sb("base", [P, NT])
    gate = sb("gate", [P, NT])
    left = sb("left", [P, NT])
    pick = sb("pick", [P, NT, P])
    pickT = sb("pickT", [P, NT, P])
    xgT = sb("xgT", [P, DK, NSEL])
    hT = sb("hT", [P, FT, NSEL])
    y = sb("y", [P, SEL_T, D])
    ps = [ctx.enter_context(nc.psum_tensor(f"e_ps{i}", [P, 512], F32)) for i in range(8)]
    in_c, in_w = sem("in_c"), sem("in_w")
    wrb_made, chain = sem("wrb_made"), sem("chain")
    r_full, r_done, le_ready, cnt_full = sem("r_full"), sem("r_done"), sem("le_ready"), sem("cnt_full")
    sel_ready, cum_full, pick_ready = sem("sel_ready"), sem("cum_full"), sem("pick_ready")
    g_full, g_done, pt_full, pt_done = sem("g_full"), sem("g_done"), sem("pt_full"), sem("pt_done")
    h_full, h_done, y_full, y_done = sem("h_full"), sem("h_done"), sem("y_full"), sem("y_done")
    b_full, b_done = sem("b_full"), sem("b_done")
    NB = NT * P // 512
    norm = Norm(nc, ctx, t, x, xn, xT, "e_", ps)

    with nc.Block() as block:
        @block.sync
        def _(sp):
            norm.sync(sp)
            sp.dma_start(upper[:], t["upper"]).then_inc(in_c, 16)
            sp.dma_start(iota[:], t["iota"]).then_inc(in_c, 16)
            sp.dma_start(base[:], t["cap_base"]).then_inc(in_c, 16)
            sp.dma_start(wr[:], t["L0_ffn_W_r"].rearrange("(c d) o -> d (c o)", d=P),
                         allow_slow_non_contiguous=True).then_inc(in_c, 16)
            sp.dma_start(br[:], t["L0_ffn_b_r"].partition_broadcast(P)).then_inc(in_c, 16)
            sp.dma_start(b1[:], t["L0_ffn_b1"].rearrange("(f p) -> p f", p=P),
                         allow_slow_non_contiguous=True).then_inc(in_w, 16)
            sp.dma_start(b2[:], t["L0_ffn_b2"].partition_broadcast(P)).then_inc(in_w, 16)
            sp.dma_start(w1[:], t["L0_ffn_W1"].rearrange("(c d) f -> d c f", d=P)).then_inc(in_w, 16)
            sp.dma_start(w2[:], t["L0_ffn_W2"].rearrange("(f p) d -> p f d", p=P)).then_inc(in_w, 16)

        @block.gpsimd
        def _(pool):
            norm.gpsimd(pool)

        @block.vector
        def _(dve):
            norm.vector(dve)
            count = [0]

            def link(ins):
                count[0] += 1
                ins.then_inc(chain, 1)
                dve.wait_ge(chain, count[0])

            link(nc.vector.memset(onesf[:], 1.0))
            link(nc.vector.memset(onesb[:], 1.0))
            dve.wait_ge(in_c, 80)
            for c in range(DK):
                nc.vector.tensor_scalar(wrb[:, c, :], onesf[:], wr[:, c:c + 1], None,
                                        ALU.mult).then_inc(wrb_made, 1)
            for k in range(NB):
                dve.wait_ge(r_full, k + 1)
                nc.vector.tensor_scalar(rows[:, k * 512:(k + 1) * 512], ps[k][:], br[:, 0:1], None,
                                        ALU.add).then_inc(r_done, 1)
            dve.wait_ge(r_done, NB)
            link(nc.vector.tensor_tensor(diag[:], rows[:].rearrange("p (t q) -> p t q", t=NT),
                                         norm.ident[:].unsqueeze(1).broadcast_to([P, NT, P]), ALU.mult))
            link(nc.vector.tensor_reduce(wcol[:], diag[:], AX.X, ALU.add))
            for j in range(NT):
                b = j // ST
                nc.vector.tensor_scalar(le[:, j, :], rows[:, b * S:(b + 1) * S], wcol[:, j:j + 1], None,
                                        ALU.is_le).then_inc(le_ready, 1)
            dve.wait_ge(cnt_full, 1)
            link(nc.vector.tensor_scalar(sel[:], ps[4][:, 0:NT], CAP - 0.5, None, ALU.is_lt))
            nc.vector.tensor_copy(selb[:], sel[:]).then_inc(sel_ready, 1)
            link(nc.vector.tensor_scalar(left[:], sel[:], -1.0, 1.0, ALU.mult, ALU.add))
            link(nc.vector.tensor_tensor(gate[:], wcol[:], sel[:], ALU.mult))
            link(nc.vector.scalar_tensor_tensor(out=base[:], in0=left[:], scalar=OUT_OF_RANGE, in1=base[:],
                                                op0=ALU.mult, op1=ALU.add))
            dve.wait_ge(cum_full, 1)
            link(nc.vector.tensor_tensor(slot[:], ps[5][:, 0:NT], base[:], ALU.add))
            for k in range(SEL_T):
                tiles = slice(k * TPS, (k + 1) * TPS)
                nc.vector.tensor_tensor(pick[:, tiles, :], slot[:, tiles].unsqueeze(2).broadcast_to([P, TPS, P]),
                                        iota[:].unsqueeze(1).broadcast_to([P, TPS, P]),
                                        ALU.is_equal).then_inc(pick_ready, 1)
            for k in range(SEL_T):
                dve.wait_ge(g_full, k + 1)
                nc.vector.tensor_copy(xgT[:, :, k * P:(k + 1) * P],
                                      ps[k][:, 0:DK * P].rearrange("p (c s) -> p c s", c=DK)).then_inc(g_done, 1)
            norm.wait_rows(dve)
            for j in range(NT):
                link(nc.vector.scalar_tensor_tensor(out=x[:, j, :], in0=xn[:, j, :], scalar=left[:, j:j + 1],
                                                    in1=x[:, j, :], op0=ALU.mult, op1=ALU.add))
            for k in range(SEL_T + 1):
                if k < SEL_T:
                    dve.wait_ge(y_full, k + 1)
                    nc.vector.tensor_tensor(y[:, k, :], ps[k][:, 0:D], b2[:], ALU.add).then_inc(y_done, 1)
                for j in range(max(k - 1, 0) * TPS, k * TPS):
                    dve.wait_ge(b_full, j + 1)
                    nc.vector.scalar_tensor_tensor(out=x[:, j, :], in0=ps[4 + j % 4][:, 0:D],
                                                   scalar=gate[:, j:j + 1], in1=x[:, j, :],
                                                   op0=ALU.mult, op1=ALU.add).then_inc(b_done, 1)

        @block.tensor
        def _(pe):
            def put_back(j):
                pe.wait_ge(y_done, j // TPS + 1)
                if j >= 4:
                    pe.wait_ge(b_done, j - 3)
                pe.matmul(ps[4 + j % 4][:, 0:D], pickT[:, j, :], y[:, j // TPS, :],
                          start=True, stop=True).then_inc(b_full, 1)

            norm.tensor(pe)
            norm.wait_columns(pe)
            pe.wait_ge(wrb_made, DK)
            for k in range(NB):
                for c in range(DK):
                    mm = pe.matmul(ps[k][:], wrb[:, c, :], xT[:, c, k * 512:(k + 1) * 512],
                                   start=(c == 0), stop=(c == DK - 1))
                mm.then_inc(r_full, 1)
            pe.wait_ge(in_c, 80)
            for b in range(B):
                pe.wait_ge(le_ready, ST * b + ST)
                for s in range(ST):
                    for j in range(ST):
                        mm = pe.matmul(ps[4][:, ST * b + s:ST * b + s + 1], le[:, ST * b + j, s * P:(s + 1) * P],
                                       onesb[:, 0:1], start=(j == 0), stop=(j == ST - 1))
            mm.then_inc(cnt_full, 1)
            pe.wait_ge(sel_ready, 1)
            pe.matmul(ps[5][:, 0:NT:2], upper[:], selb[:, 0:NT:2], start=True, stop=True)
            pe.matmul(ps[5][:, 1:NT:2], upper[:], selb[:, 1:NT:2], start=True, stop=False)
            pe.matmul(ps[5][:, 1:NT:2], onesb[:], selb[:, 0:NT:2], start=False,
                      stop=True).then_inc(cum_full, 1)
            for k in range(SEL_T):
                pe.wait_ge(pick_ready, k + 1)
                for c in range(DK):
                    for i in range(TPS):
                        j = k * TPS + i
                        mm = pe.matmul(ps[k][:, c * P:(c + 1) * P], xn[:, j, c * P:(c + 1) * P], pick[:, j, :],
                                       start=(i == 0), stop=(i == TPS - 1))
                mm.then_inc(g_full, 1)
            for g in range(NT // 4):
                for i in range(4):
                    mm = pe.transpose(ps[4 + g][:, i * P:(i + 1) * P], pick[:, 4 * g + i, :], norm.ident[:])
                mm.then_inc(pt_full, 1)
            pe.wait_ge(in_w, 64)
            pe.wait_ge(g_done, SEL_T)
            for f in range(FT):
                if f < 4:
                    pe.wait_ge(pt_done, f + 1)
                else:
                    pe.wait_ge(h_done, f - 3)
                for c in range(DK):
                    mm = pe.matmul(ps[4 + f % 4][:], w1[:, c, f * P:(f + 1) * P], xgT[:, c, :],
                                   start=(c == 0), stop=(c == DK - 1))
                mm.then_inc(h_full, 1)
            pe.wait_ge(h_done, FT)
            for k in range(SEL_T):
                for f in range(FT):
                    mm = pe.matmul(ps[k][:, 0:D], hT[:, f, k * P:(k + 1) * P], w2[:, f, :],
                                   start=(f == 0), stop=(f == FT - 1))
                mm.then_inc(y_full, 1)
                for i in range(TPS if k > 0 else 0):
                    put_back((k - 1) * TPS + i)
            for i in range(TPS):
                put_back((SEL_T - 1) * TPS + i)

        @block.scalar
        def _(act):
            norm.scalar_root(act)
            norm.scalar_columns(act)
            for g in range(NT // 4):
                act.wait_ge(pt_full, g + 1)
                nc.scalar.activation(pickT[:, 4 * g:4 * g + 4, :].rearrange("p j c -> p (j c)"), ps[4 + g][:],
                                     ACT.Copy).then_inc(pt_done, 1)
            act.wait_ge(in_w, 64)
            for f in range(FT):
                act.wait_ge(h_full, f + 1)
                nc.scalar.activation(hT[:, f, :], ps[4 + f % 4][:], ACT.Gelu_apprx_tanh,
                                     bias=b1[:, f:f + 1]).then_inc(h_done, 1)


H1, HD = 16, 16
SCALE1 = 1.0 / float(np.sqrt(HD))
NH = P // HD
HH = H1 // NH
VROW = P + HD
MASKED = -3.0e38


def phase_qkv1(nc, ctx, t, x, xn, xT, qT, kT, v, vm):
    def sb(name, shape, dt=F32):
        return ctx.enter_context(nc.sbuf_tensor("f_" + name, shape, dt))

    def sem(name):
        return new_semaphore(nc, "f_" + name)

    wq = sb("wq", [P, DK, D])
    wkv = sb("wkv", [P, 2 * DK, DC])
    c = sb("c", [P, NT, DC])
    wqT = sb("wqT", [P, DK, D])
    wkvT = sb("wkvT", [DC, 2 * D])
    cT = sb("cT", [DC, NT * P])
    psA = [ctx.enter_context(nc.psum_tensor(f"f_psA{i}", [P, 512], F32)) for i in range(3)]
    psD = [ctx.enter_context(nc.psum_tensor(f"f_psD{i}", [P, 512], F32)) for i in range(3)]
    psN = [ctx.enter_context(nc.psum_tensor(f"f_psN{i}", [P, 512], F32)) for i in range(2)]
    in_c, in_wq = sem("in_c"), sem("in_wq")
    a_full, a_done, d_full, d_done = sem("a_full"), sem("a_done"), sem("d_full"), sem("d_done")
    NQ = B * S // 512
    norm = Norm(nc, ctx, t, x, xn, xT, "f_", psN)
    vm_zeroed = sem("vm_zeroed")

    with nc.Block() as block:
        @block.sync
        def _(sp):
            norm.sync(sp)
            sp.dma_start(wkv[:], t["L1_xattn_Wkv_expand"].rearrange("(c e) d -> e c d", e=P)).then_inc(in_c, 16)
            for b in range(B):
                sp.dma_start(c[:, b * ST:(b + 1) * ST, :],
                             t["ctx_512"][b, 0:S, :].rearrange("(s p) d -> p s d", p=P)).then_inc(in_c, 16)
            sp.dma_start(wq[:], t["L1_xattn_Wq"].rearrange("(c e) d -> e c d", e=P)).then_inc(in_wq, 16)

        @block.gpsimd
        def _(pool):
            for u in range(2):
                nc.gpsimd.memset(vm[u][:], 0.0).then_inc(vm_zeroed, 1)
            norm.gpsimd(pool)
            pool.wait_ge(vm_zeroed, 2)

        @block.tensor
        def _(pe):
            pe.wait_ge(norm.in_ident, 16)
            pe.wait_ge(in_c, 16 * (1 + B))
            for ec in range(2 * DK):
                mm = pe.transpose(psA[0][0:DC, ec * P:(ec + 1) * P], wkv[:, ec, :], norm.ident[:])
            mm.then_inc(a_full, 1)
            for g in range(NQ):
                n = 1 + g
                if n >= 3:
                    pe.wait_ge(a_done, n - 2)
                for i in range(4):
                    mm = pe.transpose(psA[n % 3][0:DC, i * P:(i + 1) * P], c[:, 4 * g + i, :], norm.ident[:])
                mm.then_inc(a_full, 1)
            pe.wait_ge(in_wq, 16)
            n = 1 + NQ
            pe.wait_ge(a_done, n - 2)
            for dk in range(DK):
                for ec in range(DK):
                    mm = pe.transpose(psA[n % 3][:, dk * D + ec * P:dk * D + (ec + 1) * P],
                                      wq[:, ec, dk * P:(dk + 1) * P], norm.ident[:])
            mm.then_inc(a_full, 1)
            for e in range(DK):
                for g in range(NQ):
                    n = 2 + NQ + e * NQ + g
                    pe.wait_ge(a_done, max(n - 2, 1 + NQ))
                    pe.matmul(psA[n % 3][:], wkvT[:, e * P:(e + 1) * P], cT[:, g * 512:(g + 1) * 512],
                              start=True, stop=True).then_inc(a_full, 1)
            for g in range(NT // 2):
                if g >= 3:
                    pe.wait_ge(d_done, g - 2)
                for u in range(2):
                    i = 2 * g + u
                    mm = pe.matmul(psD[g % 3][:, u * D:(u + 1) * D], cT[:, i * P:(i + 1) * P],
                                   wkvT[:, D:2 * D], start=True, stop=True)
                mm.then_inc(d_full, 1)
            norm.tensor(pe)
            pe.wait_ge(a_done, 2 + NQ)
            for g in range(NQ):
                for e in range(DK):
                    n = NT // 2 + g * DK + e
                    pe.wait_ge(d_done, n - 2)
                    pe.wait_ge(norm.done, 2 * g + 2)
                    for dk in range(DK):
                        mm = pe.matmul(psD[n % 3][:], wqT[:, dk, e * P:(e + 1) * P],
                                       xT[:, dk, g * 512:(g + 1) * 512], start=(dk == 0), stop=(dk == DK - 1))
                    mm.then_inc(d_full, 1)

        @block.scalar
        def _(act):
            norm.scalar_root(act)
            act.wait_ge(a_full, 1)
            nc.scalar.activation(wkvT[:], psA[0][0:DC, :], ACT.Copy).then_inc(a_done, 1)
            for g in range(NQ):
                act.wait_ge(a_full, 2 + g)
                nc.scalar.activation(cT[:, g * 512:(g + 1) * 512], psA[(1 + g) % 3][0:DC, :],
                                     ACT.Copy).then_inc(a_done, 1)
            act.wait_ge(a_full, 2 + NQ)
            nc.scalar.activation(wqT[:].rearrange("p c e -> p (c e)"), psA[(1 + NQ) % 3][:],
                                 ACT.Copy).then_inc(a_done, 1)
            for e in range(DK):
                for g in range(NQ):
                    n = 2 + NQ + e * NQ + g
                    act.wait_ge(a_full, n + 1)
                    nc.scalar.activation(kT[:, e, g * 512:(g + 1) * 512], psA[n % 3][:],
                                         ACT.Copy).then_inc(a_done, 1)
            norm.scalar_columns(act)

        @block.vector
        def _(dve):
            norm.vector(dve)
            for g in range(NT // 2):
                dve.wait_ge(d_full, g + 1)
                nc.vector.tensor_copy(v[:, 2 * g:2 * g + 2, :].rearrange("p g e -> p (g e)"),
                                      psD[g % 3][:]).then_inc(d_done, 1)
            for g in range(NQ):
                for e in range(DK):
                    n = NT // 2 + g * DK + e
                    dve.wait_ge(d_full, n + 1)
                    nc.vector.tensor_copy(qT[:, e, g * 512:(g + 1) * 512], psD[n % 3][:]).then_inc(d_done, 1)


def phase_attention1(nc, ctx, t, x, qT, kT, v, vm):
    def sb(name, shape, dt=F32):
        return ctx.enter_context(nc.sbuf_tensor("g_" + name, shape, dt))

    def sem(name):
        return new_semaphore(nc, "g_" + name)

    ident = sb("ident", [P, P])
    identb = sb("identb", [P, P], BF16)
    causal = sb("causal", [P, P], BF16)
    hmask = sb("hmask", [P, NH])
    wo = sb("wo", [P, DK, D])
    woT = sb("woT", [P, DK, D])
    q = [sb(f"q{i}", [P, HH, S]) for i in range(2)]
    km = [sb(f"km{i}", [P, HH, NH, S]) for i in range(2)]
    prob = [sb(f"prob{i}", [P, 1024]) for i in range(2)]
    pT = [sb(f"pT{i}", [P, 1024]) for i in range(2)]
    mx = [sb(f"mx{i}", [P, NH]) for i in range(2)]
    bias = [sb(f"bias{i}", [P, NH]) for i in range(2)]
    sums = sb("sums", [P, HH, ST * NH])
    rec = sb("rec", [P, ST * NH])
    recx = sb("recx", [P, ST, NH, HD])
    rT = sb("rT", [P, S])
    oT = [sb(f"oT{i}", [P, S]) for i in range(HH)]
    psS = [ctx.enter_context(nc.psum_tensor(f"g_psS{i}", [P, 1024], F32)) for i in range(2)]
    psT = ctx.enter_context(nc.psum_tensor("g_psT", [P, 1024], F32))
    psO = ctx.enter_context(nc.psum_tensor("g_psO", [P, 512], F32))
    psX = ctx.enter_context(nc.psum_tensor("g_psX", [P, 512], F32))

    in_c, wo_full, wo_done = sem("in_c"), sem("wo_full"), sem("wo_done")
    q_ready, km_ready, vm_ready = sem("q_ready"), sem("km_ready"), sem("vm_ready")
    s_full = sem("s_full")
    mx_done, bias_ready = sem("mx_done"), sem("bias_ready")
    exp_done = sem("exp_done")
    t_full = sem("t_full")
    pt_done = sem("pt_done")
    pv_done = sem("pv_done")
    r_chain, r_ready, r_full = sem("r_chain"), sem("r_ready"), sem("r_full")
    r_copied = sem("r_copied")
    o_done = sem("o_done")
    p_full = sem("p_full")
    p_done = sem("p_done")
    UNITS = 3 * HH

    def heads(k):
        kind = k % 3
        return ((0, NH), P, 0) if kind == 0 else ((4 * (kind - 1), 4 * kind), S, 1)

    def nxt(b):
        return (b + 1) % B

    with nc.Block() as block:
        @block.sync
        def _(sp):
            sp.dma_start(ident[:], t["ident"]).then_inc(in_c, 16)
            sp.dma_start(identb[:], t["identb"]).then_inc(in_c, 16)
            sp.dma_start(causal[:], t["causal"]).then_inc(in_c, 16)
            sp.dma_start(hmask[:], t["hmask"]).then_inc(in_c, 16)
            sp.dma_start(wo[:], t["L1_xattn_Wout"].rearrange("(c e) d -> e c d", e=P)).then_inc(in_c, 16)

        @block.gpsimd
        def _(pool):
            def keys(b, u):
                for hh in range(HH):
                    ins = nc.gpsimd.tensor_tensor(
                        km[u][:, hh], kT[:, hh:hh + 1, bass.ds(b * S, S)].broadcast_to([P, NH, S]),
                        hmask[:].unsqueeze(2).broadcast_to([P, NH, S]), ALU.mult)
                ins.then_inc(km_ready, 1)

            def values(b, u):
                nc.gpsimd.tensor_copy(
                    vm[u][:].rearrange("p a (h w) -> p a h w", w=VROW)[:, :, :, 0:HD],
                    v[:, bass.ds(b * ST, ST), :].rearrange("p s (a h w) -> p (s a) h w", a=HH, h=NH)
                ).then_inc(vm_ready, 1)

            pool.wait_ge(in_c, 80)
            keys(0, 0)
            values(0, 0)
            with pool.Fori(0, B // 2) as j:
                for u in range(2):
                    b = 2 * j + u
                    pool.wait_ge(s_full, UNITS * b + 1)
                    keys(nxt(b), 1 - u)
                    pool.wait_ge(pv_done, UNITS * b + 2)
                    values(nxt(b), 1 - u)

        @block.tensor
        def _(pe):
            def scores(b_count, k, u):
                (h0, h1), w, st = heads(k)
                hh = k // 3
                slot = psS[k % 2]
                if k == 0:
                    pe.wait_ge(q_ready, b_count + 1)
                    pe.wait_ge(km_ready, b_count + 1)
                per = 512 // w
                for half in range(2):
                    ha = h0 + half * per
                    bank = slot[:, half * 512:(half + 1) * 512]
                    pe.matmul(bank, q[u][:, hh, st * P:(st + 1) * P],
                              km[u][:, hh, ha:ha + per, 0:w], start=True, stop=True)
                    diag = bank.rearrange("p (h k) -> p h k", h=per)[:, :, w - P:w]
                    mm = pe.matmul(diag, identb[:], causal[:].unsqueeze(1).broadcast_to([P, per, P]),
                                   start=False, stop=True, skip_group_check=True)
                mm.then_inc(s_full, 1)

            def transposes(b, k):
                n = UNITS * b + k
                pe.wait_ge(exp_done, n + 2)
                pe.wait_ge(pt_done, n + 1)
                for i in range(8):
                    mm = pe.transpose(psT[:, i * P:(i + 1) * P], prob[k % 2][:, i * P:(i + 1) * P], ident[:])
                mm.then_inc(t_full, 1)

            def values(b, k, u):
                (h0, h1), w, st = heads(k)
                hh = k // 3
                n = UNITS * b + k
                pe.wait_ge(pt_done, n + 2)
                if k % 3 == 0:
                    pe.wait_ge(o_done, HH * b + hh + 1)
                    if hh == 0:
                        pe.wait_ge(vm_ready, b + 1)
                i = 0
                for h in range(h0, h1):
                    for kt in range(w // P):
                        mm = pe.matmul(psO[:, st * P:(st + 1) * P],
                                       vm[u][:, kt * HH + hh, h * P:(h + 1) * P],
                                       pT[k % 2][:, i * P:(i + 1) * P],
                                       start=(k % 3 == 0 and i == 0),
                                       stop=(k % 3 != 1 and i == 7), skip_group_check=True)
                        i += 1
                mm.then_inc(pv_done, 1)

            def reciprocals(b, hh):
                n = HH * b + hh
                pe.wait_ge(r_ready, n + 1)
                pe.wait_ge(r_copied, n + 1)
                pe.wait_ge(p_done, b + 1)
                for st in range(ST):
                    mm = pe.transpose(psX[:, st * P:(st + 1) * P],
                                      recx[:, st].rearrange("p h w -> p (h w)"), ident[:])
                mm.then_inc(r_full, 1)

            def project(b):
                pe.wait_ge(o_done, HH * b + HH + 1)
                for st in range(ST):
                    for hh in range(HH):
                        mm = pe.matmul(psX[:, st * D:(st + 1) * D], oT[hh][:, st * P:(st + 1) * P], woT[:, hh, :],
                                       start=(hh == 0), stop=(hh == HH - 1))
                mm.then_inc(p_full, 1)

            pe.wait_ge(in_c, 80)
            for dk in range(DK):
                for ec in range(DK):
                    mm = pe.transpose(psX[:, dk * D + ec * P:dk * D + (ec + 1) * P],
                                      wo[:, ec, dk * P:(dk + 1) * P], ident[:])
            mm.then_inc(wo_full, 1)
            pe.sem_inc(t_full, 1)
            pe.sem_inc(pv_done, 2)
            pe.wait_ge(wo_done, 1)
            scores(0, 0, 0)

            def batch(b, u, first=False):
                for k in range(UNITS):
                    pe.wait_ge(exp_done, UNITS * b + k + 1)
                    if k < UNITS - 1:
                        scores(b, k + 1, u)
                    else:
                        scores(b + 1, 0, 1 - u)
                    transposes(b, k)
                    if k == 0 and not first:
                        project(b - 1)
                    if k >= 1:
                        values(b, k - 1, u)
                    if k == 3:
                        reciprocals(b, 0)
                values(b, UNITS - 1, u)
                reciprocals(b, 1)

            batch(0, 0, first=True)
            with pe.Fori(0, B // 2 - 1) as j:
                batch(2 * j + 1, 1)
                batch(2 * j + 2, 0)
            batch(B - 1, 1)
            project(B - 1)

        @block.scalar
        def _(act):
            def exps(b, k):
                (h0, h1), w, st = heads(k)
                hh = k // 3
                n = UNITS * b + k
                act.wait_ge(bias_ready, n + 1)
                if not isinstance(n, int) or n > 0:
                    act.wait_ge(t_full, n)
                for h in range(h0, h1):
                    i = h - h0
                    ins = nc.scalar.activation(prob[k % 2][:, i * w:(i + 1) * w], psS[k % 2][:, i * w:(i + 1) * w],
                                               ACT.Exp, bias=bias[k % 2][:, i:i + 1], scale=SCALE1,
                                               accum_out=sums[:, hh, st * NH + h:st * NH + h + 1])
                ins.then_inc(exp_done, 1)

            def copy_r(b, hh):
                n = HH * b + hh
                act.wait_ge(r_full, n + 1)
                act.wait_ge(o_done, n + 1)
                nc.scalar.activation(rT[:], psX[:, 0:S], ACT.Copy).then_inc(r_copied, 1)

            act.sem_inc(exp_done, 1)
            act.sem_inc(r_copied, 1)
            exps(0, 0)
            with act.Fori(0, B // 2) as j:
                for u in range(2):
                    b = 2 * j + u
                    for k in range(UNITS):
                        if k < UNITS - 1:
                            exps(b, k + 1)
                        else:
                            exps(b + 1, 0)
                        if k == 3:
                            copy_r(b, 0)
                    copy_r(b, 1)

        @block.vector
        def _(dve):
            def maxima(b, k):
                (h0, h1), w, st = heads(k)
                n = UNITS * b + k
                dve.wait_ge(s_full, n + 1)
                nh = h1 - h0
                nc.vector.tensor_reduce(mx[k % 2][:, 0:nh], psS[k % 2][:].rearrange("p (h k) -> p h k", h=nh),
                                        AX.X, ALU.max).then_inc(mx_done, 1)
                dve.wait_ge(mx_done, n + 1)
                nc.vector.tensor_scalar(bias[k % 2][:, 0:nh], mx[k % 2][:, 0:nh], -SCALE1, None,
                                        ALU.mult).then_inc(bias_ready, 1)

            def drain_t(b, k):
                n = UNITS * b + k
                dve.wait_ge(t_full, n + 2)
                dve.wait_ge(pv_done, n + 1)
                nc.vector.tensor_copy(pT[k % 2][:], psT[:]).then_inc(pt_done, 1)

            def reciprocals(b, hh):
                n = HH * b + hh
                dve.wait_ge(exp_done, UNITS * b + 3 * hh + 4)
                nc.vector.reciprocal(rec[:], sums[:, hh, :]).then_inc(r_chain, 1)
                dve.wait_ge(r_chain, n + 1)
                nc.vector.tensor_copy(recx[:].rearrange("p s h w -> p (s h) w"),
                                      rec[:].unsqueeze(2).broadcast_to([P, ST * NH, HD])).then_inc(r_ready, 1)

            def normalise(b, hh):
                n = HH * b + hh
                dve.wait_ge(r_copied, n + 2)
                dve.wait_ge(pv_done, UNITS * b + 3 * hh + 5)
                nc.vector.tensor_tensor(oT[hh][:], psO[:, 0:S], rT[:], ALU.mult).then_inc(o_done, 1)

            def add(b):
                dve.wait_ge(p_full, b + 1)
                rows = x[:, bass.ds(b * ST, ST), :]
                nc.vector.tensor_tensor(rows, rows, psX[:].rearrange("p (s d) -> p s d", s=ST),
                                        ALU.add).then_inc(p_done, 1)

            def queries(b, u):
                nc.vector.tensor_copy(q[u][:], qT[:, :, bass.ds(b * S, S)]).then_inc(q_ready, 1)

            dve.wait_ge(wo_full, 1)
            nc.vector.tensor_copy(woT[:].rearrange("p c e -> p (c e)"), psX[:]).then_inc(wo_done, 1)
            dve.sem_inc(pt_done, 1)
            dve.sem_inc(o_done, 1)
            dve.sem_inc(p_done, 1)
            queries(0, 0)
            maxima(0, 0)

            def batch(b, u, first=False):
                dve.wait_ge(s_full, UNITS * b + 1)
                queries(nxt(b), 1 - u)
                for k in range(UNITS):
                    if k < UNITS - 1:
                        maxima(b, k + 1)
                    else:
                        maxima(b + 1, 0)
                    if k == 0 and not first:
                        normalise(b - 1, 1)
                    drain_t(b, k)
                    if k == 0 and not first:
                        add(b - 1)
                    if k == 2:
                        reciprocals(b, 0)
                    if k == 3:
                        normalise(b, 0)
                reciprocals(b, 1)

            batch(0, 0, first=True)
            with dve.Fori(0, B // 2 - 1) as j:
                batch(2 * j + 1, 1)
                batch(2 * j + 2, 0)
            batch(B - 1, 1)
            normalise(B - 1, 1)
            add(B - 1)


E1, HID = 8, 352
CAP1 = B * S // E1
FT1 = [(0, 128), (128, 128), (256, 96)]


def phase_moe(nc, ctx, t, x, xn, xT):
    def sb(name, shape, dt=F32):
        return ctx.enter_context(nc.sbuf_tensor("m_" + name, shape, dt))

    def sem(name):
        return new_semaphore(nc, "m_" + name)

    FTN = len(FT1)
    ident = sb("ident", [P, P])
    upper = sb("upper", [P, P], BF16)
    onesb = sb("ones", [P, P], BF16)
    wg = sb("wg", [P, DK, E1])
    rank = sb("rank", [P, E1])
    ebase = sb("ebase", [P, E1])
    sw1 = sb("sw1", [P, DK, HID])
    sw3 = sb("sw3", [P, DK, HID])
    sw2 = sb("sw2", [P, FTN, D])
    w1 = [sb(f"w1_{i}", [P, DK, HID]) for i in range(2)]
    w3 = [sb(f"w3_{i}", [P, DK, HID]) for i in range(2)]
    w2 = [sb(f"w2_{i}", [P, FTN, D]) for i in range(2)]
    xt = [sb(f"xt{i}", [P, DK, CAP1]) for i in range(2)]
    xd = [sb(f"xd{i}", [P, 2, D]) for i in range(2)]
    act_s = [sb(f"s{i}", [P, FTN, CAP1]) for i in range(2)]
    g = [sb(f"g{i}", [P, FTN, CAP1]) for i in range(2)]
    yo = [sb(f"yo{i}", [P, 2, D]) for i in range(2)]
    zero = sb("zero", [P, NT * D // 4])
    logit = sb("logit", [P, NT, E1])
    top = sb("top", [P, NT])
    ex = sb("ex", [P, NT, E1])
    tot = sb("tot", [P, NT])
    val = sb("val", [P, NT, E1])
    oh = sb("oh", [P, NT, E1])
    ohb = sb("ohb", [P, NT, E1], BF16)
    cum = sb("cum", [P, NT, E1])
    pos = sb("pos", [P, NT])
    ebs = sb("ebs", [P, NT])
    keepm = sb("keepm", [P, NT])
    gate = sb("gate", [P, NT])
    slot = sb("slot", [P, NT])
    s_idx = sb("s_idx", [P, NT], U32)
    g_idx = sb("g_idx", [P, NT], U32)
    back = sb("back", [P, NT, D])
    psR = ctx.enter_context(nc.psum_tensor("m_psR", [P, 512], F32))
    psH = [ctx.enter_context(nc.psum_tensor(f"m_psH{i}", [P, 512], F32)) for i in range(4)]
    psY = [ctx.enter_context(nc.psum_tensor(f"m_psY{i}", [P, 512], F32)) for i in range(2)]

    in_c, in_s, in_z = sem("in_c"), sem("in_s"), sem("in_z")
    in_w = [sem(f"in_w{i}") for i in range(2)]
    in_xd = [sem(f"in_xd{i}") for i in range(2)]
    zeroed, chain, const = sem("zeroed"), sem("chain"), sem("const")
    l_full, l_done, ex_ready = sem("l_full"), sem("l_done"), sem("ex_ready")
    oh_ready, cum_full, idx_ready = sem("oh_ready"), sem("cum_full"), sem("idx_ready")
    scattered, gathered = sem("scattered"), sem("gathered")
    xt_full, xt_done = sem("xt_full"), sem("xt_done")
    h_full, silu_done, g_done = sem("h_full"), sem("silu_done"), sem("g_done")
    y_full, y_done = sem("y_full"), sem("y_done")
    stored = [sem(f"stored{i}") for i in range(2)]
    out_sent = sem("out_sent")
    x_final = sem("x_final")
    NS = B * S // CAP1
    HEAD = NS // 2
    TAILS = [(HEAD + E1 + i, HEAD + i) for i in range(NS - HEAD)]
    norm = Norm(nc, ctx, t, x, xn, xT, "m_", psH)

    def load_ffn(sp, s, d1, d3, d2, a1, a3, a2):
        sp.dma_start(d1[:], a1.rearrange("(c d) f -> d c f", d=P)).then_inc(s, 16)
        sp.dma_start(d3[:], a3.rearrange("(c d) f -> d c f", d=P)).then_inc(s, 16)
        sp.dma_start(d2[:, 0:2, :], a2[0:256, :].rearrange("(c f) d -> f c d", f=P)).then_inc(s, 16)
        sp.dma_start(d2[0:96, 2, :], a2[256:352, :]).then_inc(s, 16)

    with nc.Block() as block:
        @block.sync
        def _(sp):
            norm.sync(sp)
            sp.dma_start(ident[:], t["ident"]).then_inc(in_c, 16)
            sp.dma_start(upper[:], t["upper"]).then_inc(in_c, 16)
            sp.dma_start(rank[:], t["rank"]).then_inc(in_c, 16)
            sp.dma_start(ebase[:], t["ebase"]).then_inc(in_c, 16)
            sp.dma_start(wg[:], t["L1_ffn_Wg"].rearrange("(c d) e -> d c e", d=P)).then_inc(in_c, 16)
            load_ffn(sp, in_s, sw1, sw3, sw2, t["L1_ffn_sw1"], t["L1_ffn_sw3"], t["L1_ffn_sw2"])
            sp.wait_ge(zeroed, 1)
            for k in range(4):
                sp.dma_start(t["xd_scr"].rearrange("(k p r) d -> k p (r d)", k=4, p=P)[k],
                             zero[:]).then_inc(in_z, 16)

            def weights(e, u):
                ap = [a[bass.ds(e, 1)].rearrange("o a b -> (o a) b")
                      for a in (t["L1_ffn_W1"], t["L1_ffn_W3"], t["L1_ffn_W2"])]
                load_ffn(sp, in_w[u], w1[u], w3[u], w2[u], *ap)

            for u in range(2):
                sp.sem_inc(stored[u], 16)
            weights(0, 0)
            weights(1, 1)
            sp.wait_ge(scattered, 16 * NT)
            for u in range(2):
                sp.dma_start(xd[u][:], t["xd_scr"][u * CAP1:(u + 1) * CAP1, :].rearrange("(c p) d -> p c d", p=P)
                             ).then_inc(in_xd[u], 16)
            with sp.Fori(0, E1 // 2) as j:
                for u in range(2):
                    e = 2 * j + u
                    sp.wait_ge(y_full, 2 * (HEAD + e) + 2)
                    weights((e + 2) % E1, u)
                    sp.dma_start(xd[u][:], t["xd_scr"][bass.ds(((e + 2) % E1) * CAP1, CAP1), :]
                                 .rearrange("(c p) d -> p c d", p=P)).then_inc(in_xd[u], 16)
                    sp.wait_ge(y_done, 2 * (HEAD + e) + 4)
                    sp.dma_start(t["oe_scr"][bass.ds(e * CAP1, CAP1), :].rearrange("(c p) d -> p c d", p=P),
                                 yo[u][:]).then_inc(stored[u], 16)
            for u in range(2):
                sp.wait_ge(in_w[u], 64 * (E1 // 2 + 1))
                sp.wait_ge(in_xd[u], 16 * (E1 // 2 + 1))
                sp.wait_ge(stored[u], 16 + 16 * (E1 // 2))
            for j in range(NT // 4):
                sp.wait_ge(x_final, 4 * j + 4)
                sp.dma_start(t["out"].rearrange("b (s p) d -> p (b s) d", p=P)[:, 4 * j:4 * j + 4, :],
                             x[:, 4 * j:4 * j + 4, :]).then_inc(out_sent, 16)
            sp.wait_ge(out_sent, 16 * (NT // 4))

        @block.gpsimd
        def _(pool):
            nc.gpsimd.memset(zero[:], 0.0).then_inc(zeroed, 1)
            norm.gpsimd(pool)
            pool.wait_ge(in_z, 64)
            pool.wait_ge(idx_ready, 1)
            norm.wait_rows(pool)
            for j in range(NT):
                nc.gpsimd.indirect_dma_start(
                    out=t["xd_scr"], out_offset=bass.IndirectOffsetOnAxis(ap=s_idx[:, j:j + 1], axis=0),
                    in_=xn[:, j, :], in_offset=None, bounds_check=E1 * CAP1 - 1, oob_is_err=False
                ).then_inc(scattered, 16)
            for u in range(2):
                pool.wait_ge(stored[u], 16 + 16 * (E1 // 2))
            for j in range(NT):
                nc.gpsimd.indirect_dma_start(
                    out=back[:, j, :], out_offset=None, in_=t["oe_scr"],
                    in_offset=bass.IndirectOffsetOnAxis(ap=g_idx[:, j:j + 1], axis=0),
                    bounds_check=E1 * CAP1 - 1, oob_is_err=False).then_inc(gathered, 16)
            pool.wait_ge(gathered, 16 * NT)

        @block.tensor
        def _(pe):
            def hidden(n, a1, a3, moving, part):
                for f in ((0,), (1, 2))[part]:
                    f0, fw = FT1[f]
                    slot = psH[f]
                    pe.wait_ge(g_done, FTN * n + f + 1)
                    for k, a in enumerate((a1, a3)):
                        for c in range(DK):
                            mm = pe.matmul(slot[0:fw, k * CAP1:(k + 1) * CAP1], a[:, c, f0:f0 + fw],
                                           moving(c), start=(c == 0), stop=(c == DK - 1))
                    mm.then_inc(h_full, 1)

            def down(n, a2, u):
                for r in range(2):
                    if r == 0:
                        pe.wait_ge(g_done, FTN * n + 6)
                    pe.wait_ge(y_done, 2 * n + r + 1)
                    for f, (_, fw) in enumerate(FT1):
                        mm = pe.matmul(psY[r][:, 0:D], g[u][0:fw, f, r * P:(r + 1) * P], a2[0:fw, f, :],
                                       start=(f == 0), stop=(f == FTN - 1))
                    mm.then_inc(y_full, 1)

            norm.tensor(pe)
            norm.wait_columns(pe)
            pe.wait_ge(in_c, 80)
            for j in range(NT):
                for c in range(DK):
                    mm = pe.matmul(psR[:, j * E1:(j + 1) * E1], xT[:, c, j * P:(j + 1) * P], wg[:, c, :],
                                   start=(c == 0), stop=(c == DK - 1))
            mm.then_inc(l_full, 1)
            pe.wait_ge(in_s, 64)
            def shared(n, i, last):
                moving = (lambda c: xT[:, c, i * CAP1:(i + 1) * CAP1] if isinstance(i, int) else
                          xT[:, c, bass.ds(i * CAP1, CAP1)])
                hidden(n, sw1, sw3, moving, 0)
                if last is not None:
                    down(*last)
                hidden(n, sw1, sw3, moving, 1)

            def own(e, j, u, last):
                pe.wait_ge(in_xd[u], 16 * j + 16)
                pe.wait_ge(xt_done, e + 1)
                for c in range(DK):
                    for r in range(2):
                        mm = pe.transpose(psH[3][:, c * 256 + r * P:c * 256 + (r + 1) * P],
                                          xd[u][:, r, c * P:(c + 1) * P], ident[:])
                mm.then_inc(xt_full, 1)
                down(*last)
                pe.wait_ge(in_w[u], 64 * j + 64)
                pe.wait_ge(xt_done, e + 2)
                hidden(HEAD + e, w1[u], w3[u], lambda c: xt[u][:, c, :], 0)
                hidden(HEAD + e, w1[u], w3[u], lambda c: xt[u][:, c, :], 1)

            shared(0, 0, None)
            shared(1, 1, (0, sw2, 0))
            pe.wait_ge(oh_ready, 1)
            pe.wait_ge(const, 1)
            w = NT * E1
            pe.matmul(psR[:, 0:w], upper[:], ohb[:].rearrange("p t e -> p (t e)"), start=True, stop=True)
            for j in range(NT - 1):
                left = NT - 1 - j
                mm = pe.matmul(psR[:, (j + 1) * E1:w], onesb[:],
                               ohb[:, j:j + 1, :].broadcast_to([P, left, E1]),
                               start=False, stop=True, skip_group_check=True)
            mm.then_inc(cum_full, 1)
            with pe.Fori(1, HEAD // 2) as j:
                for u in range(2):
                    n = 2 * j + u
                    shared(n, n, (n - 1, sw2, 1 - u))
            own(0, 0, 0, (HEAD - 1, sw2, 1))
            with pe.Fori(0, E1 // 2 - 1) as j:
                own(2 * j + 1, j, 1, (HEAD + 2 * j, w2[0], 0))
                own(2 * j + 2, j + 1, 0, (HEAD + 2 * j + 1, w2[1], 1))
            own(E1 - 1, E1 // 2 - 1, 1, (HEAD + E1 - 2, w2[0], 0))
            last = (HEAD + E1 - 1, w2[1], 1)
            for n, i in TAILS:
                shared(n, i, last)
                last = (n, sw2, n % 2)
            down(*last)

        @block.scalar
        def _(act):
            def silu(n, u, fs=(0, 1, 2)):
                for f in fs:
                    fw = FT1[f][1]
                    act.wait_ge(h_full, FTN * n + f + 1)
                    act.wait_ge(g_done, FTN * n + f + 1)
                    nc.scalar.activation(act_s[u][0:fw, f, :], psH[f][0:fw, 0:CAP1], ACT.Silu
                                         ).then_inc(silu_done, 1)

            def copy_out(e, j, u):
                for r in range(2):
                    if r == 0:
                        act.wait_ge(stored[u], 16 * j + 16)
                    act.wait_ge(y_full, 2 * (HEAD + e) + r + 1)
                    nc.scalar.activation(yo[u][:, r, :], psY[r][:, 0:D], ACT.Copy).then_inc(y_done, 1)

            def own(e, u, last=None):
                act.wait_ge(xt_full, e + 1)
                nc.scalar.activation(xt[u][:].rearrange("p c s -> p (c s)"), psH[3][:],
                                     ACT.Copy).then_inc(xt_done, 1)
                if last is not None:
                    copy_out(*last)
                silu(HEAD + e, u)

            norm.scalar_root(act)
            norm.scalar_columns(act)
            act.wait_ge(l_done, 2)
            nc.scalar.activation(ex[:], ex[:], ACT.Exp).then_inc(ex_ready, 1)
            with act.Fori(0, HEAD // 2) as j:
                for u in range(2):
                    silu(2 * j + u, u)
            act.sem_inc(xt_done, 1)
            own(0, 0)
            with act.Fori(0, E1 // 2 - 1) as j:
                own(2 * j + 1, 1, (2 * j, j, 0))
                own(2 * j + 2, 0, (2 * j + 1, j, 1))
            own(E1 - 1, 1, (E1 - 2, E1 // 2 - 1, 0))
            for k, (n, _) in enumerate(TAILS):
                silu(n, n % 2, (0,))
                if k == 0:
                    copy_out(E1 - 1, E1 // 2 - 1, 1)
                silu(n, n % 2, (1, 2))

        @block.vector
        def _(dve):
            count = [0]

            def link(ins):
                count[0] += 1
                ins.then_inc(chain, 1)
                dve.wait_ge(chain, count[0])

            def gated(n, u, fs=(0, 1, 2)):
                for f in fs:
                    fw = FT1[f][1]
                    dve.wait_ge(silu_done, FTN * n + f + 1)
                    nc.vector.tensor_tensor(g[u][0:fw, f, :], act_s[u][0:fw, f, :],
                                            psH[f][0:fw, CAP1:2 * CAP1], ALU.mult).then_inc(g_done, 1)

            def add_shared(n, i):
                for r in range(2):
                    dve.wait_ge(y_full, 2 * n + r + 1)
                    row = x[:, bass.ds(2 * i + r, 1), :].rearrange("p o d -> p (o d)")
                    nc.vector.tensor_tensor(row, row, psY[r][:, 0:D], ALU.add).then_inc(y_done, 1)

            norm.vector(dve)
            nc.vector.memset(onesb[:], 1.0).then_inc(const, 1)
            dve.sem_inc(g_done, FTN)
            dve.sem_inc(y_done, 2)
            dve.wait_ge(in_c, 80)
            dve.wait_ge(l_full, 1)
            nc.vector.tensor_copy(logit[:].rearrange("p t e -> p (t e)"), psR[:, 0:NT * E1]).then_inc(l_done, 1)
            dve.wait_ge(l_done, 1)
            link(nc.vector.tensor_reduce(top[:], logit[:], AX.X, ALU.max))
            nc.vector.tensor_tensor(ex[:], logit[:], top[:].unsqueeze(2).broadcast_to([P, NT, E1]),
                                    ALU.subtract).then_inc(l_done, 1)
            dve.wait_ge(ex_ready, 1)
            link(nc.vector.tensor_reduce(tot[:], ex[:], AX.X, ALU.add))
            link(nc.vector.tensor_reduce(top[:], ex[:], AX.X, ALU.max))
            link(nc.vector.tensor_tensor(val[:], ex[:], top[:].unsqueeze(2).broadcast_to([P, NT, E1]), ALU.is_ge))
            link(nc.vector.tensor_tensor(val[:], val[:], rank[:].unsqueeze(1).broadcast_to([P, NT, E1]), ALU.mult))
            link(nc.vector.tensor_reduce(pos[:], val[:], AX.X, ALU.max))
            link(nc.vector.tensor_tensor(oh[:], val[:], pos[:].unsqueeze(2).broadcast_to([P, NT, E1]),
                                         ALU.is_equal))
            nc.vector.tensor_copy(ohb[:], oh[:]).then_inc(oh_ready, 1)
            link(nc.vector.reciprocal(tot[:], tot[:]))
            link(nc.vector.tensor_tensor(gate[:], tot[:], top[:], ALU.mult))
            link(nc.vector.tensor_tensor(val[:], oh[:], ebase[:].unsqueeze(1).broadcast_to([P, NT, E1]), ALU.mult))
            link(nc.vector.tensor_reduce(ebs[:], val[:], AX.X, ALU.add))
            gated(0, 0)
            gated(1, 1, (0,))
            add_shared(0, 0)
            gated(1, 1, (1, 2))
            dve.wait_ge(cum_full, 1)
            link(nc.vector.tensor_tensor(cum[:].rearrange("p t e -> p (t e)"), psR[:, 0:NT * E1],
                                         oh[:].rearrange("p t e -> p (t e)"), ALU.mult))
            link(nc.vector.tensor_reduce(pos[:], cum[:], AX.X, ALU.add))
            link(nc.vector.tensor_scalar(keepm[:], pos[:], CAP1 + 0.5, None, ALU.is_lt))
            link(nc.vector.scalar_tensor_tensor(out=slot[:], in0=pos[:], scalar=-1.0, in1=ebs[:],
                                                op0=ALU.add, op1=ALU.add))
            link(nc.vector.tensor_tensor(slot[:], slot[:], keepm[:], ALU.mult))
            link(nc.vector.tensor_copy(g_idx[:], slot[:]))
            link(nc.vector.tensor_tensor(gate[:], gate[:], keepm[:], ALU.mult))
            link(nc.vector.tensor_scalar(keepm[:], keepm[:], -OUT_OF_RANGE, OUT_OF_RANGE, ALU.mult, ALU.add))
            link(nc.vector.tensor_tensor(slot[:], slot[:], keepm[:], ALU.add))
            nc.vector.tensor_copy(s_idx[:], slot[:]).then_inc(idx_ready, 1)
            with dve.Fori(1, HEAD // 2) as j:
                for u in range(2):
                    n = 2 * j + u
                    gated(n, u, (0,))
                    add_shared(n - 1, n - 1)
                    gated(n, u, (1, 2))
            add_shared(HEAD - 1, HEAD - 1)
            with dve.Fori(0, E1 // 2) as j:
                for u in range(2):
                    gated(HEAD + 2 * j + u, u)

            def add_own(j0, j1):
                for j in range(j0, j1):
                    nc.vector.scalar_tensor_tensor(out=x[:, j, :], in0=back[:, j, :], scalar=gate[:, j:j + 1],
                                                   in1=x[:, j, :], op0=ALU.mult, op1=ALU.add).then_inc(x_final, 1)

            for k, (n, i) in enumerate(TAILS):
                gated(n, n % 2, (0,))
                if k > 0:
                    add_shared(n - 1, i - 1)
                gated(n, n % 2, (1, 2))
            dve.wait_ge(gathered, 16 * NT)
            dve.wait_ge(y_done, 2 * n + 2)
            add_own(0, NT - 4)
            add_shared(n, i)
            dve.wait_ge(y_done, 2 * n + 4)
            add_own(NT - 4, NT)


SCRATCH = {
    "w2_scr": (H0, P, DK * DCQ),
    "m_scr": (H0, HALF, 4 * DC),
    "wvo_scr": (P, H0 // 2, D),
    "acc_scr": (B * H0, P, ST, 2 * DC + 1),
    "xd_scr": (E1 * CAP1, D),
    "oe_scr": (E1 * CAP1, D),
}


def tables():
    def rope(length, dim):
        e = np.arange(0, dim, 2, dtype=np.float32) / np.float32(dim)
        inv = (np.float32(1.0) / np.power(10000.0, e.astype(np.float64)).astype(np.float32)).astype(np.float32)
        f = (np.arange(length, dtype=np.float32)[:, None] * inv[None, :]).astype(np.float64)
        return (np.repeat(np.sin(f), 2, axis=1).astype(np.float32),
                np.repeat(np.cos(f), 2, axis=1).astype(np.float32))

    sin_q, cos_q = rope(S, DCQ)
    sin_k, cos_k = rope(L, DC)
    sq, cq = sin_q.T, cos_q.T
    tabs = {
        "tabA": np.concatenate([cq[:HALF], cq[HALF:]], axis=1),
        "tabB": np.concatenate([sq[HALF:], -sq[:HALF]], axis=1),
    }
    sgn = np.concatenate([-sin_k[:, :DC // 2], sin_k[:, DC // 2:]], axis=1)
    for name, tab in (("cosk", cos_k), ("sink", sgn)):
        full = np.zeros((LT * P, DC), np.float32)
        full[:L] = tab
        tabs[name] = full.reshape(LT, P, DC).transpose(1, 0, 2)
    tabs["ident"] = np.eye(P, dtype=np.float32)
    tabs["upper"] = np.triu(np.ones((P, P), np.float32)).astype(BF_NP)
    tabs["iota"] = np.broadcast_to(np.arange(P, dtype=np.float32), (P, P))
    first = np.repeat(np.arange(B, dtype=np.float32) % 2 * CAP - 1.0, ST)
    tabs["cap_base"] = np.broadcast_to(first, (P, NT))
    tabs["identb"] = np.eye(P, dtype=np.float32).astype(BF_NP)
    tabs["causal"] = np.where(np.tril(np.ones((P, P), bool)), 0.0, MASKED).astype(np.float32).astype(BF_NP)
    tabs["hmask"] = np.repeat(np.eye(NH, dtype=np.float32), HD, axis=0)
    tabs["rank"] = np.broadcast_to(np.arange(E1, 0, -1, dtype=np.float32), (P, E1))
    tabs["ebase"] = np.broadcast_to(np.arange(E1, dtype=np.float32) * CAP1, (P, E1))
    tabs["ident16"] = np.eye(P, dtype=np.float16)
    return {k: np.ascontiguousarray(v) for k, v in tabs.items()}


def build(nc, t):
    LIVE.clear()
    with ExitStack() as whole:
        def sb(ctx, name, shape, dt=F32):
            return ctx.enter_context(nc.sbuf_tensor(name, shape, dt))

        k_unscale = sb(whole, "k_unscale", [P, 1])
        kv = sb(whole, "kv", [P, B * LT * DC])[:]
        n_acc = H0 * ST * (2 * DC + 1)
        acc0 = kv[:, 0:n_acc].rearrange("p (h s w) -> p h s w", h=H0, s=ST)
        wvo = kv[:, n_acc:n_acc + H0 // 2 * D].rearrange("p (g d) -> p g d", g=H0 // 2)
        layer0 = whole.enter_context(ExitStack())
        keep = {
            "qscale": sb(layer0, "qscale", [P, H0]),
            "qk_scale": sb(layer0, "qk_scale", [P, H0]),
            "k_unscale": k_unscale,
            "acc0": acc0,
            "wvo": wvo,
            "in_acc0": new_semaphore(nc, "in_acc0"),
            "in_wvo": new_semaphore(nc, "in_wvo"),
            **{name: new_semaphore(nc, name) for name in ("in_tab", "in_w2", "in_m", "in_xb")},
            "amax": sb(layer0, "amax", [P, B]),
            "ln1024": sb(layer0, "ln1024", [P, 1]),
            "ident16": sb(layer0, "ident16_sb", [P, P], F16),
            "kv": kv.rearrange("p (b t d) -> p b t d", b=B, t=LT),
            "xh": sb(layer0, "xh", [P, DK, B * S], F16),
            "xl": sb(layer0, "xl", [P, DK, B * S], F16),
        }
        with ExitStack() as ctx:
            phase_weights(nc, ctx, t, keep)
        keep["tabA"] = sb(layer0, "c_tabA", [HALF, 2 * S])
        keep["tabB"] = sb(layer0, "c_tabB", [HALF, 2 * S])
        keep["w2s"] = sb(layer0, "c_w2s", [P, DK * DCQ])
        keep["ms"] = sb(layer0, "c_ms", [HALF, 2, P])
        keep["xb"] = sb(layer0, "c_xb", [P, 2, DK, S], F16)
        keep["V"] = sb(layer0, "V", [P, B, LT, 2 * DC + 1], F16)
        keep["KK1"] = sb(layer0, "KK1", [P, B * L], F16)
        keep["KK2"] = sb(layer0, "KK2", [P, B * L], F16)
        with ExitStack() as ctx:
            phase_context(nc, ctx, t, keep)
        with ExitStack() as ctx:
            phase_attention0(nc, ctx, t, keep)
        layer0.close()
        x = sb(whole, "x_rows", [P, NT, D])
        xn = sb(whole, "xn_rows", [P, NT, D])
        xT = sb(whole, "xT_rows", [P, DK, B * S])
        with ExitStack() as ctx:
            phase_project0(nc, ctx, t, keep, x)
        with ExitStack() as ctx:
            phase_ffn0(nc, ctx, t, x, xn, xT)
        clear_semaphores(nc)
        with ExitStack() as layer1:
            qT = sb(layer1, "qT", [P, DK, B * S])
            kT = sb(layer1, "kT", [P, DK, B * S])
            v = kv[:, 0:NT * D].rearrange("p (j d) -> p j d", j=NT)
            vm = [sb(layer1, f"vm{i}", [P, ST * HH, NH * VROW]) for i in range(2)]
            with ExitStack() as ctx:
                phase_qkv1(nc, ctx, t, x, xn, xT, qT, kT, v, vm)
            with ExitStack() as ctx:
                phase_attention1(nc, ctx, t, x, qT, kT, v, vm)
        with ExitStack() as ctx:
            phase_moe(nc, ctx, t, x, xn, xT)


_INS = ["x", "ctx_512", "L0_xattn_Wq", "L0_xattn_w_kc_q", "L0_xattn_w_kc_kv", "L0_xattn_W_qr", "L0_xattn_W_kr",
        "L0_xattn_Wo", "L0_ffn_W_r", "L0_ffn_b_r", "L0_ffn_W1", "L0_ffn_b1", "L0_ffn_W2", "L0_ffn_b2",
        "L1_xattn_Wq", "L1_xattn_Wkv_expand", "L1_xattn_Wout", "L1_ffn_Wg", "L1_ffn_W1", "L1_ffn_W3",
        "L1_ffn_W2", "L1_ffn_sw1", "L1_ffn_sw3", "L1_ffn_sw2"]


def kernel(**inputs):
    import numpy as _np
    import concourse.bacc as _bacc
    from concourse import mybir as _mybir
    from concourse.bass_utils import run_bass_kernel_spmd as _run

    nc = _bacc.Bacc("TRN2", target_bir_lowering=False, num_devices=1)
    arrays, t = {}, {}
    given = {name: _np.ascontiguousarray(inputs[name]) for name in _INS}
    for name, a in {**given, **tables()}.items():
        arrays[f"in_{name}"] = a
        t[name] = nc.dram_tensor(f"in_{name}", a.shape, _mybir.dt.from_np(a.dtype), kind="ExternalInput").ap()
    for name, shape in SCRATCH.items():
        t[name] = nc.dram_tensor(name, shape, _mybir.dt.float32, kind="Internal").ap()
    t["out"] = nc.dram_tensor("out_dram", (B, S, D), _mybir.dt.float32, kind="ExternalOutput").ap()
    build(nc, t)
    r = _run(nc, [arrays], core_ids=[0])
    return r.results[0]["out_dram"]
```
